# Optimizing a Trainium2 kernel written in Bass

```python
import numpy as np
import jax
import jax.numpy as jnp

def _softmax(x, axis=-1):
    return jax.nn.softmax(x, axis=axis)

def _gelu(x):
    return jax.nn.gelu(x, approximate=True)

def _silu(x):
    return jax.nn.silu(x)

def _sigmoid(x):
    return jax.nn.sigmoid(x)

def _layernorm(x, axis=-1, eps=1e-05):
    m = jnp.mean(x, axis=axis, keepdims=True)
    v = jnp.var(x, axis=axis, keepdims=True)
    return (x - m) / jnp.sqrt(v + eps)

def _scatter_add(tgt, idx, src, axis=0):
    return tgt.at[idx].add(src)

def _segment_sum(src, seg, n):
    return jax.ops.segment_sum(src, seg, n)
kernel_name = 'mk_adaln_d1_jaxref_r8_61d2ea'

def setup_inputs(seed: int=0):
    np.random.seed(seed)
    _w = jnp.asarray

    def _L0_attn_setup():
        import jax, jax.numpy as jnp
        import numpy as np
        NUM_HEAD = 16
        D_Q = 64
        D_KV = 64
        ROPE_BASE = 10000.0

        def _cos_sin(seq_len, dim):
            pos = jnp.arange(seq_len, dtype=jnp.float32)[:, None]
            ids = jnp.arange(dim // 2, dtype=jnp.float32)
            theta = ROPE_BASE ** (-2.0 * ids) / (dim // 2)
            r = pos * theta[None, :]
            return (jnp.cos(r), jnp.sin(r))

        def _rope(x, cos, sin):
            b, s, d = x.shape
            xv = x.reshape(b, s, d // 2, 2)
            x0, x1 = (xv[..., 0], xv[..., 1])
            out = jnp.stack([x0 * cos - x1 * sin, x1 * cos + x0 * sin], axis=-1)
            return out.reshape(b, s, d)
        key = jax.random.key(seed)
        ks = jax.random.split(key, 10)
        d_model, d_q, d_kv = (128, D_Q, D_KV)
        b, s = (2, 256)
        w = lambda k, i, o: jax.random.normal(k, (i, o), dtype=jnp.float32) * 0.02
        return {'x': jax.random.normal(ks[0], (b, s, d_model), dtype=jnp.float32), 'Wd_q_w': w(ks[1], d_model, d_q), 'Wd_q_b': jnp.zeros((d_q,), jnp.float32), 'Wu_q_w': w(ks[2], d_q, d_model), 'Wu_q_b': jnp.zeros((d_model,), jnp.float32), 'Wq_r_w': w(ks[3], d_q, d_model), 'Wq_r_b': jnp.zeros((d_model,), jnp.float32), 'Wk_r_w': w(ks[4], d_model, d_model), 'Wk_r_b': jnp.zeros((d_model,), jnp.float32), 'Wd_kv_w': w(ks[5], d_model, d_kv), 'Wd_kv_b': jnp.zeros((d_kv,), jnp.float32), 'Wu_k_w': w(ks[6], d_kv, d_model), 'Wu_k_b': jnp.zeros((d_model,), jnp.float32), 'Wu_v_w': w(ks[7], d_kv, d_model), 'Wu_v_b': jnp.zeros((d_model,), jnp.float32), 'Wo_w': w(ks[8], d_model, d_model), 'Wo_b': jnp.zeros((d_model,), jnp.float32)}
    _L0_attn_in = _L0_attn_setup()

    def _L0_ffn_setup():
        import jax, jax.numpy as jnp
        import numpy as np
        B, L, H, E, FF, C = (4, 256, 128, 8, 512, 2)
        key = jax.random.key(seed)
        ks = jax.random.split(key, 6)
        s = 0.02
        return {'x': jax.random.normal(ks[0], (B, L, H), dtype=jnp.float32), 'Wg': jax.random.normal(ks[1], (H, E), dtype=jnp.float32) * s, 'W1': jax.random.normal(ks[2], (E, H, FF), dtype=jnp.float32) * s, 'b1': jnp.zeros((E, FF), dtype=jnp.float32), 'W2': jax.random.normal(ks[3], (E, FF, H), dtype=jnp.float32) * s, 'b2': jnp.zeros((E, H), dtype=jnp.float32)}
    _L0_ffn_in = _L0_ffn_setup()
    _L0_c = _w((lambda *s: np.random.randn(*s).astype(np.float32) * 0.05)(4, 128))
    _L0_wmod = _w((lambda *s: np.random.randn(*s).astype(np.float32) * 0.05)(128, 6 * 128) * 128 ** (-0.5))
    _d = {'L0_attn_x': _L0_attn_in['x'], 'L0_attn_Wd_q_w': _L0_attn_in['Wd_q_w'], 'L0_attn_Wd_q_b': _L0_attn_in['Wd_q_b'], 'L0_attn_Wu_q_w': _L0_attn_in['Wu_q_w'], 'L0_attn_Wu_q_b': _L0_attn_in['Wu_q_b'], 'L0_attn_Wq_r_w': _L0_attn_in['Wq_r_w'], 'L0_attn_Wq_r_b': _L0_attn_in['Wq_r_b'], 'L0_attn_Wk_r_w': _L0_attn_in['Wk_r_w'], 'L0_attn_Wk_r_b': _L0_attn_in['Wk_r_b'], 'L0_attn_Wd_kv_w': _L0_attn_in['Wd_kv_w'], 'L0_attn_Wd_kv_b': _L0_attn_in['Wd_kv_b'], 'L0_attn_Wu_k_w': _L0_attn_in['Wu_k_w'], 'L0_attn_Wu_k_b': _L0_attn_in['Wu_k_b'], 'L0_attn_Wu_v_w': _L0_attn_in['Wu_v_w'], 'L0_attn_Wu_v_b': _L0_attn_in['Wu_v_b'], 'L0_attn_Wo_w': _L0_attn_in['Wo_w'], 'L0_attn_Wo_b': _L0_attn_in['Wo_b'], 'L0_ffn_Wg': _L0_ffn_in['Wg'], 'L0_ffn_W1': _L0_ffn_in['W1'], 'L0_ffn_b1': _L0_ffn_in['b1'], 'L0_ffn_W2': _L0_ffn_in['W2'], 'L0_ffn_b2': _L0_ffn_in['b2'], 'L0_c': _L0_c, 'L0_wmod': _L0_wmod}
    _x0 = _d['L0_attn_x']
    _d['L0_attn_x'] = jax.random.normal(jax.random.fold_in(jax.random.key(seed), 1), (4, 512, 128), dtype=_x0.dtype)
    del _x0
    return _d

def reference(L0_attn_x, L0_attn_Wd_q_w, L0_attn_Wd_q_b, L0_attn_Wu_q_w, L0_attn_Wu_q_b, L0_attn_Wq_r_w, L0_attn_Wq_r_b, L0_attn_Wk_r_w, L0_attn_Wk_r_b, L0_attn_Wd_kv_w, L0_attn_Wd_kv_b, L0_attn_Wu_k_w, L0_attn_Wu_k_b, L0_attn_Wu_v_w, L0_attn_Wu_v_b, L0_attn_Wo_w, L0_attn_Wo_b, L0_ffn_Wg, L0_ffn_W1, L0_ffn_b1, L0_ffn_W2, L0_ffn_b2, L0_c, L0_wmod):

    def _L0_attn_ref(x, Wd_q_w, Wd_q_b, Wu_q_w, Wu_q_b, Wq_r_w, Wq_r_b, Wk_r_w, Wk_r_b, Wd_kv_w, Wd_kv_b, Wu_k_w, Wu_k_b, Wu_v_w, Wu_v_b, Wo_w, Wo_b):
        import jax, jax.numpy as jnp
        import numpy as np
        NUM_HEAD = 16
        D_Q = 64
        D_KV = 64
        ROPE_BASE = 10000.0

        def _cos_sin(seq_len, dim):
            pos = jnp.arange(seq_len, dtype=jnp.float32)[:, None]
            ids = jnp.arange(dim // 2, dtype=jnp.float32)
            theta = ROPE_BASE ** (-2.0 * ids) / (dim // 2)
            r = pos * theta[None, :]
            return (jnp.cos(r), jnp.sin(r))

        def _rope(x, cos, sin):
            b, s, d = x.shape
            xv = x.reshape(b, s, d // 2, 2)
            x0, x1 = (xv[..., 0], xv[..., 1])
            out = jnp.stack([x0 * cos - x1 * sin, x1 * cos + x0 * sin], axis=-1)
            return out.reshape(b, s, d)
        b, s, d_model = x.shape
        h = NUM_HEAD
        hd = d_model // h
        scale = jnp.sqrt(jnp.float32(h + D_KV + D_Q))

        def heads(t):
            return t.reshape(b, s, h, hd).transpose(0, 2, 1, 3)
        cos, sin = _cos_sin(s, d_model)
        ct_q = x @ Wd_q_w + Wd_q_b
        qt_c = heads(ct_q @ Wu_q_w + Wu_q_b)
        qt_r = heads(_rope(ct_q @ Wq_r_w + Wq_r_b, cos, sin))
        query = qt_c + qt_r
        ct_kv = x @ Wd_kv_w + Wd_kv_b
        kt_c = heads(ct_kv @ Wu_k_w + Wu_k_b)
        kt_r = heads(_rope(x @ Wk_r_w + Wk_r_b, cos, sin))
        key = kt_c + kt_r
        value = heads(ct_kv @ Wu_v_w + Wu_v_b)
        attn = jnp.einsum('bhqd,bhkd->bhqk', query, key) / scale
        attn = jax.nn.softmax(attn, axis=-1)
        out = jnp.einsum('bhqk,bhkd->bhqd', attn, value)
        out = out.transpose(0, 2, 1, 3).reshape(b, s, d_model)
        return out @ Wo_w + Wo_b

    def _L0_ffn_ref(x, Wg, W1, b1, W2, b2):
        import jax, jax.numpy as jnp
        import numpy as np
        B, L, H, E, FF, C = (4, 256, 128, 8, 512, 2)
        b, l, h = x.shape
        e = Wg.shape[1]
        n = b * l
        k = min(max(int(n * C / e), 1), n)
        xt = x.reshape(n, h)
        S = jax.nn.sigmoid(xt @ Wg).T
        G, I = jax.lax.top_k(S, k)
        ex = xt[I]
        hid = jax.nn.gelu(jnp.einsum('ekh,ehf->ekf', ex, W1) + b1[:, None, :], approximate=False)
        out = (jnp.einsum('ekf,efh->ekh', hid, W2) + b2[:, None, :]) * G[..., None]
        new_x = jnp.zeros_like(xt).at[I.reshape(-1)].add(out.reshape(-1, h))
        return new_x.reshape(b, l, h)
    x = L0_attn_x
    mod = (_silu(L0_c) @ L0_wmod).reshape(L0_c.shape[0], 6, 1, -1)
    sa, ca, ga, sb, cb, gb = (mod[:, 0], mod[:, 1], mod[:, 2], mod[:, 3], mod[:, 4], mod[:, 5])
    ga = (2 * (ga >= 0) - 1) * jnp.maximum(jnp.abs(ga), 0.25)
    gb = (2 * (gb >= 0) - 1) * jnp.maximum(jnp.abs(gb), 0.25)
    h = _layernorm(x, axis=-1) * (1 + ca) + sa
    x = x + ga * _L0_attn_ref(h, L0_attn_Wd_q_w, L0_attn_Wd_q_b, L0_attn_Wu_q_w, L0_attn_Wu_q_b, L0_attn_Wq_r_w, L0_attn_Wq_r_b, L0_attn_Wk_r_w, L0_attn_Wk_r_b, L0_attn_Wd_kv_w, L0_attn_Wd_kv_b, L0_attn_Wu_k_w, L0_attn_Wu_k_b, L0_attn_Wu_v_w, L0_attn_Wu_v_b, L0_attn_Wo_w, L0_attn_Wo_b)
    h = _layernorm(x, axis=-1) * (1 + cb) + sb
    x = x + gb * _L0_ffn_ref(h, L0_ffn_Wg, L0_ffn_W1, L0_ffn_b1, L0_ffn_W2, L0_ffn_b2)
    return x

_drawn_inputs = setup_inputs


def setup_inputs(seed=0):
    import zlib

    import numpy as np

    out = dict(_drawn_inputs(seed))
    spreads = {'L0_attn_Wd_q_b': (0.0, 0.8),
     'L0_attn_Wu_q_b': (0.0, 0.8),
     'L0_attn_Wq_r_b': (0.0, 0.8),
     'L0_attn_Wk_r_b': (0.0, 0.8),
     'L0_attn_Wd_kv_b': (0.0, 0.8),
     'L0_attn_Wu_k_b': (0.0, 0.8),
     'L0_attn_Wu_v_b': (0.0, 0.8),
     'L0_attn_Wo_b': (0.0, 0.314),
     'L0_ffn_b1': (0.0, 0.8),
     'L0_ffn_b2': (0.0, 0.404)}
    factors = {'L0_attn_Wd_q_w': 8.0,
     'L0_attn_Wu_q_w': 8.0,
     'L0_attn_Wq_r_w': 8.0,
     'L0_attn_Wk_r_w': 8.0,
     'L0_attn_Wd_kv_w': 8.0,
     'L0_attn_Wu_k_w': 8.0,
     'L0_attn_Wu_v_w': 8.0,
     'L0_attn_Wo_w': 8.0,
     'L0_ffn_Wg': 2.796,
     'L0_ffn_W1': 5.222,
     'L0_ffn_W2': 4.752}
    for name, (base, spread) in spreads.items():
        noise = np.random.default_rng([zlib.crc32(name.encode()), seed]).standard_normal(out[name].shape)
        drawn = base * np.exp(spread * noise) if base else spread * noise
        out[name] = jnp.asarray(drawn.astype(out[name].dtype))
    for name, factor in factors.items():
        out[name] = (out[name] * factor).astype(out[name].dtype)
    return out
```

```python
import numpy as np
import concourse.bass as bass
from concourse import mybir
from contextlib import ExitStack

NB, L, D = 4, 512, 128
NT = NB * L
NH, HD = 16, 8
DC = 64
TC = L // 128
NS = NB * NH // 4
NE, FF, CAP = 8, 512, 2
TOP = NT * CAP // NE
FC = FF // 128
SC = TOP // 128
SCALE = 1.0 / 12.0
EPS = 1e-5
PART_Q = [0, 0, 1, 1, 0, 2]
PART_K = [0, 1, 0, 1, 2, 0]
PR = 8 * len(PART_Q)
HW = D + NE + D
M_GA, M_SB, M_CB, M_GB = range(4)


def build(nc, t, out):
    fp32, bf16, fp16, i32 = mybir.dt.float32, mybir.dt.bfloat16, mybir.dt.float16, mybir.dt.int32
    ACT = mybir.ActivationFunctionType
    ALU = mybir.AluOpType
    AX = mybir.AxisListType
    ds = bass.ds

    qs_dram = nc.dram_tensor("q_parts", [NB, 2, PR, 8, L], bf16, kind="Internal").ap()
    ks_dram = nc.dram_tensor("k_parts", [NB, 2, PR, 8, L], bf16, kind="Internal").ap()
    logit_dram = nc.dram_tensor("logits", [NE, NT], fp32, kind="Internal").ap()
    rows_dram = nc.dram_tensor("rows", [NT, HW], fp32, kind="Internal").ap()

    ctx = ExitStack()
    with ctx:
        def sb(name, shape, dt=fp32):
            return ctx.enter_context(nc.sbuf_tensor(name, shape, dt))

        def sem(name):
            return ctx.enter_context(nc.semaphore(name))

        X = sb("X", [128, NB * TC, D])
        cT = sb("cT", [D, NB])
        wmod = sb("wmod", [D, 6 * D])
        w_x = sb("w_x", [D, 3 * D])
        w_ct = sb("w_ct", [128, 3 * D])
        bcol = sb("bcol", [D, 7])
        bv_row = sb("bv_row", [128, D])
        bo_row = sb("bo_row", [128, D])
        cos_t = sb("cos_t", [D, L])
        sin_t = sb("sin_t", [D, L])
        wo = sb("wo", [D, D])
        wg = sb("wg", [D, NE])
        ident = sb("ident", [128, 128])

        se = sb("se", [D, 4, NB])
        modcol = sb("modcol", [D, 2, NB])
        modrow = sb("modrow", [128, NB, 4 * D])
        wo_g = sb("wo_g", [D, NB, D])
        bo_g = sb("bo_g", [128, NB, D])

        stat = sb("stat", [128, TC, 6])
        mv = sb("mv", [128, TC, 2])
        mean = sb("mean", [128, NB * TC])
        var = sb("var", [128, NB * TC])
        rstd = sb("rstd", [128, NB * TC])
        mhalf = sb("mhalf", [128, NB * TC])
        Vall = sb("Vall", [128, NB, 4, TC, 32])

        MQ, MK, EQ, EK = (sb(n, [128, 2, 2, L], bf16) for n in ("MQ", "MK", "EQ", "EK"))
        mx = sb("mx", [128, 2, 16])
        mxn, mxr = (sb(n, [16, 128]) for n in ("mxn", "mxr"))
        mxp = sb("mxp", [16, 2, 3, 128], bf16)
        big = sb("big", [128, 2 * 4 * TC * L])
        PT = big[:, :].rearrange("p (u j c q) -> p u j c q", u=2, j=4, c=TC)
        VA = sb("VA", [128, 2, TC, 4, 32])
        osb = sb("osb", [128, L])
        rs = sb("rs", [128, 16])
        An = sb("An", [128, NS, TC, 32])

        def carve():
            at = [0]

            def view(*shape, dt=fp32):
                n = int(np.prod(shape)) * (4 if dt in (fp32, i32) else 2) // 4
                v = big[:, at[0]:at[0] + n]
                at[0] += n
                assert at[0] <= 2 * 4 * TC * L
                v = v if dt == fp32 else v.bitcast(dt)
                names = "abcd"[:len(shape)]
                return v.rearrange(f"p ({' '.join(names)}) -> p {' '.join(names)}", **dict(zip(names, shape)))
            return view

        view = carve()
        xn = view(2, TC, D)
        hT, ct = view(2, L), view(2, L)
        kcs, kss, kad, kf, kr = (view(L) for _ in range(5))
        qcs, qss, qad, qu, qf, qr = (view(L) for _ in range(6))
        kp, qp = view(2, 3, L, dt=bf16), view(2, 3, L, dt=bf16)
        sgn, mag = sb("sgn", [128, NB, 2, D]), sb("mag", [128, NB, 2, D])
        view = carve()
        Ab, aT, x2 = view(2, TC, D), view(2, L), view(2, TC, D)
        stat2, mv2, var2, rstd2 = view(TC, 6), view(TC, 2), view(TC), view(TC)
        xn2, rw = view(TC, D), view(2, TC, D + NE)
        h2T, lgs, ge = view(2, L), view(2, L), view(TC * NE)

        NSEG = 128 // NE
        lg = view(128)
        sv, junk, gt, eq, ep, sel, pp = (view(128) for _ in range(7))
        cnt, cnt_gt, lim, lim1 = (view(1) for _ in range(4))
        cand, flip = view(1, dt=i32), view(1, dt=i32)
        posi, posa, posb = (view(128, dt=i32) for _ in range(3))
        one_a, one_b = view(128, 16, dt=fp16), view(128, 32, dt=fp16)
        slots = view(NE * 32)
        assert NSEG * 128 == NT
        ex = sb("ex", [128, 2, SC, HW])
        w1s, w2s = sb("w1s", [D, 2, FF]), sb("w2s", [128, 2, FC, D])
        view = carve()
        exT, hid, yb, ys = view(2, TOP), view(FC, TOP), view(SC, D), view(2, SC, D)
        idx = sb("idx", [128, NE, SC], i32)
        idg, ids = sb("idg", [128, 2, SC], i32), sb("ids", [128, 2, SC], i32)
        b1c, b2r = sb("b1c", [128, NE, FC]), sb("b2r", [128, NE, D])
        same_e, lower = sb("same_e", [128, 128]), sb("lower", [128, 128])
        bitf, bitn = sb("bitf", [128, 30]), sb("bitn", [128, 30], i32)
        iota32, tok16 = sb("iota32", [128, 32]), sb("tok16", [128, NSEG])
        ones = sb("ones", [128, 128])

        ps = ctx.enter_context(nc.psum_tensor("ps", [128, 8, 512], fp32))

        l_x, l_w, l_tab, l_c = sem("l_x"), sem("l_w"), sem("l_tab"), sem("l_c")
        s_silu, s_mod, s_modc, s_modr = sem("s_silu"), sem("s_mod"), sem("s_modc"), sem("s_modr")
        s_stat, s_ln = sem("s_stat"), sem("s_ln")
        s_const = sem("s_const")
        s_rstd, s_xc, s_xn = sem("s_rstd"), sem("s_xc"), sem("s_xn")
        s_held = sem("s_held")
        s_T, s_vd, s_kt, s_qt, s_kf, s_u, s_qad, s_qf = (
            sem(n) for n in ("s_T", "s_vd", "s_kt", "s_qt", "s_kf", "s_u", "s_qad", "s_qf"))
        s_hT, s_CT, s_kAB, s_ct, s_qAB, s_qc, s_kc, s_V = (
            sem(n) for n in ("s_hT", "s_CT", "s_kAB", "s_ct", "s_qAB", "s_qc", "s_kc", "s_V"))
        s_kad, s_kh, s_kr, s_km, s_kl = (sem(n) for n in ("s_kad", "s_kh", "s_kr", "s_km", "s_kl"))
        s_qh, s_qr, s_qm, s_ql = (sem(n) for n in ("s_qh", "s_qr", "s_qm", "s_ql"))
        w_k = [sem(f"w_k{u}") for u in range(2)]
        w_q = [sem(f"w_q{u}") for u in range(2)]

        s_one = sem("s_one")
        s_gate = sem("s_gate")
        l_m = [sem(f"l_m{u}") for u in range(2)]
        l_e = [sem(f"l_e{u}") for u in range(2)]
        s_mx, s_mxd, s_mt, s_mn, s_pp, s_parts = (
            sem(n) for n in ("s_mx", "s_mxd", "s_mt", "s_mn", "s_pp", "s_parts"))
        s_sc, s_ex, s_va, s_pv, s_oe, s_ot, s_rs, s_no = (
            sem(n) for n in ("s_sc", "s_ex", "s_va", "s_pv", "s_oe", "s_ot", "s_rs", "s_no"))
        s_prep = sem("s_prep")

        s_ab, s_aT, s_aTe, s_y, s_x2 = (sem(n) for n in ("s_ab", "s_aT", "s_aTe", "s_y", "s_x2"))
        s_st2, s_v2, s_r2, s_xn2, s_xm2, s_h2 = (
            sem(n) for n in ("s_st2", "s_v2", "s_r2", "s_xn2", "s_xm2", "s_h2"))
        s_h2t, s_h2e, s_lg, s_lge, s_gl, s_ge, s_g1, s_g = (
            sem(n) for n in ("s_h2t", "s_h2e", "s_lg", "s_lge", "s_gl", "s_ge", "s_g1", "s_g"))
        w_out = [sem(f"w_out{u}") for u in range(2)]
        w_row = [sem(f"w_row{u}") for u in range(2)]
        w_lg = [sem(f"w_lg{u}") for u in range(2)]
        w_gb = sem("w_gb")

        l_top, l_lg = sem("l_top"), sem("l_lg")
        s_cnt, s_tot, s_cand, s_sig, s_sel, s_selp, s_tk = (
            sem(n) for n in ("s_cnt", "s_tot", "s_cand", "s_sig", "s_sel", "s_selp", "s_tk"))
        s_slot, s_idx, s_ones = sem("s_slot"), sem("s_idx"), sem("s_ones")
        l_w12 = [sem(f"l_w12_{u}") for u in range(2)]
        g_in = [sem(f"g_in{u}") for u in range(2)]
        w_sc = [sem(f"w_sc{u}") for u in range(2)]
        s_ig, s_is = sem("s_ig"), sem("s_is")
        s_gt, s_gx, s_up, s_gelu, s_dn, s_yb, s_yo = (
            sem(n) for n in ("s_gt", "s_gx", "s_up", "s_gelu", "s_dn", "s_yb", "s_yo"))

        block = ctx.enter_context(nc.Block())

        @block.sync
        def _(sp):
            sp.dma_start(cT[:], t["cT"]).then_inc(l_c, 16)
            sp.dma_start(wmod[:], t["wmod"]).then_inc(l_c, 16)
            for b in range(NB):
                sp.dma_start(X[:, b * TC:(b + 1) * TC, :],
                             t["x"][b].rearrange("(c p) d -> p c d", p=128)).then_inc(l_x, 16)
            for dst, src in ((ident, "ident"), (w_x, "w_x"), (w_ct, "w_ct"), (bcol, "bcol")):
                sp.dma_start(dst[:], t[src]).then_inc(l_w, 16)
            sp.dma_start(cos_t[:], t["cos"]).then_inc(l_tab, 16)
            sp.dma_start(sin_t[:], t["sin"]).then_inc(l_tab, 16)
            sp.dma_start(bv_row[:], t["brow"][0:1, :].to_broadcast([128, D])).then_inc(l_tab, 16)
            sp.dma_start(bo_row[:], t["brow"][1:2, :].to_broadcast([128, D])).then_inc(l_tab, 16)
            sp.dma_start(wo[:], t["wo"]).then_inc(l_tab, 16)
            sp.dma_start(wg[:], t["wg"]).then_inc(l_tab, 16)
            for dst, src in ((b1c, "b1c"), (same_e, "same_e"), (lower, "lower"), (bitf, "bitf"), (bitn, "bitn"),
                             (iota32, "iota32"), (tok16, "tok16")):
                sp.dma_start(dst[:], t[src]).then_inc(l_top, 16)
            sp.dma_start(b2r[:], t["b2"].unsqueeze(0).to_broadcast([128, NE, D])).then_inc(l_top, 16)

            with sp.Fori(0, NB // 2) as it:
                for u in range(2):
                    b = it * 2 + u
                    for buf, part, order, done, w in ((kp, ks_dram, PART_K, s_kl, w_k),
                                                      (qp, qs_dram, PART_Q, s_ql, w_q)):
                        sp.wait_ge(done, b + 1)
                        for j, p in enumerate(order):
                            for half in range(2):
                                sp.dma_start(
                                    part[ds(b, 1), half, 8 * j:8 * j + 8, :, :].rearrange("o d h t -> (o d h) t"),
                                    buf[64 * half:64 * half + 64, u, p, :]).then_inc(w[u], 16)
            for u in range(2):
                sp.wait_ge(w_k[u], 16 + 192 * (NB // 2))
                sp.wait_ge(w_q[u], 16 + 192 * (NB // 2))

            def load_group(s, kbuf, qbuf, slot, done):
                for buf, part in ((kbuf, ks_dram), (qbuf, qs_dram)):
                    for half in range(2):
                        if isinstance(s, int):
                            src = part[s // 4:s // 4 + 1, half, :, 2 * (s % 4):2 * (s % 4) + 2, :]
                        else:
                            src = part[ds(s // 4, 1), half, :, ds((s % 4) * 2, 2), :]
                        sp.dma_start(buf[64 * half:64 * half + PR, slot, :, :],
                                     src.rearrange("o r i t -> (o r) i t")).then_inc(done, 16)

            def load_max(s, slot):
                sp.wait_ge(s_parts, s + 1)
                for half in range(2):
                    for p in range(3):
                        r = 64 * half + PR + p
                        sp.dma_start(EQ[r:r + 1, slot, :, :].rearrange("p i q -> p (i q)"),
                                     mxp[8 * half:8 * half + 8, slot, p, :]).then_inc(l_e[slot], 16)

            def step(s, u, more_max=True, more=True):
                if more_max:
                    sp.wait_ge(s_mx, 8 * (s + 2))
                    load_group(s + 3, MK, MQ, 1 - u, l_m[1 - u])
                if more:
                    if not (isinstance(s, int) and s == 0):
                        sp.wait_ge(s_sc, 16 * s)
                    load_group(s + 1, EK, EQ, 1 - u, l_e[1 - u])
                    load_max(s + 1, 1 - u)

            load_group(0, MK, MQ, 0, l_m[0])
            load_group(1, MK, MQ, 1, l_m[1])
            sp.wait_ge(s_one, 2)
            load_group(0, EK, EQ, 0, l_e[0])
            sp.wait_ge(s_mx, 8)
            load_group(2, MK, MQ, 0, l_m[0])
            load_max(0, 0)
            step(0, 0)
            step(1, 1)
            with sp.Fori(1, NS // 2 - 2) as it:
                step(it * 2, 0)
                step(it * 2 + 1, 1)
            step(12, 0)
            step(13, 1, more_max=False)
            step(14, 0, more_max=False)

            sp.wait_ge(s_gate, 1)
            for b in range(NB):
                sp.dma_start(
                    rows_dram[b * L:(b + 1) * L, D + NE:HW].rearrange("(c p) d -> p c d", p=128),
                    modrow[:, b:b + 1, M_GB * D:(M_GB + 1) * D].to_broadcast([128, TC, D])).then_inc(w_gb, 16)

            with sp.Fori(0, NB // 2) as it:
                for u in range(2):
                    b = it * 2 + u
                    sp.wait_ge(s_x2, b + 2)
                    sp.dma_start(out[ds(b, 1), :, :].rearrange("o (c p) d -> p (o c) d", p=128),
                                 x2[:, u, :, :]).then_inc(w_out[u], 16)
                    sp.wait_ge(s_lge, b + 2)
                    sp.dma_start(logit_dram[:, ds(b * L, L)], lgs[0:NE, u, :]).then_inc(w_lg[u], 16)
                    sp.wait_ge(s_g, b + 2)
                    sp.dma_start(rows_dram[ds(b * L, L), 0:D + NE].rearrange("(c p) d -> p c d", p=128),
                                 rw[:, u, :, :]).then_inc(w_row[u], 16)
            for u in range(2):
                sp.wait_ge(w_lg[u], 16 + 16 * (NB // 2))
            sp.dma_start(lg, logit_dram.rearrange("e (s k) -> (e s) k", k=128)).then_inc(l_lg, 16)

            def load_expert(e, u):
                if isinstance(e, int):
                    a, b = t["w1"][e], t["w2"][e]
                else:
                    sp.wait_ge(s_dn, e - 1)
                    a = t["w1"][ds(e, 1)].rearrange("o h f -> (o h) f")
                    b = t["w2"][ds(e, 1)].rearrange("o f h -> (o f) h")
                sp.dma_start(w1s[:, u, :], a).then_inc(l_w12[u], 16)
                sp.dma_start(w2s[:, u, :, :], b.rearrange("(c p) h -> p c h", p=128)).then_inc(l_w12[u], 16)

            load_expert(0, 0)
            load_expert(1, 1)
            with sp.Fori(1, NE // 2) as it:
                for u in range(2):
                    load_expert(it * 2 + u, u)

        @block.gpsimd
        def _(pool):
            pool.sem_inc(s_T, 2)
            for s_ in (s_vd, s_kt, s_qt, s_kf, s_u, s_qad, s_qf):
                pool.sem_inc(s_, 1)
            for s_ in (*w_k, *w_q, *w_out, *w_row, *w_lg):
                pool.sem_inc(s_, 16)
            pool.sem_inc(s_aT, 2)
            pool.sem_inc(s_yo, 2)
            pool.sem_inc(s_h2t, 2)
            for s_ in (s_aTe, s_x2, s_h2e, s_lge, s_ge, s_g):
                pool.sem_inc(s_, 1)
            nc.gpsimd.memset(mhalf[:], -0.5).then_inc(s_const, 1)
            nc.gpsimd.memset(ones[:], 1.0).then_inc(s_ones, 1)
            pool.wait_ge(s_ln, NB)
            pool.wait_ge(s_const, 1)
            nc.gpsimd.tensor_tensor(rstd[:], var[:], mhalf[:], ALU.pow).then_inc(s_rstd, 1)
            pool.wait_ge(s_rstd, 1)
            with pool.Fori(0, NB // 2) as it:
                for u in range(2):
                    b = it * 2 + u
                    t4 = ds(b * TC, TC)
                    pool.wait_ge(s_T, b + 1)
                    nc.gpsimd.tensor_tensor(xn[:, u], X[:, t4, :],
                                            mean[:, t4].unsqueeze(2).to_broadcast([128, TC, D]),
                                            ALU.subtract).then_inc(s_xc, 1)
                    pool.wait_ge(s_xc, b + 1)
                    nc.gpsimd.tensor_tensor(xn[:, u], xn[:, u],
                                            rstd[:, t4].unsqueeze(2).to_broadcast([128, TC, D]),
                                            ALU.mult).then_inc(s_xn, 1)
                    pool.wait_ge(s_qt, b + 2)
                    nc.gpsimd.tensor_tensor(qad[:], qcs[:], qss[:], ALU.add).then_inc(s_qad, 1)
                    pool.wait_ge(s_qad, b + 2)
                    pool.wait_ge(s_u, b + 2)
                    nc.gpsimd.tensor_tensor(qf[:], qad[:], qu[:], ALU.add).then_inc(s_qf, 1)
                    pool.wait_ge(s_qf, b + 2)
                    pool.wait_ge(w_q[u], it * 192 + 16)
                    pool.sem_inc(s_held, 1)
                    nc.gpsimd.tensor_copy(qp[:, u, 0, :], qf[:]).then_inc(s_qh, 1)
                    pool.wait_ge(s_qh, b + 1)
                    nc.gpsimd.tensor_tensor(qr[:], qf[:], qp[:, u, 0, :], ALU.subtract).then_inc(s_qr, 1)
                    pool.wait_ge(s_qr, b + 1)
                    pool.sem_inc(s_held, 1)
                    nc.gpsimd.tensor_copy(qp[:, u, 1, :], qr[:]).then_inc(s_qm, 1)
                    pool.wait_ge(s_qm, b + 1)
                    nc.gpsimd.tensor_tensor(qp[:, u, 2, :], qr[:], qp[:, u, 1, :], ALU.subtract).then_inc(s_ql, 1)

            nc.gpsimd.memset(EK[:], 1.0).then_inc(s_one, 1)
            nc.gpsimd.memset(EQ[:], 0.0).then_inc(s_one, 1)
            nc.gpsimd.memset(VA[:], 0.0).then_inc(s_prep, 1)
            pool.wait_ge(s_prep, 1)
            nc.gpsimd.memset(VA[:, :, :, :, HD:HD + 1], 1.0).then_inc(s_prep, 1)
            pool.wait_ge(s_prep, 2)

            def values(s, u):
                if not (isinstance(s, int) and s < 2):
                    pool.wait_ge(s_pv, s - 1)
                pool.sem_inc(s_held, 1)
                src = (Vall[:, s // 4, s % 4] if isinstance(s, int)
                       else Vall[:, ds(s // 4, 1), ds(s % 4, 1)].rearrange("p a b c d -> p (a b c) d"))
                nc.gpsimd.tensor_copy(VA[:, u, :, :, 0:HD],
                                      src.rearrange("p c (j d) -> p c j d", d=HD)).then_inc(s_va, 1)

            def max_parts(s, u):
                if not (isinstance(s, int) and s < 2):
                    pool.wait_ge(l_e[u], (s // 2) * 160)
                pool.wait_ge(s_mn, s + 1)
                pool.sem_inc(s_held, 1)
                nc.gpsimd.tensor_copy(mxp[:, u, 0, :], mxn[:]).then_inc(s_pp, 1)
                pool.wait_ge(s_pp, 3 * s + 1)
                nc.gpsimd.tensor_tensor(mxr[:], mxn[:], mxp[:, u, 0, :], ALU.subtract).then_inc(s_pp, 1)
                pool.wait_ge(s_pp, 3 * s + 2)
                pool.sem_inc(s_held, 1)
                nc.gpsimd.tensor_copy(mxp[:, u, 1, :], mxr[:]).then_inc(s_pp, 1)
                pool.wait_ge(s_pp, 3 * s + 3)
                nc.gpsimd.tensor_tensor(mxp[:, u, 2, :], mxr[:], mxp[:, u, 1, :],
                                        ALU.subtract).then_inc(s_parts, 1)

            max_parts(0, 0)
            values(0, 0)
            max_parts(1, 1)

            v = modrow[:, :, :].rearrange("p b (j c) -> p b j c", c=D)[:, :, 0:4:3, :]
            pool.wait_ge(s_modr, NB)
            nc.gpsimd.tensor_scalar(sgn[:], v, 0.0, 2.0, ALU.is_ge, ALU.mult).then_inc(s_prep, 1)
            pool.wait_ge(s_prep, 3)
            nc.gpsimd.tensor_scalar(sgn[:], sgn[:], -1.0, None, ALU.add).then_inc(s_prep, 1)
            pool.wait_ge(s_prep, 4)
            nc.gpsimd.tensor_tensor(mag[:], v, sgn[:], ALU.mult).then_inc(s_prep, 1)
            pool.wait_ge(s_prep, 5)
            nc.gpsimd.tensor_scalar(mag[:], mag[:], 0.25, None, ALU.max).then_inc(s_prep, 1)
            pool.wait_ge(s_prep, 6)
            nc.gpsimd.tensor_tensor(v, sgn[:], mag[:], ALU.mult).then_inc(s_prep, 1)
            cb = modrow[:, :, M_CB * D:(M_CB + 1) * D]
            nc.gpsimd.tensor_scalar(cb, cb, 1.0, None, ALU.add).then_inc(s_gate, 1)
            pool.wait_ge(s_prep, 7)
            ga = modrow[:, :, M_GA * D:(M_GA + 1) * D]
            pool.wait_ge(l_tab, 96)
            nc.gpsimd.tensor_tensor(wo_g[:], ga, wo[:].unsqueeze(1).to_broadcast([D, NB, D]),
                                    ALU.mult).then_inc(s_prep, 1)
            nc.gpsimd.tensor_tensor(bo_g[:], ga, bo_row[:].unsqueeze(1).to_broadcast([128, NB, D]),
                                    ALU.mult).then_inc(s_prep, 1)
            pool.wait_ge(s_prep, 9)
            xv = X[:, :, :].rearrange("p (b c) d -> p b c d", b=NB)
            nc.gpsimd.tensor_tensor(xv, xv, bo_g[:].unsqueeze(2).to_broadcast([128, NB, TC, D]),
                                    ALU.add).then_inc(s_prep, 1)

            values(1, 1)
            max_parts(2, 0)
            with pool.Fori(1, NS // 2 - 1) as it:
                values(it * 2, 0)
                max_parts(it * 2 + 1, 1)
                values(it * 2 + 1, 1)
                max_parts(it * 2 + 2, 0)
            values(14, 0)
            max_parts(15, 1)
            values(15, 1)

            pool.wait_ge(s_no, NS)
            with pool.Fori(0, NB // 2) as it:
                for u in range(2):
                    b = it * 2 + u
                    pool.wait_ge(s_aT, b + 1)
                    pool.sem_inc(s_held, 1)
                    nc.gpsimd.tensor_copy(
                        Ab[:, u, :, :].rearrange("p q (g c) -> p q g c", c=32),
                        An[:, ds(b * 4, 4), :, :].rearrange("p g q c -> p q g c")).then_inc(s_ab, 1)
                    pool.wait_ge(s_v2, b + 1)
                    nc.gpsimd.tensor_tensor(rstd2[:], var2[:], mhalf[:, 0:TC], ALU.pow).then_inc(s_r2, 1)
                    pool.wait_ge(s_xm2, b + 1)
                    pool.wait_ge(w_row[u], it * 16 + 16)
                    nc.gpsimd.tensor_tensor(
                        rw[:, u, :, 0:D], xn2[:],
                        modrow[:, ds(b, 1), M_SB * D:(M_SB + 1) * D].to_broadcast([128, TC, D]),
                        ALU.add).then_inc(s_h2, 1)

            out_rows = out.rearrange("b l d -> (b l) d")

            def indices(e, dst, done):
                pool.sem_inc(s_held, 1)
                src = idx[:, e, :] if isinstance(e, int) else idx[:, ds(e, 1), :].rearrange("p o c -> p (o c)")
                nc.gpsimd.tensor_copy(dst, src).then_inc(done, 1)
                pool.wait_ge(done, e + 1)
                pool.sem_inc(s_held, 1)

            def gather(e, u):
                pool.wait_ge(s_yo, e + 1)
                indices(e, idg[:, u, :], s_ig)
                for c in range(SC):
                    pool.indirect_dma_start(
                        out=ex[:, u, c, :], out_offset=None, in_=rows_dram,
                        in_offset=bass.IndirectOffsetOnAxis(ap=idg[:, u, c:c + 1], axis=0)).then_inc(g_in[u], 16)

            def scatter(e, u):
                pool.wait_ge(s_yo, e + 3)
                indices(e, ids[:, u, :], s_is)
                if not (isinstance(e, int) and e == 0):
                    pool.wait_ge(w_sc[1 - u], ((e + 1) // 2) * 64)
                    pool.sem_inc(s_held, 1)
                for c in range(SC):
                    pool.indirect_dma_start(
                        out=out_rows, out_offset=bass.IndirectOffsetOnAxis(ap=ids[:, u, c:c + 1], axis=0),
                        in_=ys[:, u, c, :], in_offset=None, compute_op=ALU.add).then_inc(w_sc[u], 16)

            pool.wait_ge(w_gb, 16 * NB)
            for u in range(2):
                pool.wait_ge(w_row[u], 16 + 16 * (NB // 2))
                pool.wait_ge(w_out[u], 16 + 16 * (NB // 2))
            pool.wait_ge(s_idx, 4)
            gather(0, 0)
            gather(1, 1)
            scatter(0, 0)
            with pool.Fori(0, NE // 2 - 1) as it:
                gather(it * 2 + 2, 0)
                scatter(it * 2 + 1, 1)
                gather(it * 2 + 3, 1)
                scatter(it * 2 + 2, 0)
            scatter(NE - 1, 1)
            for u in range(2):
                pool.wait_ge(w_sc[u], 64 * (NE // 2))

        @block.scalar
        def _(act):
            act.wait_ge(l_c, 32)
            nc.scalar.activation(se[:, 0, :], cT[:], ACT.Exp, scale=-1.0).then_inc(s_silu, 1)
            for b in range(NB):
                act.wait_ge(s_mod, b + 2)
                nc.scalar.activation(modrow[:, b, :], ps[:, b, :], ACT.Copy).then_inc(s_modr, 1)
            act.wait_ge(l_w, 64)
            act.wait_ge(s_modc, 2)
            with act.Fori(0, NB // 2) as it:
                for u in range(2):
                    b = it * 2 + u
                    act.wait_ge(s_T, b + 3)
                    nc.scalar.activation(hT[:, u, :], ps[:, 0, :], ACT.Identity,
                                         bias=modcol[:, 0, ds(b, 1)], scale=modcol[:, 1, ds(b, 1)]).then_inc(s_hT, 1)
                    act.wait_ge(s_CT, b + 1)
                    nc.scalar.activation(ct[:, u, :], ps[:, 1, :], ACT.Identity, bias=bcol[:, 0:1]).then_inc(s_ct, 1)
                    act.wait_ge(s_qc, b + 1)
                    act.wait_ge(s_qf, b + 1)
                    nc.scalar.activation(qu[:], ps[:, 4, :], ACT.Identity, bias=bcol[:, 1:2]).then_inc(s_u, 1)
                    act.wait_ge(s_kf, b + 2)
                    act.wait_ge(w_k[u], it * 192 + 16)
                    nc.scalar.activation(kp[:, u, 0, :], kf[:], ACT.Copy).then_inc(s_kh, 1)
                    act.wait_ge(s_kr, b + 1)
                    nc.scalar.activation(kp[:, u, 1, :], kr[:], ACT.Copy).then_inc(s_km, 1)

            def max_out(s):
                act.wait_ge(s_mt, s + 1)
                if not (isinstance(s, int) and s == 0):
                    act.wait_ge(s_parts, s)
                nc.scalar.activation(mxn[:], ps[0:16, 7, 0:128], ACT.Copy).then_inc(s_mn, 1)

            def out_copy(s):
                act.wait_ge(s_pv, s + 1)
                if not (isinstance(s, int) and s == 0):
                    act.wait_ge(s_ot, s)
                nc.scalar.activation(osb[:], ps[:, 6, :], ACT.Copy).then_inc(s_oe, 1)

            def step(s, u, prev=True, more_max=True):
                for n in range(16):
                    if n == 1 and prev:
                        out_copy(s - 2)
                    if n == 4 and more_max:
                        max_out(s + 1)
                    i, kc, half = n // 8, (n // 2) % 4, n % 2
                    if n == 0 and not (isinstance(s, int) and s < 2):
                        act.wait_ge(s_pv, s - 1)
                    act.wait_ge(s_sc, 16 * s + n + 1)
                    nc.scalar.activation(PT[:, u, 2 * i + half, kc, :], ps[:, 4 + half, :], ACT.Exp,
                                         scale=SCALE).then_inc(s_ex, 1)

            max_out(0)
            max_out(1)
            step(0, 0, prev=False, more_max=False)
            step(1, 1, prev=False)
            with act.Fori(1, NS // 2 - 1) as it:
                step(it * 2, 0)
                step(it * 2 + 1, 1)
            step(14, 0)
            step(15, 1, more_max=False)
            out_copy(14)
            out_copy(15)

            with act.Fori(0, NB // 2) as it:
                for u in range(2):
                    b = it * 2 + u
                    act.wait_ge(s_aT, b + 3)
                    nc.scalar.activation(aT[:, u, :], ps[:, 0, :], ACT.Copy).then_inc(s_aTe, 1)
                    act.wait_ge(s_h2t, b + 3)
                    nc.scalar.activation(h2T[:, u, :], ps[:, 2, :], ACT.Copy).then_inc(s_h2e, 1)
                    act.wait_ge(s_gl, b + 1)
                    act.wait_ge(w_lg[u], it * 16 + 16)
                    nc.scalar.activation(lgs[0:NE, u, :], ps[0:NE, 3, :], ACT.Copy).then_inc(s_lge, 1)
                    act.wait_ge(s_g, b + 1)
                    nc.scalar.activation(ge[:], ps[:, 4, 0:TC * NE], ACT.Exp, scale=-1.0).then_inc(s_ge, 1)

            act.wait_ge(l_lg, 16)
            nc.scalar.activation(sv, lg, ACT.Exp, scale=-1.0).then_inc(s_sig, 1)
            act.wait_ge(s_slot, 2)
            nc.scalar.activation(slots[0:16, :], ps[0:16, 1, 0:NE * 32], ACT.Copy).then_inc(s_slot, 1)
            act.wait_ge(l_top, 16 * 8)
            act.wait_ge(s_gx, 1)
            with act.Fori(0, NE) as e:
                for f in range(FC):
                    act.wait_ge(s_up, e * FC + f + 1)
                    nc.scalar.activation(hid[:, f, :], ps[:, 1 + f, :], ACT.Gelu,
                                         bias=b1c[:, ds(e, 1), f]).then_inc(s_gelu, 1)

        @block.vector
        def _(dve):
            dve.wait_ge(s_silu, 1)
            nc.vector.tensor_scalar_add(se[:, 1, :], se[:, 0, :], 1.0).then_inc(s_silu, 1)
            dve.wait_ge(s_silu, 2)
            nc.vector.reciprocal(se[:, 2, :], se[:, 1, :]).then_inc(s_silu, 1)
            dve.wait_ge(s_silu, 3)
            nc.vector.tensor_tensor(se[:, 3, :], se[:, 2, :], cT[:], ALU.mult).then_inc(s_silu, 1)
            dve.wait_ge(l_x, 16 * NB)
            with dve.Fori(0, NB) as b:
                for c in range(TC):
                    ins = nc.vector.bn_stats(stat[:, c, :], X[:, ds(b * TC + c, 1), :].rearrange("p o d -> p (o d)"))
                ins.then_inc(s_stat, 1)
                dve.wait_ge(s_stat, b * 2 + 1)
                dve.sem_inc(s_held, 1)
                for c in range(TC):
                    ins = nc.vector.bn_aggr(mv[:, c, :], stat[:, c, :])
                ins.then_inc(s_stat, 1)
                dve.wait_ge(s_stat, b * 2 + 2)
                nc.vector.tensor_copy(mean[:, ds(b * TC, TC)], mv[:, :, 0])
                nc.vector.tensor_scalar_add(var[:, ds(b * TC, TC)], mv[:, :, 1], EPS).then_inc(s_ln, 1)
            dve.wait_ge(s_mod, 1)
            nc.vector.tensor_copy(modcol[:, 0, :], ps[:, 4, 0:NB]).then_inc(s_modc, 1)
            nc.vector.tensor_scalar_add(modcol[:, 1, :], ps[:, 4, NB:2 * NB], 1.0).then_inc(s_modc, 1)

            dve.wait_ge(l_tab, 96)
            dve.wait_ge(l_w, 64)
            with dve.Fori(0, NB // 2) as it:
                for u in range(2):
                    b = it * 2 + u
                    dve.wait_ge(s_kAB, b + 1)
                    nc.vector.scalar_tensor_tensor(out=kcs[:], in0=ps[:, 2, :], scalar=bcol[:, 5:6], in1=cos_t[:],
                                                   op0=ALU.add, op1=ALU.mult)
                    nc.vector.scalar_tensor_tensor(out=kss[:], in0=ps[:, 3, :], scalar=bcol[:, 6:7], in1=sin_t[:],
                                                   op0=ALU.add, op1=ALU.mult).then_inc(s_kt, 1)
                    dve.wait_ge(s_kt, b + 2)
                    nc.vector.tensor_tensor(kad[:], kcs[:], kss[:], ALU.add).then_inc(s_kad, 1)
                    dve.wait_ge(s_kad, b + 1)
                    dve.wait_ge(s_kc, b + 1)
                    nc.vector.scalar_tensor_tensor(out=kf[:], in0=ps[:, 5, :], scalar=bcol[:, 4:5], in1=kad[:],
                                                   op0=ALU.add, op1=ALU.add).then_inc(s_kf, 1)
                    dve.wait_ge(s_qAB, b + 1)
                    dve.wait_ge(s_qad, b + 1)
                    nc.vector.scalar_tensor_tensor(out=qcs[:], in0=ps[:, 6, :], scalar=bcol[:, 2:3], in1=cos_t[:],
                                                   op0=ALU.add, op1=ALU.mult)
                    nc.vector.scalar_tensor_tensor(out=qss[:], in0=ps[:, 7, :], scalar=bcol[:, 3:4], in1=sin_t[:],
                                                   op0=ALU.add, op1=ALU.mult).then_inc(s_qt, 1)
                    dve.wait_ge(s_kh, b + 1)
                    nc.vector.tensor_tensor(kr[:], kf[:], kp[:, u, 0, :], ALU.subtract).then_inc(s_kr, 1)
                    dve.wait_ge(s_V, b + 1)
                    nc.vector.tensor_tensor(
                        Vall[:, ds(b, 1), :, :, :].rearrange("p o g c d -> p (o g) c d"),
                        ps[:, 0, :].rearrange("p (c g d) -> p g c d", c=TC, g=4),
                        bv_row[:].rearrange("p (g d) -> p g d", g=4).unsqueeze(2).to_broadcast([128, 4, TC, 32]),
                        ALU.add).then_inc(s_vd, 1)
                    dve.wait_ge(s_km, b + 1)
                    nc.vector.tensor_tensor(kp[:, u, 2, :], kr[:], kp[:, u, 1, :], ALU.subtract).then_inc(s_kl, 1)

            def normed(s):
                dve.wait_ge(s_ot, s + 1)
                o = ps[:, 7, :].rearrange("p (a d) -> p a d", d=32)
                nc.vector.reciprocal(rs[:].unsqueeze(2), o[:, :, HD:HD + 1]).then_inc(s_rs, 1)
                dve.wait_ge(s_rs, s + 1)
                dst = (An[:, s] if isinstance(s, int) else
                       An[:, ds(s, 1)].rearrange("p o q c -> p (o q) c"))
                nc.vector.tensor_tensor(dst.rearrange("p q (j d) -> p (q j) d", d=HD), o[:, :, 0:HD],
                                        rs[:].unsqueeze(2).to_broadcast([128, 16, HD]), ALU.mult).then_inc(s_no, 1)

            def maxima(s, u, n):
                if n == 0 and not (isinstance(s, int) and s < 2):
                    dve.wait_ge(s_mt, s - 1)
                dve.wait_ge(s_mx, 8 * s + n + 1)
                nc.vector.tensor_reduce(mx[:, u, :].rearrange("p (h a) -> p h a", h=2)[:, :, n],
                                        ps[:, 2 * (n % 2):2 * (n % 2) + 2, :], AX.X, ALU.max,
                                        negate=True).then_inc(s_mxd, 1)

            def step(s, u, prev=True, more_max=True):
                for n in range(8):
                    if more_max:
                        maxima(s + 2, u, n)
                    if n == 5 and prev:
                        normed(s - 2)

            for n in range(8):
                maxima(0, 0, n)
            for n in range(8):
                maxima(1, 1, n)
            step(0, 0, prev=False)
            step(1, 1, prev=False)
            with dve.Fori(1, NS // 2 - 1) as it:
                step(it * 2, 0)
                step(it * 2 + 1, 1)
            step(14, 0, more_max=False)
            step(15, 1, more_max=False)
            normed(14)
            normed(15)

            dve.wait_ge(s_prep, 10)
            dve.wait_ge(s_gate, 1)
            with dve.Fori(0, NB // 2) as it:
                for u in range(2):
                    b = it * 2 + u
                    dve.wait_ge(s_y, b + 1)
                    dve.wait_ge(w_out[u], it * 16 + 16)
                    nc.vector.tensor_tensor(x2[:, u], ps[:, 1, :].rearrange("p (c d) -> p c d", c=TC),
                                            X[:, ds(b * TC, TC), :], ALU.add).then_inc(s_x2, 1)
                    dve.wait_ge(s_x2, b + 2)
                    for c in range(TC):
                        ins = nc.vector.bn_stats(stat2[:, c, :], x2[:, u, c, :])
                    ins.then_inc(s_st2, 1)
                    dve.wait_ge(s_st2, b * 2 + 1)
                    dve.sem_inc(s_held, 1)
                    for c in range(TC):
                        ins = nc.vector.bn_aggr(mv2[:, c, :], stat2[:, c, :])
                    ins.then_inc(s_st2, 1)
                    dve.wait_ge(s_st2, b * 2 + 2)
                    nc.vector.tensor_scalar_add(var2[:], mv2[:, :, 1], EPS).then_inc(s_v2, 1)
                    dve.wait_ge(s_r2, b + 1)
                    for c in range(TC):
                        ins = nc.vector.tensor_scalar(xn2[:, c, :], x2[:, u, c, :], mv2[:, c, 0:1], rstd2[:, c:c + 1],
                                                      ALU.subtract, ALU.mult)
                    ins.then_inc(s_xn2, 1)
                    dve.wait_ge(s_xn2, b + 1)
                    nc.vector.tensor_tensor(xn2[:], xn2[:],
                                            modrow[:, ds(b, 1), M_CB * D:(M_CB + 1) * D].to_broadcast([128, TC, D]),
                                            ALU.mult).then_inc(s_xm2, 1)
                    dve.wait_ge(s_ge, b + 2)
                    nc.vector.tensor_scalar_add(ge[:], ge[:], 1.0).then_inc(s_g1, 1)
                    dve.wait_ge(s_g1, b + 1)
                    nc.vector.reciprocal(rw[:, u, :, D:D + NE], ge[:].rearrange("p (c e) -> p c e", e=NE)).then_inc(s_g, 1)

            dve.wait_ge(s_sig, 1)
            nc.vector.tensor_scalar_add(junk, sv, 1.0).then_inc(s_sig, 1)
            dve.wait_ge(l_top, 16 * 8)
            dve.wait_ge(s_sig, 2)
            nc.vector.reciprocal(sv, junk).then_inc(s_sig, 1)
            nc.vector.memset(cand, 1 << 29).then_inc(s_sig, 1)
            dve.wait_ge(s_sig, 4)
            with dve.Fori(0, 30) as k:
                nc.vector.tensor_scalar(junk, sv, cand.bitcast(fp32), None, ALU.is_ge, ALU.add,
                                        accum_out=cnt).then_inc(s_cnt, 1)
                dve.wait_ge(s_tot, k + 1)
                nc.vector.tensor_scalar(flip, ps[:, 0, 0:1], float(TOP), bitf[:, ds(k, 1)], ALU.is_lt,
                                        ALU.mult).then_inc(s_cand, 1)
                dve.wait_ge(s_cand, k * 2 + 1)
                nc.vector.scalar_tensor_tensor(out=cand, in0=cand, scalar=bitn[:, ds(k, 1)], in1=flip,
                                               op0=ALU.bitwise_xor, op1=ALU.bitwise_xor).then_inc(s_cand, 1)
                dve.wait_ge(s_cand, k * 2 + 2)

            step_ = [0]

            def link(ins):
                step_[0] += 1
                ins.then_inc(s_tk, 1)
                dve.wait_ge(s_tk, step_[0])

            link(nc.vector.tensor_scalar(gt, sv, cand.bitcast(fp32), None, ALU.is_gt, ALU.add, accum_out=cnt_gt))
            link(nc.vector.tensor_scalar(eq, sv, cand.bitcast(fp32), None, ALU.is_equal))
            dve.wait_ge(s_ones, 1)
            nc.vector.tensor_tensor_scan(ep, ones[:], eq, 0.0, ALU.mult, ALU.add).then_inc(s_sel, 1)
            dve.wait_ge(s_selp, 1)
            link(nc.vector.tensor_scalar(lim1, ps[:, 0, 0:1], -1.0, float(TOP), ALU.mult, ALU.add))
            link(nc.vector.tensor_tensor(lim, lim1, ps[:, 0, 1:2], ALU.subtract))
            link(nc.vector.scalar_tensor_tensor(out=junk, in0=ep, scalar=lim, in1=eq, op0=ALU.is_le, op1=ALU.mult))
            link(nc.vector.tensor_tensor(sel, junk, gt, ALU.add))
            nc.vector.tensor_tensor_scan(pp, ones[:], sel, 0.0, ALU.mult, ALU.add).then_inc(s_sel, 1)
            dve.wait_ge(s_selp, 2)
            nc.vector.scalar_tensor_tensor(out=junk, in0=pp, scalar=ps[:, 0, 2:3], in1=sel, op0=ALU.add,
                                           op1=ALU.mult).then_inc(s_sel, 1)
            dve.wait_ge(s_selp, 3)
            link(nc.vector.tensor_scalar(posi, ps[:, 1, 0:128], -1.0, None, ALU.add))
            link(nc.vector.tensor_scalar(posa, posi, 5, None, ALU.arith_shift_right))
            link(nc.vector.tensor_scalar(posb, posi, 31, None, ALU.bitwise_and))
            link(nc.vector.tensor_tensor(one_a, posa.unsqueeze(2).to_broadcast([128, 128, 16]),
                                         iota32[:, 0:16].unsqueeze(1).to_broadcast([128, 128, 16]), ALU.is_equal))
            link(nc.vector.tensor_tensor(one_a.rearrange("p (e s) a -> p e s a", e=NE),
                                         one_a.rearrange("p (e s) a -> p e s a", e=NE),
                                         tok16[:].unsqueeze(1).unsqueeze(3).to_broadcast([128, NE, NSEG, 16]),
                                         ALU.mult))
            nc.vector.tensor_tensor(one_b, posb.unsqueeze(2).to_broadcast([128, 128, 32]),
                                    iota32[:].unsqueeze(1).to_broadcast([128, 128, 32]),
                                    ALU.is_equal).then_inc(s_slot, 1)
            dve.wait_ge(s_slot, 4)
            for w in range(4):
                nc.vector.tensor_copy(idx[32 * w:32 * w + 32, :, :],
                                      ps[0:32, 2, 0:128].rearrange("p (e c w) -> p e c w", e=NE, w=4)[:, :, :, w]
                                      ).then_inc(s_idx, 1)

            def rows_up(e, u):
                dve.wait_ge(s_gt, e + 1)
                nc.vector.tensor_copy(exT[:, u, :], ps[:, 0, :]).then_inc(s_gx, 1)

            def gated(e, u):
                dve.wait_ge(s_dn, e + 1)
                if not (isinstance(e, int) and e < 2):
                    dve.wait_ge(w_sc[u], (e // 2) * 64)
                dve.wait_ge(s_yo, e + 2)
                b2v = b2r[:, e:e + 1, :] if isinstance(e, int) else b2r[:, ds(e, 1), :]
                nc.vector.tensor_tensor(yb, ps[:, 5 + u, :].rearrange("p (c d) -> p c d", c=SC),
                                        b2v.to_broadcast([128, SC, D]), ALU.add).then_inc(s_yb, 1)
                dve.wait_ge(s_yb, e + 1)
                for c in range(SC):
                    g = ex[:, u, c, D + e:D + e + 1] if isinstance(e, int) else ex[:, u, c, ds(e + D, 1)]
                    ins = nc.vector.scalar_tensor_tensor(out=ys[:, u, c, :], in0=yb[:, c, :], scalar=g,
                                                         in1=ex[:, u, c, D + NE:HW], op0=ALU.mult, op1=ALU.mult)
                ins.then_inc(s_yo, 1)

            rows_up(0, 0)
            rows_up(1, 1)
            gated(0, 0)
            rows_up(2, 0)
            gated(1, 1)
            with dve.Fori(1, NE // 2 - 1) as it:
                rows_up(it * 2 + 1, 1)
                gated(it * 2, 0)
                rows_up(it * 2 + 2, 0)
                gated(it * 2 + 1, 1)
            rows_up(NE - 1, 1)
            gated(NE - 2, 0)
            gated(NE - 1, 1)

        @block.tensor
        def _(pe):
            mm = nc.tensor.matmul
            pe.wait_ge(s_silu, 4)
            for j in range(2):
                ins = mm(ps[:, 4, j * NB:(j + 1) * NB], wmod[:, j * D:(j + 1) * D], se[:, 3, :], start=True, stop=True)
            ins.then_inc(s_mod, 1)
            for b in range(NB):
                mm(ps[:, b, :], se[:, 3, b:b + 1].to_broadcast([D, 128]), wmod[:, 2 * D:6 * D],
                   start=True, stop=True).then_inc(s_mod, 1)

            pe.wait_ge(l_w, 64)
            pe.wait_ge(s_modr, NB)
            pe.wait_ge(s_modc, 2)
            with pe.Fori(0, NB // 2) as it:
                for u in range(2):
                    b = it * 2 + u
                    pe.wait_ge(s_xn, b + 1)
                    pe.wait_ge(s_vd, b + 1)
                    for c in range(TC):
                        ins = nc.tensor.transpose(ps[:, 0, c * 128:(c + 1) * 128], xn[:, u, c, :], ident[:])
                    ins.then_inc(s_T, 1)
                    pe.wait_ge(s_hT, b + 1)
                    mm(ps[:, 1, :], w_x[:, 0:D], hT[:, u, :], start=True, stop=True).then_inc(s_CT, 1)
                    pe.wait_ge(s_kt, b + 1)
                    mm(ps[:, 2, :], w_x[:, D:2 * D], hT[:, u, :], start=True, stop=True)
                    mm(ps[:, 3, :], w_x[:, 2 * D:3 * D], hT[:, u, :], start=True, stop=True).then_inc(s_kAB, 1)
                    pe.wait_ge(s_ct, b + 1)
                    pe.wait_ge(s_kf, b + 1)
                    mm(ps[:, 5, :], w_ct[64:128, 0:D], ct[64:128, u, :], start=True, stop=True).then_inc(s_kc, 1)
                    pe.wait_ge(s_qt, b + 1)
                    mm(ps[:, 6, :], w_ct[0:64, D:2 * D], ct[0:64, u, :], start=True, stop=True)
                    mm(ps[:, 7, :], w_ct[0:64, 2 * D:3 * D], ct[0:64, u, :], start=True, stop=True).then_inc(s_qAB, 1)
                    pe.wait_ge(s_u, b + 1)
                    mm(ps[:, 4, :], w_ct[0:64, 0:D], ct[0:64, u, :], start=True, stop=True).then_inc(s_qc, 1)
                    for c in range(TC):
                        ins = mm(ps[:, 0, c * 128:(c + 1) * 128], ct[64:128, u, c * 128:(c + 1) * 128],
                                 w_ct[64:128, D:2 * D], start=True, stop=True)
                    ins.then_inc(s_V, 1)

            def max_unit(s, u, n):
                i, qc = n // 4, n % 4
                if n == 0:
                    pe.wait_ge(l_m[u], (s // 2 + 1) * 64)
                if not (isinstance(s, int) and 8 * s + n < 2):
                    pe.wait_ge(s_mxd, 8 * s + n - 1)
                for half in range(2):
                    r = slice(64 * half, 64 * half + PR)
                    ins = mm(ps[:, 2 * (n % 2) + half, :], MQ[r, u, i, qc * 128:(qc + 1) * 128], MK[r, u, i, :],
                             start=True, stop=True)
                ins.then_inc(s_mx, 1)

            def max_turn(s, u):
                pe.wait_ge(s_mxd, 8 * s + 8)
                if not (isinstance(s, int) and s < 4):
                    pe.wait_ge(s_no, s - 3)
                if not (isinstance(s, int) and s == 0):
                    pe.wait_ge(s_mn, s)
                nc.tensor.transpose(ps[0:16, 7, 0:128], mx[:, u, :], ident[:]).then_inc(s_mt, 1)

            def exp_unit(s, u, n):
                i, kc, half = n // 8, (n // 2) % 4, n % 2
                if n == 0:
                    pe.wait_ge(l_e[u], (s // 2 + 1) * 160)
                if not (isinstance(s, int) and 16 * s + n < 2):
                    pe.wait_ge(s_ex, 16 * s + n - 1)
                r = slice(64 * half, 64 * half + PR + 3)
                mm(ps[:, 4 + half, :], EK[r, u, i, kc * 128:(kc + 1) * 128], EQ[r, u, i, :],
                   start=True, stop=True).then_inc(s_sc, 1)

            def weigh(s, u, kc):
                if kc == 0:
                    pe.wait_ge(s_ex, 16 * s + 16)
                    pe.wait_ge(s_va, s + 1)
                    if not (isinstance(s, int) and s == 0):
                        pe.wait_ge(s_oe, s)
                for j in range(4):
                    ins = mm(ps[32 * j:32 * j + 32, 6, :], VA[:, u, kc, j, :], PT[:, u, j, kc, :],
                             start=kc == 0, stop=kc == TC - 1)
                if kc == TC - 1:
                    ins.then_inc(s_pv, 1)

            def out_turn(s):
                pe.wait_ge(s_oe, s + 1)
                pe.wait_ge(s_mn, s + 4 if not isinstance(s, int) else min(s + 4, NS))
                if not (isinstance(s, int) and s == 0):
                    pe.wait_ge(s_no, s)
                for c in range(TC):
                    ins = nc.tensor.transpose(ps[:, 7, c * 128:(c + 1) * 128], osb[:, c * 128:(c + 1) * 128], ident[:])
                ins.then_inc(s_ot, 1)

            def step(s, u, prev=True, prev2=True, more_max=True, turn=True):
                for n in range(8):
                    if n == 1 and turn:
                        max_turn(s + 1, 1 - u)
                    if n == 4 and prev2:
                        out_turn(s - 2)
                    if more_max:
                        max_unit(s + 2, u, n)
                    exp_unit(s, u, 2 * n)
                    exp_unit(s, u, 2 * n + 1)
                    if n % 2 and prev:
                        weigh(s - 1, 1 - u, n // 2)

            for n in range(8):
                max_unit(0, 0, n)
            max_turn(0, 0)
            for n in range(8):
                max_unit(1, 1, n)
            max_turn(1, 1)
            step(0, 0, prev=False, prev2=False, turn=False)
            step(1, 1, prev2=False)
            with pe.Fori(1, NS // 2 - 1) as it:
                step(it * 2, 0)
                step(it * 2 + 1, 1)
            step(14, 0, more_max=False)
            step(15, 1, more_max=False, turn=False)
            for kc in range(TC):
                weigh(15, 1, kc)
            out_turn(14)
            out_turn(15)

            pe.wait_ge(s_prep, 10)
            with pe.Fori(0, NB // 2) as it:
                for u in range(2):
                    b = it * 2 + u
                    pe.wait_ge(s_ab, b + 1)
                    pe.wait_ge(s_aTe, b + 1)
                    for c in range(TC):
                        ins = nc.tensor.transpose(ps[:, 0, c * 128:(c + 1) * 128], Ab[:, u, c, :], ident[:])
                    ins.then_inc(s_aT, 1)
                    pe.wait_ge(s_aTe, b + 2)
                    pe.wait_ge(s_x2, b + 1)
                    for c in range(TC):
                        ins = mm(ps[:, 1, c * 128:(c + 1) * 128], aT[:, u, c * 128:(c + 1) * 128],
                                 wo_g[:, ds(b, 1), :].rearrange("p o d -> p (o d)"), start=True, stop=True)
                    ins.then_inc(s_y, 1)
                    pe.wait_ge(s_h2, b + 1)
                    pe.wait_ge(s_h2e, b + 1)
                    for c in range(TC):
                        ins = nc.tensor.transpose(ps[:, 2, c * 128:(c + 1) * 128], rw[:, u, c, 0:D], ident[:])
                    ins.then_inc(s_h2t, 1)
                    pe.wait_ge(s_h2e, b + 2)
                    pe.wait_ge(s_lge, b + 1)
                    pe.wait_ge(s_ge, b + 1)
                    mm(ps[0:NE, 3, :], wg[:], h2T[:, u, :], start=True, stop=True)
                    for c in range(TC):
                        ins = mm(ps[:, 4, c * NE:(c + 1) * NE], h2T[:, u, c * 128:(c + 1) * 128], wg[:],
                                 start=True, stop=True)
                    ins.then_inc(s_gl, 1)

            pe.wait_ge(l_top, 16 * 8)
            with pe.Fori(0, 30) as k:
                pe.wait_ge(s_cnt, k + 1)
                mm(ps[:, 0, 0:1], same_e[:], cnt, start=True, stop=True).then_inc(s_tot, 1)
            pe.wait_ge(s_sel, 1)
            mm(ps[:, 0, 0:1], same_e[:], cnt_gt, start=True, stop=True)
            mm(ps[:, 0, 1:2], lower[:], ep[:, 127:128], start=True, stop=True).then_inc(s_selp, 1)
            pe.wait_ge(s_sel, 2)
            mm(ps[:, 0, 2:3], lower[:], pp[:, 127:128], start=True, stop=True).then_inc(s_selp, 1)
            pe.wait_ge(s_sel, 3)
            nc.tensor.transpose(ps[:, 1, 0:128], junk, ident[:]).then_inc(s_selp, 1)
            pe.wait_ge(s_slot, 1)
            for e in range(NE):
                for s in range(NSEG):
                    ins = mm(ps[0:16, 1, 32 * e:32 * e + 32], one_a[:, e * NSEG + s, :], one_b[:, e * NSEG + s, :],
                             start=s == 0, stop=s == NSEG - 1)
            ins.then_inc(s_slot, 1)
            pe.wait_ge(s_slot, 3)
            for e in range(NE):
                ins = nc.tensor.transpose(ps[0:32, 2, 16 * e:16 * e + 16], slots[0:16, 32 * e:32 * e + 32],
                                          ident[0:16, 0:16])
            ins.then_inc(s_slot, 1)

            def turn(e, u):
                pe.wait_ge(g_in[u], (e // 2 + 1) * 64)
                for c in range(SC):
                    ins = nc.tensor.transpose(ps[:, 0, c * 128:(c + 1) * 128], ex[:, u, c, 0:D], ident[:])
                ins.then_inc(s_gt, 1)

            def expert(e, u, more=True):
                pe.wait_ge(s_gx, e + 1)
                pe.wait_ge(l_w12[u], (e // 2 + 1) * 32)
                for f in range(FC):
                    mm(ps[:, 1 + f, :], w1s[:, u, f * 128:(f + 1) * 128], exT[:, u, :],
                       start=True, stop=True).then_inc(s_up, 1)
                if more:
                    turn(e + 1, 1 - u)
                pe.wait_ge(s_gelu, e * FC + FC)
                pe.wait_ge(s_yo, e + 1)
                for c in range(SC):
                    for f in range(FC):
                        ins = mm(ps[:, 5 + u, c * 128:(c + 1) * 128], hid[:, f, c * 128:(c + 1) * 128],
                                 w2s[:, u, f, :], start=f == 0, stop=f == FC - 1)
                ins.then_inc(s_dn, 1)

            turn(0, 0)
            with pe.Fori(0, NE // 2 - 1) as it:
                expert(it * 2, 0)
                expert(it * 2 + 1, 1)
            expert(NE - 2, 0)
            expert(NE - 1, 1, more=False)


def tables():
    ids = np.arange(D // 2, dtype=np.float32)
    theta = (np.float32(10000.0) ** (np.float32(-2.0) * ids) / np.float32(D // 2)).astype(np.float32)
    r = np.arange(L, dtype=np.float32)[None, :] * theta[:, None]
    cos, sin = np.repeat(np.cos(r), 2, 0), np.repeat(np.sin(r), 2, 0)
    sin[0::2] *= -1.0
    return cos.astype(np.float32), sin.astype(np.float32)


def kernel(**inputs):
    import concourse.bacc as bacc
    from concourse.bass_utils import run_bass_kernel_spmd as run

    a = {k.replace("L0_attn_", "").replace("L0_ffn_", "").replace("L0_", ""): np.asarray(v) for k, v in inputs.items()}
    order = np.array([(8 * half + h8) * HD + d for half in range(2) for d in range(HD) for h8 in range(8)])
    swapped = order ^ 1
    vorder = np.array([(8 * half + 2 * g + i) * HD + d
                       for g in range(4) for i in range(2) for half in range(2) for d in range(HD)])
    cos, sin = tables()
    part = np.arange(128)
    seg = part // (128 // NE)
    arrays = {
        "x": a["x"],
        "cT": a["c"].T,
        "wmod": a["wmod"],
        "w_x": np.concatenate([a["Wd_q_w"], a["Wd_kv_w"], a["Wk_r_w"][:, order], a["Wk_r_w"][:, swapped]], 1),
        "w_ct": np.concatenate([
            np.concatenate([a["Wu_q_w"][:, order], a["Wq_r_w"][:, order], a["Wq_r_w"][:, swapped]], 1),
            np.concatenate([a["Wu_k_w"][:, order], a["Wu_v_w"][:, vorder], np.zeros((DC, D), np.float32)], 1)], 0),
        "bcol": np.stack([np.concatenate([a["Wd_q_b"], a["Wd_kv_b"]]), a["Wu_q_b"][order], a["Wq_r_b"][order],
                          a["Wq_r_b"][swapped], a["Wu_k_b"][order], a["Wk_r_b"][order], a["Wk_r_b"][swapped]], 1),
        "brow": np.stack([a["Wu_v_b"][vorder], a["Wo_b"]]),
        "cos": cos[order], "sin": sin[order],
        "wo": a["Wo_w"][vorder, :],
        "wg": a["Wg"],
        "ident": np.eye(128, dtype=np.float32),
        "w1": a["W1"], "w2": a["W2"], "b2": a["b2"],
        "b1c": a["b1"].reshape(NE, FC, 128).transpose(2, 0, 1),
        "same_e": (seg[:, None] == seg[None, :]).astype(np.float32),
        "lower": ((seg[:, None] == seg[None, :]) & (part[:, None] < part[None, :])).astype(np.float32),
        "bitf": np.tile(2.0 ** np.arange(29, -1, -1), (128, 1)).astype(np.float32),
        "bitn": np.tile(np.append(1 << np.arange(28, -1, -1), 0), (128, 1)).astype(np.int32),
        "iota32": np.tile(np.arange(32), (128, 1)).astype(np.float32),
        "tok16": (np.arange(128 // NE)[None, :] * 128 + part[:, None]).astype(np.float32),
    }
    arrays = {k: np.ascontiguousarray(v) for k, v in arrays.items()}
    nc = bacc.Bacc("TRN2", target_bir_lowering=False, num_devices=1)
    t = {k: nc.dram_tensor("in_" + k, list(v.shape), mybir.dt.from_np(v.dtype), kind="ExternalInput").ap()
         for k, v in arrays.items()}
    out = nc.dram_tensor("out", [NB, L, D], mybir.dt.float32, kind="ExternalOutput").ap()
    build(nc, t, out)
    r = run(nc, [{"in_" + k: v for k, v in arrays.items()}], core_ids=[0])
    return r.results[0]["out"]
```

```python
import numpy as np
import concourse.bass as bass
from concourse import mybir
from contextlib import ExitStack

NB, L, D = 4, 512, 128
NT = NB * L
NH, HD = 16, 8
DC = 64
TC = L // 128
NS = NB * NH // 4
NE, FF, CAP = 8, 512, 2
TOP = NT * CAP // NE
FC = FF // 128
SC = TOP // 128
SCALE = 1.0 / 12.0
EPS = 1e-5
PART_Q = [0, 0, 0, 1, 1, 2]
PART_K = [1, 0, 2, 0, 1, 0]
PR = 8 * len(PART_Q)
HW = D + NE + D
ROUNDS = 15
M_GA, M_SB, M_CB, M_GB = range(4)


def build(nc, t, out):
    fp32, bf16, fp16, i32 = mybir.dt.float32, mybir.dt.bfloat16, mybir.dt.float16, mybir.dt.int32
    ACT = mybir.ActivationFunctionType
    ALU = mybir.AluOpType
    AX = mybir.AxisListType
    ds = bass.ds

    qs_dram = nc.dram_tensor("q_parts", [NB, len(PART_Q), 2, HD, 8, L], bf16, kind="Internal").ap()
    ks_dram = nc.dram_tensor("k_parts", [NB, len(PART_Q), 2, HD, 8, L], bf16, kind="Internal").ap()
    logit_dram = nc.dram_tensor("logits", [NE, NT], fp32, kind="Internal").ap()
    rows_dram = nc.dram_tensor("rows", [NT, HW], fp32, kind="Internal").ap()

    ctx = ExitStack()
    with ctx:
        def sb(name, shape, dt=fp32):
            return ctx.enter_context(nc.sbuf_tensor(name, shape, dt))

        def sem(name):
            return ctx.enter_context(nc.semaphore(name))

        X = sb("X", [128, NB * TC, D])
        cT = sb("cT", [D, NB])
        wmod = sb("wmod", [D, 6 * D])
        w_x = sb("w_x", [D, 3 * D])
        w_ct = sb("w_ct", [128, 5 * D])
        bcol = sb("bcol", [D, 7])
        bv_row = sb("bv_row", [128, D])
        bo_row = sb("bo_row", [128, D])
        cos_t = sb("cos_t", [D, L])
        sin_t = sb("sin_t", [D, L])
        wo = sb("wo", [D, D])
        wg = sb("wg", [D, NE])
        ident = sb("ident", [128, 128])

        se = sb("se", [D, 4, NB])
        modcol = sb("modcol", [D, 2, NB])
        modrow = sb("modrow", [128, NB, 4 * D])
        wo_g = sb("wo_g", [D, NB, D])
        bo_g = sb("bo_g", [128, NB, D])

        stat = sb("stat", [128, NB * TC, 6])
        mv = sb("mv", [128, NB * TC, 2])
        var = sb("var", [128, NB * TC])
        rstd = sb("rstd", [128, NB * TC])
        mhalf = sb("mhalf", [128, NB * TC])
        Vall = sb("Vall", [128, NB, 4, TC, 32])

        MQ, EK = (sb(n, [128, 2, 2, L], bf16) for n in ("MQ", "EK"))
        MK, EQ = (sb(n, [128, 2, 2, 2, L], bf16) for n in ("MK", "EQ"))
        mx = sb("mx", [128, 2, 16])
        mxn, mxr = (sb(n, [16, 128]) for n in ("mxn", "mxr"))
        mxp = sb("mxp", [16, 2, 3, 128], bf16)
        big = sb("big", [128, 2 * 4 * TC * L])
        PT = big[:, :].rearrange("p (u j c q) -> p u j c q", u=2, j=4, c=TC)
        VA = sb("VA", [128, 2, TC, 4, 32])
        osb = sb("osb", [128, L])
        rs = sb("rs", [128, 16])
        An = sb("An", [128, NB, TC, 4, 32])

        def carve():
            at = [0]

            def view(*shape, dt=fp32):
                n = int(np.prod(shape)) * (4 if dt in (fp32, i32) else 2) // 4
                v = big[:, at[0]:at[0] + n]
                at[0] += n
                assert at[0] <= 2 * 4 * TC * L
                v = v if dt == fp32 else v.bitcast(dt)
                names = "abcd"[:len(shape)]
                return v.rearrange(f"p ({' '.join(names)}) -> p {' '.join(names)}", **dict(zip(names, shape)))
            return view

        view = carve()
        xn = view(NB * TC, D)
        hT, ct = view(NB, L), view(NB, L)
        kcs, kss, kad, kf, kr = (view(L) for _ in range(5))
        qcs, qss, qad, qu, qf, qr = (view(L) for _ in range(6))
        kp, qp = view(2, 3, L, dt=bf16), view(2, 3, L, dt=bf16)
        sgn, mag = sb("sgn", [128, NB, 2, D]), sb("mag", [128, NB, 2, D])
        view = carve()
        x2, rw = view(NB * TC, D), view(NB * TC, D + NE)
        aT, xn2, h2T = view(2, L), view(2, TC, D), view(2, L)
        lgs, ge = view(NT), view(NB * TC * NE)
        stat2, mv2 = view(NB * TC, 6), view(NB * TC, 2)
        var2, rstd2 = view(NB * TC), view(NB * TC)

        NSEG = 128 // NE
        lg = view(128)
        sv, junk, gt, eq, ep, sel, pp = (view(128) for _ in range(7))
        cnt3, reach3, ge3 = view(3), view(3), view(3, 128)
        reached, cnt_gt, lim, lim1 = (view(1) for _ in range(4))
        cand3, base, found = view(3, dt=i32), view(1, dt=i32), view(1, dt=i32)
        posi, posa, posb = (view(128, dt=i32) for _ in range(3))
        one_a, one_b = view(128, 16, dt=fp16), view(128, 32, dt=fp16)
        slots = view(NE * 32)
        assert NSEG * 128 == NT
        ex = sb("ex", [128, 2, SC, HW])
        w1s, w2s = sb("w1s", [D, 2, FF]), sb("w2s", [128, 2, FC, D])
        view = carve()
        exT, hid, yb, gg, ys = view(2, TOP), view(2, FC, TOP), view(2, SC, D), view(2, SC, D), view(2, SC, D)
        idx = sb("idx", [128, NE, SC], i32)
        b1c, b2r = sb("b1c", [128, NE, FC]), sb("b2r", [128, NE, D])
        same_e, lower = sb("same_e", [128, 128]), sb("lower", [128, 128])
        scale_t, cand_t = sb("scale_t", [128, ROUNDS]), sb("cand_t", [128, ROUNDS + 1, 3], i32)
        iota32, tok16 = sb("iota32", [128, 32]), sb("tok16", [128, NSEG])
        ones = sb("ones", [128, 128])

        ps = ctx.enter_context(nc.psum_tensor("ps", [128, 8, 512], fp32))

        l_x = [sem(f"l_x{b}") for b in range(NB)]
        l_w, l_tab, l_c = sem("l_w"), sem("l_tab"), sem("l_c")
        s_silu, s_mod, s_modc, s_modr = sem("s_silu"), sem("s_mod"), sem("s_modc"), sem("s_modr")
        s_stat, s_ln = sem("s_stat"), sem("s_ln")
        s_const = sem("s_const")
        s_rstd, s_xn = sem("s_rstd"), sem("s_xn")
        s_T, s_hT, s_CT, s_ct, s_V, s_vd = (sem(n) for n in ("s_T", "s_hT", "s_CT", "s_ct", "s_V", "s_vd"))
        s_held = sem("s_held")
        s_kt, s_qt, s_kf, s_u, s_qad, s_qf = (sem(n) for n in ("s_kt", "s_qt", "s_kf", "s_u", "s_qad", "s_qf"))
        s_kAB, s_qAB, s_qc, s_kc = (sem(n) for n in ("s_kAB", "s_qAB", "s_qc", "s_kc"))
        s_kad, s_kh, s_kr, s_km, s_kl = (sem(n) for n in ("s_kad", "s_kh", "s_kr", "s_km", "s_kl"))
        s_qh, s_qr, s_qm, s_ql = (sem(n) for n in ("s_qh", "s_qr", "s_qm", "s_ql"))
        w_k = [sem(f"w_k{u}") for u in range(2)]
        w_q = [sem(f"w_q{u}") for u in range(2)]

        s_one = sem("s_one")
        s_gate = sem("s_gate")
        l_m = [sem(f"l_m{u}") for u in range(2)]
        l_e = [sem(f"l_e{u}") for u in range(2)]
        s_mx, s_mxd, s_mt, s_mn, s_pp, s_parts = (
            sem(n) for n in ("s_mx", "s_mxd", "s_mt", "s_mn", "s_pp", "s_parts"))
        s_sc, s_ex, s_va, s_pv, s_oe, s_ot, s_rs, s_no = (
            sem(n) for n in ("s_sc", "s_ex", "s_va", "s_pv", "s_oe", "s_ot", "s_rs", "s_no"))
        s_prep = sem("s_prep")

        s_aT, s_aTe, s_y, s_x2 = (sem(n) for n in ("s_aT", "s_aTe", "s_y", "s_x2"))
        s_st2, s_v2, s_r2, s_xn2, s_xm2, s_h2 = (
            sem(n) for n in ("s_st2", "s_v2", "s_r2", "s_xn2", "s_xm2", "s_h2"))
        s_h2t, s_h2e, s_lg, s_lge, s_gl, s_ge, s_g1, s_g = (
            sem(n) for n in ("s_h2t", "s_h2e", "s_lg", "s_lge", "s_gl", "s_ge", "s_g1", "s_g"))
        w_out, w_row = sem("w_out"), sem("w_row")
        w_gb = sem("w_gb")

        l_top, l_lg = sem("l_top"), sem("l_lg")
        s_cnt, s_tot, s_cand, s_sig, s_sel, s_selp, s_tk = (
            sem(n) for n in ("s_cnt", "s_tot", "s_cand", "s_sig", "s_sel", "s_selp", "s_tk"))
        s_slot, s_idx, s_ones = sem("s_slot"), sem("s_idx"), sem("s_ones")
        l_w12 = [sem(f"l_w12_{u}") for u in range(2)]
        g_in = [sem(f"g_in{u}") for u in range(2)]
        w_sc = [sem(f"w_sc{u}") for u in range(2)]
        s_gt, s_gx, s_gg, s_up, s_gelu, s_dn, s_yb, s_yo = (
            sem(n) for n in ("s_gt", "s_gx", "s_gg", "s_up", "s_gelu", "s_dn", "s_yb", "s_yo"))

        block = ctx.enter_context(nc.Block())

        @block.sync
        def _(sp):
            sp.dma_start(cT[:], t["cT"]).then_inc(l_c, 16)
            sp.dma_start(wmod[:], t["wmod"]).then_inc(l_c, 16)
            for b in range(NB):
                sp.dma_start(X[:, b * TC:(b + 1) * TC, :],
                             t["x"][b].rearrange("(c p) d -> p c d", p=128)).then_inc(l_x[b], 16)
            for dst, src in ((ident, "ident"), (w_x, "w_x"), (w_ct, "w_ct"), (bcol, "bcol")):
                sp.dma_start(dst[:], t[src]).then_inc(l_w, 16)
            sp.dma_start(cos_t[:], t["cos"]).then_inc(l_tab, 16)
            sp.dma_start(sin_t[:], t["sin"]).then_inc(l_tab, 16)
            sp.dma_start(bv_row[:], t["brow"][0:1, :].to_broadcast([128, D])).then_inc(l_tab, 16)
            sp.dma_start(bo_row[:], t["brow"][1:2, :].to_broadcast([128, D])).then_inc(l_tab, 16)
            sp.dma_start(wo[:], t["wo"]).then_inc(l_tab, 16)
            sp.dma_start(wg[:], t["wg"]).then_inc(l_tab, 16)
            for dst, src in ((b1c, "b1c"), (same_e, "same_e"), (lower, "lower"), (scale_t, "scale_t"), (cand_t, "cand_t"),
                             (iota32, "iota32"), (tok16, "tok16")):
                sp.dma_start(dst[:], t[src]).then_inc(l_top, 16)
            sp.dma_start(b2r[:], t["b2"].unsqueeze(0).to_broadcast([128, NE, D])).then_inc(l_top, 16)

            def store_parts(b, u):
                for buf, dram, order, done, w in ((kp, ks_dram, PART_K, s_kl, w_k),
                                                  (qp, qs_dram, PART_Q, s_ql, w_q)):
                    sp.wait_ge(done, b + 1)
                    places = dram[b].rearrange("j a d h t -> (a d h) j t")
                    for p in range(3):
                        at = [j for j in range(len(order)) if order[j] == p]
                        step = at[1] - at[0] if len(at) > 1 else 1
                        sp.dma_start(
                            places[:, at[0]:at[-1] + 1:step, :],
                            buf[:, u, p, :].unsqueeze(1).to_broadcast([128, len(at), L])).then_inc(w[u], 16)

            def load_group(s, kbuf, qbuf, slot, done):
                for buf, part in ((kbuf, ks_dram), (qbuf, qs_dram)):
                    for half in range(2):
                        if isinstance(s, int):
                            src = part[s // 4:s // 4 + 1, :, half, :, 2 * (s % 4):2 * (s % 4) + 2, :]
                        else:
                            src = part[ds(s // 4, 1), :, half, :, ds((s % 4) * 2, 2), :]
                        rows = slice(64 * half, 64 * half + PR)
                        sp.dma_start(buf[rows, slot, half] if buf in (MK, EQ) else buf[rows, slot],
                                     src.rearrange("o j d i t -> (o j) d (i t)")).then_inc(done, 16)

            def load_max(s, slot):
                sp.wait_ge(s_parts, s + 1)
                for half in range(2):
                    for p in range(3):
                        r = 64 * half + PR + p
                        sp.dma_start(EQ[r:r + 1, slot, half].rearrange("p i q -> p (i q)"),
                                     mxp[8 * half:8 * half + 8, slot, p, :]).then_inc(l_e[slot], 16)

            def step(s, u, more_max=True, more=True):
                if more_max:
                    sp.wait_ge(s_mx, 8 * (s + 2))
                    load_group(s + 3, MK, MQ, 1 - u, l_m[1 - u])
                if more:
                    if not (isinstance(s, int) and s == 0):
                        sp.wait_ge(s_sc, 16 * s)
                    load_group(s + 1, EK, EQ, 1 - u, l_e[1 - u])
                    load_max(s + 1, 1 - u)

            store_parts(0, 0)
            store_parts(1, 1)
            sp.wait_ge(s_one, 4)
            sp.wait_ge(w_k[0], 16 + 48)
            sp.wait_ge(w_q[0], 16 + 48)
            load_group(0, MK, MQ, 0, l_m[0])
            load_group(1, MK, MQ, 1, l_m[1])
            load_group(0, EK, EQ, 0, l_e[0])
            store_parts(2, 0)
            store_parts(3, 1)
            sp.wait_ge(s_mx, 8)
            load_group(2, MK, MQ, 0, l_m[0])
            load_max(0, 0)
            for u in range(2):
                sp.wait_ge(w_k[u], 16 + 96)
                sp.wait_ge(w_q[u], 16 + 96)
            step(0, 0)
            step(1, 1)
            with sp.Fori(1, NS // 2 - 2) as it:
                step(it * 2, 0)
                step(it * 2 + 1, 1)
            step(12, 0)
            step(13, 1, more_max=False)
            step(14, 0, more_max=False)

            sp.wait_ge(s_gate, 1)
            for b in range(NB):
                sp.dma_start(
                    rows_dram[b * L:(b + 1) * L, D + NE:HW].rearrange("(c p) d -> p c d", p=128),
                    modrow[:, b:b + 1, M_GB * D:(M_GB + 1) * D].to_broadcast([128, TC, D])).then_inc(w_gb, 16)

            for b in range(NB):
                sp.wait_ge(s_x2, b + 1)
                sp.dma_start(out[b].rearrange("(c p) d -> p c d", p=128),
                             x2[:, b * TC:(b + 1) * TC, :]).then_inc(w_out, 16)
            sp.wait_ge(s_lge, NB)
            sp.dma_start(lg, lgs[0:NE, :]).then_inc(l_lg, 16)
            sp.wait_ge(s_g, 1)
            sp.dma_start(rows_dram[:, 0:D + NE].rearrange("(n p) d -> p n d", p=128), rw).then_inc(w_row, 16)

            def load_expert(e, u):
                if isinstance(e, int):
                    a, b = t["w1"][e], t["w2"][e]
                else:
                    sp.wait_ge(s_dn, e - 1)
                    a = t["w1"][ds(e, 1)].rearrange("o h f -> (o h) f")
                    b = t["w2"][ds(e, 1)].rearrange("o f h -> (o f) h")
                sp.dma_start(w1s[:, u, :], a).then_inc(l_w12[u], 16)
                sp.dma_start(w2s[:, u, :, :], b.rearrange("(c p) h -> p c h", p=128)).then_inc(l_w12[u], 16)

            load_expert(0, 0)
            load_expert(1, 1)
            with sp.Fori(1, NE // 2) as it:
                for u in range(2):
                    load_expert(it * 2 + u, u)

        @block.gpsimd
        def _(pool):
            for s_ in (s_kt, s_qt, s_kf, s_u, s_qad, s_qf):
                pool.sem_inc(s_, 1)
            for s_ in (*w_k, *w_q):
                pool.sem_inc(s_, 16)
            nc.gpsimd.memset(mhalf[:], -0.5).then_inc(s_const, 1)
            nc.gpsimd.memset(EK[:], 1.0).then_inc(s_one, 1)
            for buf in (MQ, MK, EQ):
                nc.gpsimd.memset(buf[:], 0.0).then_inc(s_one, 1)
            nc.gpsimd.memset(VA[:], 0.0).then_inc(s_prep, 1)
            pool.wait_ge(s_prep, 1)
            nc.gpsimd.memset(VA[:, :, :, :, HD:HD + 1], 1.0).then_inc(s_prep, 1)
            nc.gpsimd.memset(ones[:], 1.0).then_inc(s_ones, 1)
            pool.wait_ge(s_ln, 1)
            pool.wait_ge(s_const, 1)
            nc.gpsimd.tensor_tensor(rstd[:], var[:], mhalf[:], ALU.pow).then_inc(s_rstd, 1)
            with pool.Fori(0, NB // 2) as it:
                for u in range(2):
                    b = it * 2 + u
                    pool.wait_ge(s_qt, b + 2)
                    nc.gpsimd.tensor_tensor(qad[:], qcs[:], qss[:], ALU.add).then_inc(s_qad, 1)
                    pool.wait_ge(s_qad, b + 2)
                    pool.wait_ge(s_u, b + 2)
                    nc.gpsimd.tensor_tensor(qf[:], qad[:], qu[:], ALU.add).then_inc(s_qf, 1)
                    pool.wait_ge(s_qf, b + 2)
                    pool.wait_ge(s_qh, b + 1)
                    nc.gpsimd.tensor_tensor(qr[:], qf[:], qp[:, u, 0, :], ALU.subtract).then_inc(s_qr, 1)
                    pool.wait_ge(s_qm, b + 1)
                    nc.gpsimd.tensor_tensor(qp[:, u, 2, :], qr[:], qp[:, u, 1, :], ALU.subtract).then_inc(s_ql, 1)
            pool.wait_ge(s_prep, 2)

            def values(s, u):
                if not (isinstance(s, int) and s < 2):
                    pool.wait_ge(s_pv, s - 1)
                pool.sem_inc(s_held, 1)
                src = (Vall[:, s // 4, s % 4] if isinstance(s, int)
                       else Vall[:, ds(s // 4, 1), ds(s % 4, 1)].rearrange("p a b c d -> p (a b c) d"))
                nc.gpsimd.tensor_copy(VA[:, u, :, :, 0:HD],
                                      src.rearrange("p c (j d) -> p c j d", d=HD)).then_inc(s_va, 1)

            def max_parts(s, u):
                if not (isinstance(s, int) and s < 2):
                    pool.wait_ge(l_e[u], (s // 2) * 160)
                pool.wait_ge(s_mn, s + 1)
                pool.sem_inc(s_held, 1)
                nc.gpsimd.tensor_copy(mxp[:, u, 0, :], mxn[:]).then_inc(s_pp, 1)
                pool.wait_ge(s_pp, 3 * s + 1)
                nc.gpsimd.tensor_tensor(mxr[:], mxn[:], mxp[:, u, 0, :], ALU.subtract).then_inc(s_pp, 1)
                pool.wait_ge(s_pp, 3 * s + 2)
                pool.sem_inc(s_held, 1)
                nc.gpsimd.tensor_copy(mxp[:, u, 1, :], mxr[:]).then_inc(s_pp, 1)
                pool.wait_ge(s_pp, 3 * s + 3)
                nc.gpsimd.tensor_tensor(mxp[:, u, 2, :], mxr[:], mxp[:, u, 1, :],
                                        ALU.subtract).then_inc(s_parts, 1)

            max_parts(0, 0)
            values(0, 0)
            max_parts(1, 1)

            v = modrow[:, :, :].rearrange("p b (j c) -> p b j c", c=D)[:, :, 0:4:3, :]
            pool.wait_ge(s_modr, NB)
            nc.gpsimd.tensor_scalar(sgn[:], v, 0.0, 2.0, ALU.is_ge, ALU.mult).then_inc(s_prep, 1)
            pool.wait_ge(s_prep, 3)
            nc.gpsimd.tensor_scalar(sgn[:], sgn[:], -1.0, None, ALU.add).then_inc(s_prep, 1)
            pool.wait_ge(s_prep, 4)
            nc.gpsimd.tensor_tensor(mag[:], v, sgn[:], ALU.mult).then_inc(s_prep, 1)
            pool.wait_ge(s_prep, 5)
            nc.gpsimd.tensor_scalar(mag[:], mag[:], 0.25, None, ALU.max).then_inc(s_prep, 1)
            pool.wait_ge(s_prep, 6)
            nc.gpsimd.tensor_tensor(v, sgn[:], mag[:], ALU.mult).then_inc(s_prep, 1)
            cb = modrow[:, :, M_CB * D:(M_CB + 1) * D]
            nc.gpsimd.tensor_scalar(cb, cb, 1.0, None, ALU.add).then_inc(s_gate, 1)
            pool.wait_ge(s_prep, 7)
            ga = modrow[:, :, M_GA * D:(M_GA + 1) * D]
            pool.wait_ge(l_tab, 96)
            nc.gpsimd.tensor_tensor(wo_g[:], ga, wo[:].unsqueeze(1).to_broadcast([D, NB, D]),
                                    ALU.mult).then_inc(s_prep, 1)
            nc.gpsimd.tensor_tensor(bo_g[:], ga, bo_row[:].unsqueeze(1).to_broadcast([128, NB, D]),
                                    ALU.mult).then_inc(s_prep, 1)
            pool.wait_ge(s_prep, 9)
            xv = X[:, :, :].rearrange("p (b c) d -> p b c d", b=NB)
            nc.gpsimd.tensor_tensor(xv, xv, bo_g[:].unsqueeze(2).to_broadcast([128, NB, TC, D]),
                                    ALU.add).then_inc(s_prep, 1)

            values(1, 1)
            max_parts(2, 0)
            with pool.Fori(1, NS // 2 - 1) as it:
                values(it * 2, 0)
                max_parts(it * 2 + 1, 1)
                values(it * 2 + 1, 1)
                max_parts(it * 2 + 2, 0)
            values(14, 0)
            max_parts(15, 1)
            values(15, 1)

            def rstd_2(b):
                t4 = slice(b * TC, (b + 1) * TC)
                pool.wait_ge(s_v2, b + 1)
                nc.gpsimd.tensor_tensor(rstd2[:, t4], var2[:, t4], mhalf[:, 0:TC], ALU.pow).then_inc(s_r2, 1)

            def shift_2(b):
                pool.wait_ge(s_xm2, b + 1)
                nc.gpsimd.tensor_tensor(rw[:, b * TC:(b + 1) * TC, 0:D], xn2[:, b % 2],
                                        modrow[:, b:b + 1, M_SB * D:(M_SB + 1) * D].to_broadcast([128, TC, D]),
                                        ALU.add).then_inc(s_h2, 1)

            pool.wait_ge(s_gate, 1)
            rstd_2(0)
            for b in range(1, NB):
                rstd_2(b)
                shift_2(b - 1)
            shift_2(NB - 1)

            out_rows = out.rearrange("b l d -> (b l) d")

            def gather(e):
                if e >= 2:
                    pool.wait_ge(s_gg, e - 1)
                for c in range(SC):
                    pool.indirect_dma_start(
                        out=ex[:, e % 2, c, :], out_offset=None, in_=rows_dram,
                        in_offset=bass.IndirectOffsetOnAxis(ap=idx[:, e, c:c + 1], axis=0)).then_inc(g_in[e % 2], 16)

            def scatter(e):
                pool.wait_ge(s_yo, e + 1)
                if e > 0:
                    pool.wait_ge(w_sc[(e - 1) % 2], (e - 1) // 2 * 64 + 64)
                for c in range(SC):
                    pool.indirect_dma_start(
                        out=out_rows, out_offset=bass.IndirectOffsetOnAxis(ap=idx[:, e, c:c + 1], axis=0),
                        in_=ys[:, e % 2, c, :], in_offset=None, compute_op=ALU.add).then_inc(w_sc[e % 2], 16)

            pool.wait_ge(w_gb, 16 * NB)
            pool.wait_ge(w_row, 16)
            pool.wait_ge(w_out, 16 * NB)
            pool.wait_ge(s_idx, 4)
            for e in range(4):
                gather(e)
            for e in range(NE):
                scatter(e)
                if e + 4 < NE:
                    gather(e + 4)
            for u in range(2):
                pool.wait_ge(w_sc[u], 64 * (NE // 2))

        @block.scalar
        def _(act):
            act.wait_ge(l_c, 32)
            nc.scalar.activation(se[:, 0, :], cT[:], ACT.Exp, scale=-1.0).then_inc(s_silu, 1)
            for b in range(NB):
                act.wait_ge(s_mod, b + 2)
                nc.scalar.activation(modrow[:, b, :], ps[:, b, :], ACT.Copy).then_inc(s_modr, 1)
            act.wait_ge(l_w, 64)
            act.wait_ge(s_modc, 2)
            def h_out(b):
                act.wait_ge(s_T, b + 1)
                nc.scalar.activation(hT[:, b, :], ps[:, 6 + b % 2, :], ACT.Identity,
                                     bias=modcol[:, 0, b:b + 1], scale=modcol[:, 1, b:b + 1]).then_inc(s_hT, 1)

            def ct_out(b):
                act.wait_ge(s_CT, b + 1)
                nc.scalar.activation(ct[:, b, :], ps[:, b % 2, :], ACT.Identity, bias=bcol[:, 0:1]).then_inc(s_ct, 1)

            h_out(0)
            for b in range(1, NB):
                h_out(b)
                ct_out(b - 1)
            ct_out(NB - 1)
            with act.Fori(0, NB // 2) as it:
                for u in range(2):
                    b = it * 2 + u
                    act.wait_ge(s_kf, b + 2)
                    act.wait_ge(w_k[u], it * 48 + 16)
                    nc.scalar.activation(kp[:, u, 0, :], kf[:], ACT.Copy).then_inc(s_kh, 1)
                    act.wait_ge(s_kr, b + 1)
                    nc.scalar.activation(kp[:, u, 1, :], kr[:], ACT.Copy).then_inc(s_km, 1)
                    act.wait_ge(s_qc, b + 1)
                    act.wait_ge(s_qf, b + 1)
                    nc.scalar.activation(qu[:], ps[:, 4, :], ACT.Identity, bias=bcol[:, 1:2]).then_inc(s_u, 1)
                    act.wait_ge(s_qf, b + 2)
                    act.wait_ge(w_q[u], it * 48 + 16)
                    nc.scalar.activation(qp[:, u, 0, :], qf[:], ACT.Copy).then_inc(s_qh, 1)
                    act.wait_ge(s_qr, b + 1)
                    nc.scalar.activation(qp[:, u, 1, :], qr[:], ACT.Copy).then_inc(s_qm, 1)

            def max_out(s):
                act.wait_ge(s_mt, s + 1)
                if not (isinstance(s, int) and s == 0):
                    act.wait_ge(s_parts, s)
                nc.scalar.activation(mxn[:], ps[0:16, 7, 0:128], ACT.Copy).then_inc(s_mn, 1)

            def out_copy(s):
                act.wait_ge(s_pv, s + 1)
                if not (isinstance(s, int) and s == 0):
                    act.wait_ge(s_ot, s)
                nc.scalar.activation(osb[:], ps[:, 6, :], ACT.Copy).then_inc(s_oe, 1)

            def step(s, u, prev=True, more_max=True):
                for n in range(16):
                    if n == 1 and prev:
                        out_copy(s - 2)
                    if n == 4 and more_max:
                        max_out(s + 1)
                    i, kc, half = n // 8, (n // 2) % 4, n % 2
                    if n == 0 and not (isinstance(s, int) and s < 2):
                        act.wait_ge(s_pv, s - 1)
                    act.wait_ge(s_sc, 16 * s + n + 1)
                    nc.scalar.activation(PT[:, u, 2 * i + half, kc, :], ps[:, 4 + half, :], ACT.Exp,
                                         scale=SCALE).then_inc(s_ex, 1)

            max_out(0)
            max_out(1)
            step(0, 0, prev=False, more_max=False)
            step(1, 1, prev=False)
            with act.Fori(1, NS // 2 - 1) as it:
                step(it * 2, 0)
                step(it * 2 + 1, 1)
            step(14, 0)
            step(15, 1, more_max=False)
            out_copy(14)
            out_copy(15)

            def a_out(b):
                act.wait_ge(s_aT, b + 1)
                if b >= 2:
                    act.wait_ge(s_y, b - 1)
                nc.scalar.activation(aT[:, b % 2, :], ps[:, b % 2, :], ACT.Copy).then_inc(s_aTe, 1)

            def h2_out(b):
                act.wait_ge(s_h2t, b + 1)
                if b >= 2:
                    act.wait_ge(s_gl, b - 1)
                nc.scalar.activation(h2T[:, b % 2, :], ps[:, 4 + b % 2, :], ACT.Copy).then_inc(s_h2e, 1)

            def logits_out(b):
                act.wait_ge(s_gl, b + 1)
                nc.scalar.activation(lgs[0:NE, b * L:(b + 1) * L], ps[0:NE, 6, :], ACT.Copy).then_inc(s_lge, 1)

            for b in range(NB):
                a_out(b)
            h2_out(0)
            for b in range(1, NB):
                h2_out(b)
                logits_out(b - 1)
            logits_out(NB - 1)
            nc.scalar.activation(ge[:], ps[:, 7, 0:NB * TC * NE], ACT.Exp, scale=-1.0).then_inc(s_ge, 1)

            act.wait_ge(l_lg, 16)
            nc.scalar.activation(sv, lg, ACT.Exp, scale=-1.0).then_inc(s_sig, 1)
            act.wait_ge(s_slot, 2)
            nc.scalar.activation(slots[0:16, :], ps[0:16, 1, 0:NE * 32], ACT.Copy).then_inc(s_slot, 1)
            act.wait_ge(l_top, 16 * 8)

            def gelu(e, u):
                if not (isinstance(e, int) and e < 2):
                    act.wait_ge(s_dn, e - 1)
                for f in range(FC):
                    act.wait_ge(s_up, e * FC + f + 1)
                    bias = b1c[:, e, f:f + 1] if isinstance(e, int) else b1c[:, ds(e, 1), f]
                    nc.scalar.activation(hid[:, u, f, :], ps[:, 1 + f, :], ACT.Gelu, bias=bias).then_inc(s_gelu, 1)

            gelu(0, 0)
            gelu(1, 1)
            with act.Fori(1, NE // 2) as it:
                gelu(it * 2, 0)
                gelu(it * 2 + 1, 1)

        @block.vector
        def _(dve):
            dve.wait_ge(s_silu, 1)
            nc.vector.tensor_scalar_add(se[:, 1, :], se[:, 0, :], 1.0).then_inc(s_silu, 1)
            dve.wait_ge(s_silu, 2)
            nc.vector.reciprocal(se[:, 2, :], se[:, 1, :]).then_inc(s_silu, 1)
            dve.wait_ge(s_silu, 3)
            nc.vector.tensor_tensor(se[:, 3, :], se[:, 2, :], cT[:], ALU.mult).then_inc(s_silu, 1)
            for b in range(NB):
                dve.wait_ge(l_x[b], 16)
                for n in range(b * TC, (b + 1) * TC):
                    ins = nc.vector.bn_stats(stat[:, n, :], X[:, n, :])
            ins.then_inc(s_stat, 1)
            dve.wait_ge(s_stat, 1)
            for n in range(NB * TC):
                ins = nc.vector.bn_aggr(mv[:, n, :], stat[:, n, :])
            ins.then_inc(s_stat, 1)
            dve.wait_ge(s_stat, 2)
            nc.vector.tensor_scalar_add(var[:], mv[:, :, 1], EPS).then_inc(s_ln, 1)
            dve.wait_ge(s_mod, 1)
            nc.vector.tensor_copy(modcol[:, 0, :], ps[:, 4, 0:NB]).then_inc(s_modc, 1)
            nc.vector.tensor_scalar_add(modcol[:, 1, :], ps[:, 4, NB:2 * NB], 1.0).then_inc(s_modc, 1)

            dve.wait_ge(s_rstd, 1)
            for b in range(NB):
                for n in range(b * TC, (b + 1) * TC):
                    ins = nc.vector.tensor_scalar(xn[:, n, :], X[:, n, :], mv[:, n, 0:1], rstd[:, n:n + 1],
                                                  ALU.subtract, ALU.mult)
                ins.then_inc(s_xn, 1)
            dve.wait_ge(l_tab, 96)
            for b in range(NB):
                dve.wait_ge(s_V, b + 1)
                nc.vector.tensor_tensor(
                    Vall[:, b], ps[:, 4 + b % 2, :].rearrange("p (c g d) -> p g c d", c=TC, g=4),
                    bv_row[:].rearrange("p (g d) -> p g d", g=4).unsqueeze(2).to_broadcast([128, 4, TC, 32]),
                    ALU.add).then_inc(s_vd, 1)
            dve.wait_ge(l_w, 64)
            with dve.Fori(0, NB // 2) as it:
                for u in range(2):
                    b = it * 2 + u
                    dve.wait_ge(s_kAB, b + 1)
                    nc.vector.scalar_tensor_tensor(out=kcs[:], in0=ps[:, 2, :], scalar=bcol[:, 5:6], in1=cos_t[:],
                                                   op0=ALU.add, op1=ALU.mult)
                    nc.vector.scalar_tensor_tensor(out=kss[:], in0=ps[:, 3, :], scalar=bcol[:, 6:7], in1=sin_t[:],
                                                   op0=ALU.add, op1=ALU.mult).then_inc(s_kt, 1)
                    dve.wait_ge(s_kt, b + 2)
                    nc.vector.tensor_tensor(kad[:], kcs[:], kss[:], ALU.add).then_inc(s_kad, 1)
                    dve.wait_ge(s_kad, b + 1)
                    dve.wait_ge(s_kc, b + 1)
                    nc.vector.scalar_tensor_tensor(out=kf[:], in0=ps[:, 5, :], scalar=bcol[:, 4:5], in1=kad[:],
                                                   op0=ALU.add, op1=ALU.add).then_inc(s_kf, 1)
                    dve.wait_ge(s_qAB, b + 1)
                    dve.wait_ge(s_qad, b + 1)
                    nc.vector.scalar_tensor_tensor(out=qcs[:], in0=ps[:, 6, :], scalar=bcol[:, 2:3], in1=cos_t[:],
                                                   op0=ALU.add, op1=ALU.mult)
                    nc.vector.scalar_tensor_tensor(out=qss[:], in0=ps[:, 7, :], scalar=bcol[:, 3:4], in1=sin_t[:],
                                                   op0=ALU.add, op1=ALU.mult).then_inc(s_qt, 1)
                    dve.wait_ge(s_kh, b + 1)
                    nc.vector.tensor_tensor(kr[:], kf[:], kp[:, u, 0, :], ALU.subtract).then_inc(s_kr, 1)
                    dve.wait_ge(s_km, b + 1)
                    nc.vector.tensor_tensor(kp[:, u, 2, :], kr[:], kp[:, u, 1, :], ALU.subtract).then_inc(s_kl, 1)

            def normed(s):
                dve.wait_ge(s_ot, s + 1)
                o = ps[:, 7, :].rearrange("p (a d) -> p a d", d=32)
                nc.vector.reciprocal(rs[:].unsqueeze(2), o[:, :, HD:HD + 1]).then_inc(s_rs, 1)
                dve.wait_ge(s_rs, s + 1)
                dst = (An[:, s // 4, :, s % 4, :] if isinstance(s, int) else
                       An[:, ds(s // 4, 1), :, ds(s % 4, 1), :].rearrange("p a q g c -> p (a q g) c"))
                nc.vector.tensor_tensor(
                    dst.rearrange("p q (j d) -> p q j d", d=HD),
                    o.rearrange("p (q j) d -> p q j d", j=4)[:, :, :, 0:HD],
                    rs[:].rearrange("p (q j) -> p q j", j=4).unsqueeze(3).to_broadcast([128, TC, 4, HD]),
                    ALU.mult).then_inc(s_no, 1)

            def maxima(s, u, n):
                if n == 0 and not (isinstance(s, int) and s < 2):
                    dve.wait_ge(s_mt, s - 1)
                dve.wait_ge(s_mx, 8 * s + n + 1)
                nc.vector.tensor_reduce(mx[:, u, :].rearrange("p (h a) -> p h a", h=2)[:, :, n],
                                        ps[:, 2 * (n % 2):2 * (n % 2) + 2, :], AX.X, ALU.max,
                                        negate=True).then_inc(s_mxd, 1)

            def step(s, u, prev=True, more_max=True):
                for n in range(8):
                    if more_max:
                        maxima(s + 2, u, n)
                    if n == 5 and prev:
                        normed(s - 2)

            for n in range(8):
                maxima(0, 0, n)
            for n in range(8):
                maxima(1, 1, n)
            step(0, 0, prev=False)
            step(1, 1, prev=False)
            with dve.Fori(1, NS // 2 - 1) as it:
                step(it * 2, 0)
                step(it * 2 + 1, 1)
            step(14, 0, more_max=False)
            step(15, 1, more_max=False)
            normed(14)
            normed(15)

            def residual(b):
                t4 = range(b * TC, (b + 1) * TC)
                rows = slice(b * TC, (b + 1) * TC)
                dve.wait_ge(s_y, b + 1)
                nc.vector.tensor_tensor(x2[:, rows], ps[:, 2 + b % 2, :].rearrange("p (c d) -> p c d", c=TC),
                                        X[:, rows, :], ALU.add).then_inc(s_x2, 1)
                dve.wait_ge(s_x2, b + 1)
                for n in t4:
                    ins = nc.vector.bn_stats(stat2[:, n, :], x2[:, n, :])
                ins.then_inc(s_st2, 1)
                dve.wait_ge(s_st2, b * 2 + 1)
                for n in t4:
                    ins = nc.vector.bn_aggr(mv2[:, n, :], stat2[:, n, :])
                ins.then_inc(s_st2, 1)
                dve.wait_ge(s_st2, b * 2 + 2)
                nc.vector.tensor_scalar_add(var2[:, rows], mv2[:, rows, 1], EPS).then_inc(s_v2, 1)

            def normed_2(b):
                dve.wait_ge(s_r2, b + 1)
                if b >= 2:
                    dve.wait_ge(s_h2, b - 1)
                for c in range(TC):
                    n = b * TC + c
                    ins = nc.vector.tensor_scalar(xn2[:, b % 2, c, :], x2[:, n, :], mv2[:, n, 0:1], rstd2[:, n:n + 1],
                                                  ALU.subtract, ALU.mult)
                ins.then_inc(s_xn2, 1)
                dve.wait_ge(s_xn2, b + 1)
                nc.vector.tensor_tensor(xn2[:, b % 2], xn2[:, b % 2],
                                        modrow[:, b:b + 1, M_CB * D:(M_CB + 1) * D].to_broadcast([128, TC, D]),
                                        ALU.mult).then_inc(s_xm2, 1)

            dve.wait_ge(s_prep, 10)
            dve.wait_ge(s_gate, 1)
            residual(0)
            for b in range(1, NB):
                residual(b)
                normed_2(b - 1)
            normed_2(NB - 1)
            dve.wait_ge(s_ge, 1)
            nc.vector.tensor_scalar_add(ge[:], ge[:], 1.0).then_inc(s_g1, 1)
            dve.wait_ge(s_g1, 1)
            nc.vector.reciprocal(rw[:, :, D:D + NE], ge[:].rearrange("p (n e) -> p n e", e=NE)).then_inc(s_g, 1)

            dve.wait_ge(s_sig, 1)
            nc.vector.tensor_scalar_add(junk, sv, 1.0).then_inc(s_sig, 1)
            dve.wait_ge(l_top, 16 * 8)
            dve.wait_ge(s_sig, 2)
            nc.vector.reciprocal(sv, junk)
            nc.vector.memset(base, 0)
            nc.vector.tensor_copy(cand3, cand_t[:, 0, :]).then_inc(s_sig, 1)
            dve.wait_ge(s_sig, 3)
            with dve.Fori(0, ROUNDS // 3) as it:
                for v in range(3):
                    k = it * 3 + v
                    for j in range(3):
                        ins = nc.vector.tensor_scalar(ge3[:, j, :], sv, cand3[:, j:j + 1].bitcast(fp32), None, ALU.is_ge,
                                                      ALU.add, accum_out=cnt3[:, j:j + 1])
                    ins.then_inc(s_cnt, 1)
                    dve.wait_ge(s_tot, k + 1)
                    nc.vector.tensor_scalar(reach3, ps[:, 0, 0:3], float(TOP), None, ALU.is_ge, ALU.add,
                                            accum_out=reached).then_inc(s_cand, 1)
                    dve.wait_ge(s_cand, k * 3 + 1)
                    nc.vector.tensor_scalar(found, reached, scale_t[:, ds(k, 1)], None, ALU.mult).then_inc(s_cand, 1)
                    dve.wait_ge(s_cand, k * 3 + 2)
                    nc.vector.scalar_tensor_tensor(
                        out=cand3, in0=cand_t[:, ds(k + 1, 1), :].rearrange("p o j -> p (o j)"), scalar=base,
                        in1=found.to_broadcast([128, 3]), op0=ALU.bitwise_xor, op1=ALU.bitwise_xor)
                    nc.vector.tensor_tensor(base, base, found, ALU.bitwise_xor).then_inc(s_cand, 1)
                    dve.wait_ge(s_cand, k * 3 + 3)

            step_ = [0]

            def link(ins):
                step_[0] += 1
                ins.then_inc(s_tk, 1)
                dve.wait_ge(s_tk, step_[0])

            link(nc.vector.tensor_scalar(gt, sv, base.bitcast(fp32), None, ALU.is_gt, ALU.add, accum_out=cnt_gt))
            link(nc.vector.tensor_scalar(eq, sv, base.bitcast(fp32), None, ALU.is_equal))
            dve.wait_ge(s_ones, 1)
            nc.vector.tensor_tensor_scan(ep, ones[:], eq, 0.0, ALU.mult, ALU.add).then_inc(s_sel, 1)
            dve.wait_ge(s_selp, 1)
            link(nc.vector.tensor_scalar(lim1, ps[:, 0, 0:1], -1.0, float(TOP), ALU.mult, ALU.add))
            link(nc.vector.tensor_tensor(lim, lim1, ps[:, 0, 1:2], ALU.subtract))
            link(nc.vector.scalar_tensor_tensor(out=junk, in0=ep, scalar=lim, in1=eq, op0=ALU.is_le, op1=ALU.mult))
            link(nc.vector.tensor_tensor(sel, junk, gt, ALU.add))
            nc.vector.tensor_tensor_scan(pp, ones[:], sel, 0.0, ALU.mult, ALU.add).then_inc(s_sel, 1)
            dve.wait_ge(s_selp, 2)
            nc.vector.scalar_tensor_tensor(out=junk, in0=pp, scalar=ps[:, 0, 2:3], in1=sel, op0=ALU.add,
                                           op1=ALU.mult).then_inc(s_sel, 1)
            dve.wait_ge(s_selp, 3)
            link(nc.vector.tensor_scalar(posi, ps[:, 1, 0:128], -1.0, None, ALU.add))
            link(nc.vector.tensor_scalar(posa, posi, 5, None, ALU.arith_shift_right))
            link(nc.vector.tensor_scalar(posb, posi, 31, None, ALU.bitwise_and))
            link(nc.vector.tensor_tensor(one_a, posa.unsqueeze(2).to_broadcast([128, 128, 16]),
                                         iota32[:, 0:16].unsqueeze(1).to_broadcast([128, 128, 16]), ALU.is_equal))
            link(nc.vector.tensor_tensor(one_a.rearrange("p (e s) a -> p e s a", e=NE),
                                         one_a.rearrange("p (e s) a -> p e s a", e=NE),
                                         tok16[:].unsqueeze(1).unsqueeze(3).to_broadcast([128, NE, NSEG, 16]),
                                         ALU.mult))
            nc.vector.tensor_tensor(one_b, posb.unsqueeze(2).to_broadcast([128, 128, 32]),
                                    iota32[:].unsqueeze(1).to_broadcast([128, 128, 32]),
                                    ALU.is_equal).then_inc(s_slot, 1)
            dve.wait_ge(s_slot, 4)
            for w in range(4):
                nc.vector.tensor_copy(idx[32 * w:32 * w + 32, :, :],
                                      ps[0:32, 2, 0:128].rearrange("p (e c w) -> p e c w", e=NE, w=4)[:, :, :, w]
                                      ).then_inc(s_idx, 1)

            def rows_up(e, u):
                dve.wait_ge(s_gt, e + 1)
                nc.vector.tensor_copy(exT[:, u, :], ps[:, 0, :]).then_inc(s_gx, 1)

            def factors(e, u):
                if not (isinstance(e, int) and e < 2):
                    dve.wait_ge(s_yo, e - 1)
                g = ex[:, u, :, D + e:D + e + 1] if isinstance(e, int) else ex[:, u, :, ds(e + D, 1)]
                nc.vector.tensor_tensor(gg[:, u], ex[:, u, :, D + NE:HW], g.to_broadcast([128, SC, D]),
                                        ALU.mult).then_inc(s_gg, 1)

            def gated(e, u):
                dve.wait_ge(s_dn, e + 1)
                b2v = b2r[:, e:e + 1, :] if isinstance(e, int) else b2r[:, ds(e, 1), :]
                nc.vector.tensor_tensor(yb[:, u], ps[:, 5 + u, :].rearrange("p (c d) -> p c d", c=SC),
                                        b2v.to_broadcast([128, SC, D]), ALU.add).then_inc(s_yb, 1)
                dve.wait_ge(s_yb, e + 1)
                dve.wait_ge(s_gg, e + 1)
                if not (isinstance(e, int) and e < 2):
                    dve.wait_ge(w_sc[u], (e // 2) * 64)
                nc.vector.tensor_tensor(ys[:, u], yb[:, u], gg[:, u], ALU.mult).then_inc(s_yo, 1)

            rows_up(0, 0)
            factors(0, 0)
            rows_up(1, 1)
            factors(1, 1)
            with dve.Fori(0, NE // 2 - 1) as it:
                for u in range(2):
                    rows_up(it * 2 + 2 + u, u)
                    gated(it * 2 + u, u)
                    factors(it * 2 + 2 + u, u)
            gated(NE - 2, 0)
            gated(NE - 1, 1)

        @block.tensor
        def _(pe):
            mm = nc.tensor.matmul
            pe.wait_ge(s_silu, 4)
            for j in range(2):
                ins = mm(ps[:, 4, j * NB:(j + 1) * NB], wmod[:, j * D:(j + 1) * D], se[:, 3, :], start=True, stop=True)
            ins.then_inc(s_mod, 1)
            for b in range(NB):
                mm(ps[:, b, :], se[:, 3, b:b + 1].to_broadcast([D, 128]), wmod[:, 2 * D:6 * D],
                   start=True, stop=True).then_inc(s_mod, 1)

            pe.wait_ge(l_w, 64)
            pe.wait_ge(s_modr, NB)
            pe.wait_ge(s_modc, 2)
            for n in range(NB + 2):
                if n < NB:
                    b = n
                    pe.wait_ge(s_xn, b + 1)
                    if b >= 2:
                        pe.wait_ge(s_hT, b - 1)
                    for c in range(TC):
                        ins = nc.tensor.transpose(ps[:, 6 + b % 2, c * 128:(c + 1) * 128], xn[:, b * TC + c, :],
                                                  ident[:])
                    ins.then_inc(s_T, 1)
                if 1 <= n <= NB:
                    b = n - 1
                    pe.wait_ge(s_hT, b + 1)
                    if b >= 2:
                        pe.wait_ge(s_ct, b - 1)
                    mm(ps[:, b % 2, :], w_x[:, 0:D], hT[:, b, :], start=True, stop=True).then_inc(s_CT, 1)
                if n >= 2:
                    b = n - 2
                    pe.wait_ge(s_ct, b + 1)
                    if b >= 2:
                        pe.wait_ge(s_vd, b - 1)
                    for c in range(TC):
                        ins = mm(ps[:, 4 + b % 2, c * 128:(c + 1) * 128], ct[64:128, b, c * 128:(c + 1) * 128],
                                 w_ct[64:128, 4 * D:5 * D], start=True, stop=True)
                    ins.then_inc(s_V, 1)
            with pe.Fori(0, NB) as b:
                h_b = hT[:, ds(b, 1), :].rearrange("p o t -> p (o t)")
                c_b = ct[:, ds(b, 1), :].rearrange("p o t -> p (o t)")
                pe.wait_ge(s_kt, b + 1)
                mm(ps[:, 2, :], w_x[:, D:2 * D], h_b, start=True, stop=True)
                mm(ps[:, 3, :], w_x[:, 2 * D:3 * D], h_b, start=True, stop=True).then_inc(s_kAB, 1)
                pe.wait_ge(s_vd, NB)
                pe.wait_ge(s_kf, b + 1)
                mm(ps[:, 5, :], w_ct[:, 3 * D:4 * D], c_b, start=True, stop=True).then_inc(s_kc, 1)
                pe.wait_ge(s_qt, b + 1)
                mm(ps[:, 6, :], w_ct[:, D:2 * D], c_b, start=True, stop=True)
                mm(ps[:, 7, :], w_ct[:, 2 * D:3 * D], c_b, start=True, stop=True).then_inc(s_qAB, 1)
                pe.wait_ge(s_u, b + 1)
                mm(ps[:, 4, :], w_ct[:, 0:D], c_b, start=True, stop=True).then_inc(s_qc, 1)

            def max_unit(s, u, n):
                i, qc = n // 4, n % 4
                if n == 0:
                    pe.wait_ge(l_m[u], (s // 2 + 1) * 64)
                if not (isinstance(s, int) and 8 * s + n < 2):
                    pe.wait_ge(s_mxd, 8 * s + n - 1)
                for half in range(2):
                    ins = mm(ps[:, 2 * (n % 2) + half, :], MQ[:, u, i, qc * 128:(qc + 1) * 128], MK[:, u, half, i, :],
                             start=True, stop=True)
                ins.then_inc(s_mx, 1)

            def max_turn(s, u):
                pe.wait_ge(s_mxd, 8 * s + 8)
                if not (isinstance(s, int) and s < 4):
                    pe.wait_ge(s_no, s - 3)
                if not (isinstance(s, int) and s == 0):
                    pe.wait_ge(s_mn, s)
                nc.tensor.transpose(ps[0:16, 7, 0:128], mx[:, u, :], ident[:]).then_inc(s_mt, 1)

            def exp_unit(s, u, n):
                i, kc, half = n // 8, (n // 2) % 4, n % 2
                if n == 0:
                    pe.wait_ge(l_e[u], (s // 2 + 1) * 160)
                if not (isinstance(s, int) and 16 * s + n < 2):
                    pe.wait_ge(s_ex, 16 * s + n - 1)
                mm(ps[:, 4 + half, :], EK[:, u, i, kc * 128:(kc + 1) * 128], EQ[:, u, half, i, :],
                   start=True, stop=True).then_inc(s_sc, 1)

            def weigh(s, u, m):
                kc, q = m % TC, slice(256 * (m // TC), 256 * (m // TC) + 256)
                if m == 0:
                    pe.wait_ge(s_ex, 16 * s + 16)
                    pe.wait_ge(s_va, s + 1)
                    if not (isinstance(s, int) and s == 0):
                        pe.wait_ge(s_oe, s)
                for j in range(4):
                    ins = mm(ps[32 * j:32 * j + 32, 6, q], VA[:, u, kc, j, :], PT[:, u, j, kc, q],
                             start=kc == 0, stop=kc == TC - 1)
                if m == 7:
                    ins.then_inc(s_pv, 1)

            def out_turn(s):
                pe.wait_ge(s_oe, s + 1)
                pe.wait_ge(s_mn, s + 4 if not isinstance(s, int) else min(s + 4, NS))
                if not (isinstance(s, int) and s == 0):
                    pe.wait_ge(s_no, s)
                for c in range(TC):
                    ins = nc.tensor.transpose(ps[:, 7, c * 128:(c + 1) * 128], osb[:, c * 128:(c + 1) * 128], ident[:])
                ins.then_inc(s_ot, 1)

            def step(s, u, prev=True, prev2=True, more_max=True, turn=True):
                for n in range(8):
                    if n == 1 and turn:
                        max_turn(s + 1, 1 - u)
                    if n == 4 and prev2:
                        out_turn(s - 2)
                    if more_max:
                        max_unit(s + 2, u, n)
                    exp_unit(s, u, 2 * n)
                    exp_unit(s, u, 2 * n + 1)
                    if n >= 1 and prev:
                        weigh(s - 1, 1 - u, n - 1)
                if prev:
                    weigh(s - 1, 1 - u, 7)

            pe.wait_ge(s_kt, NB + 1)
            for n in range(8):
                max_unit(0, 0, n)
            for done in (s_kf, s_u, s_qt):
                pe.wait_ge(done, NB + 1)
            max_turn(0, 0)
            for n in range(8):
                max_unit(1, 1, n)
            max_turn(1, 1)
            step(0, 0, prev=False, prev2=False, turn=False)
            step(1, 1, prev2=False)
            with pe.Fori(1, NS // 2 - 1) as it:
                step(it * 2, 0)
                step(it * 2 + 1, 1)
            step(14, 0, more_max=False)
            step(15, 1, more_max=False, turn=False)
            for m in range(8):
                weigh(15, 1, m)
            out_turn(14)
            out_turn(15)

            def turn_a(b):
                pe.wait_ge(s_no, 4 * b + 4)
                if b >= 2:
                    pe.wait_ge(s_aTe, b - 1)
                for c in range(TC):
                    ins = nc.tensor.transpose(ps[:, b % 2, c * 128:(c + 1) * 128],
                                              An[:, b, c].rearrange("p g d -> p (g d)"), ident[:])
                ins.then_inc(s_aT, 1)

            def project(b):
                pe.wait_ge(s_aTe, b + 1)
                if b >= 2:
                    pe.wait_ge(s_x2, b - 1)
                for c in range(TC):
                    ins = mm(ps[:, 2 + b % 2, c * 128:(c + 1) * 128], aT[:, b % 2, c * 128:(c + 1) * 128],
                             wo_g[:, b, :], start=True, stop=True)
                ins.then_inc(s_y, 1)

            def turn_h(b):
                pe.wait_ge(s_h2, b + 1)
                if b >= 2:
                    pe.wait_ge(s_h2e, b - 1)
                for c in range(TC):
                    ins = nc.tensor.transpose(ps[:, 4 + b % 2, c * 128:(c + 1) * 128], rw[:, b * TC + c, 0:D],
                                              ident[:])
                ins.then_inc(s_h2t, 1)

            def route(b):
                pe.wait_ge(s_h2e, b + 1)
                if b >= 1:
                    pe.wait_ge(s_lge, b)
                mm(ps[0:NE, 6, :], wg[:], h2T[:, b % 2, :], start=True, stop=True)
                for c in range(TC):
                    n = b * TC + c
                    ins = mm(ps[:, 7, n * NE:(n + 1) * NE], h2T[:, b % 2, c * 128:(c + 1) * 128], wg[:],
                             start=True, stop=True)
                ins.then_inc(s_gl, 1)

            pe.wait_ge(s_prep, 10)
            turn_a(0)
            for b in range(1, NB):
                turn_a(b)
                project(b - 1)
            project(NB - 1)
            turn_h(0)
            for b in range(1, NB):
                turn_h(b)
                route(b - 1)
            route(NB - 1)

            pe.wait_ge(l_top, 16 * 8)
            with pe.Fori(0, ROUNDS // 3) as it:
                for v in range(3):
                    pe.wait_ge(s_cnt, it * 3 + v + 1)
                    mm(ps[:, 0, 0:3], same_e[:], cnt3, start=True, stop=True).then_inc(s_tot, 1)
            pe.wait_ge(s_sel, 1)
            mm(ps[:, 0, 0:1], same_e[:], cnt_gt, start=True, stop=True)
            mm(ps[:, 0, 1:2], lower[:], ep[:, 127:128], start=True, stop=True).then_inc(s_selp, 1)
            pe.wait_ge(s_sel, 2)
            mm(ps[:, 0, 2:3], lower[:], pp[:, 127:128], start=True, stop=True).then_inc(s_selp, 1)
            pe.wait_ge(s_sel, 3)
            nc.tensor.transpose(ps[:, 1, 0:128], junk, ident[:]).then_inc(s_selp, 1)
            pe.wait_ge(s_slot, 1)
            for e in range(NE):
                for s in range(NSEG):
                    ins = mm(ps[0:16, 1, 32 * e:32 * e + 32], one_a[:, e * NSEG + s, :], one_b[:, e * NSEG + s, :],
                             start=s == 0, stop=s == NSEG - 1)
            ins.then_inc(s_slot, 1)
            pe.wait_ge(s_slot, 3)
            for e in range(NE):
                ins = nc.tensor.transpose(ps[0:32, 2, 16 * e:16 * e + 16], slots[0:16, 32 * e:32 * e + 32],
                                          ident[0:16, 0:16])
            ins.then_inc(s_slot, 1)

            def turn(e, u):
                pe.wait_ge(g_in[u], (e // 2 + 1) * 64)
                if not (isinstance(e, int) and e == 0):
                    pe.wait_ge(s_gx, e)
                for c in range(SC):
                    ins = nc.tensor.transpose(ps[:, 0, c * 128:(c + 1) * 128], ex[:, u, c, 0:D], ident[:])
                ins.then_inc(s_gt, 1)

            def up(e, u):
                pe.wait_ge(s_gx, e + 1)
                pe.wait_ge(l_w12[u], (e // 2 + 1) * 32)
                for f in range(FC):
                    if not (isinstance(e, int) and e == 0):
                        pe.wait_ge(s_gelu, (e - 1) * FC + f + 1)
                    mm(ps[:, 1 + f, :], w1s[:, u, f * 128:(f + 1) * 128], exT[:, u, :],
                       start=True, stop=True).then_inc(s_up, 1)

            def down(e, u):
                pe.wait_ge(s_gelu, e * FC + FC)
                if not (isinstance(e, int) and e < 2):
                    pe.wait_ge(s_yb, e - 1)
                for c in range(SC):
                    for f in range(FC):
                        ins = mm(ps[:, 5 + u, c * 128:(c + 1) * 128], hid[:, u, f, c * 128:(c + 1) * 128],
                                 w2s[:, u, f, :], start=f == 0, stop=f == FC - 1)
                ins.then_inc(s_dn, 1)

            turn(0, 0)
            up(0, 0)
            turn(1, 1)
            up(1, 1)
            turn(2, 0)
            down(0, 0)
            up(2, 0)
            turn(3, 1)
            down(1, 1)
            with pe.Fori(1, NE // 2 - 1) as it:
                up(it * 2 + 1, 1)
                turn(it * 2 + 2, 0)
                down(it * 2, 0)
                up(it * 2 + 2, 0)
                turn(it * 2 + 3, 1)
                down(it * 2 + 1, 1)
            up(NE - 1, 1)
            down(NE - 2, 0)
            down(NE - 1, 1)


def tables():
    ids = np.arange(D // 2, dtype=np.float32)
    theta = (np.float32(10000.0) ** (np.float32(-2.0) * ids) / np.float32(D // 2)).astype(np.float32)
    r = np.arange(L, dtype=np.float32)[None, :] * theta[:, None]
    cos, sin = np.repeat(np.cos(r), 2, 0), np.repeat(np.sin(r), 2, 0)
    sin[0::2] *= -1.0
    return cos.astype(np.float32), sin.astype(np.float32)


def kernel(**inputs):
    import concourse.bacc as bacc
    from concourse.bass_utils import run_bass_kernel_spmd as run

    a = {k.replace("L0_attn_", "").replace("L0_ffn_", "").replace("L0_", ""): np.asarray(v) for k, v in inputs.items()}
    order = np.array([(8 * half + h8) * HD + d for half in range(2) for d in range(HD) for h8 in range(8)])
    swapped = order ^ 1
    vorder = np.array([(8 * half + 2 * g + i) * HD + d
                       for g in range(4) for i in range(2) for half in range(2) for d in range(HD)])
    none = np.zeros((DC, D), np.float32)
    cos, sin = tables()
    part = np.arange(128)
    seg = part // (128 // NE)
    arrays = {
        "x": a["x"],
        "cT": a["c"].T,
        "wmod": a["wmod"],
        "w_x": np.concatenate([a["Wd_q_w"], a["Wd_kv_w"], a["Wk_r_w"][:, order], a["Wk_r_w"][:, swapped]], 1),
        "w_ct": np.concatenate([
            np.concatenate([a["Wu_q_w"][:, order], a["Wq_r_w"][:, order], a["Wq_r_w"][:, swapped], none, none], 1),
            np.concatenate([none, none, none, a["Wu_k_w"][:, order], a["Wu_v_w"][:, vorder]], 1)], 0),
        "bcol": np.stack([np.concatenate([a["Wd_q_b"], a["Wd_kv_b"]]), a["Wu_q_b"][order], a["Wq_r_b"][order],
                          a["Wq_r_b"][swapped], a["Wu_k_b"][order], a["Wk_r_b"][order], a["Wk_r_b"][swapped]], 1),
        "brow": np.stack([a["Wu_v_b"][vorder], a["Wo_b"]]),
        "cos": cos[order], "sin": sin[order],
        "wo": a["Wo_w"][vorder, :],
        "wg": a["Wg"],
        "ident": np.eye(128, dtype=np.float32),
        "w1": a["W1"], "w2": a["W2"], "b2": a["b2"],
        "b1c": a["b1"].reshape(NE, FC, 128).transpose(2, 0, 1),
        "same_e": (seg[:, None] == seg[None, :]).astype(np.float32),
        "lower": ((seg[:, None] == seg[None, :]) & (part[:, None] < part[None, :])).astype(np.float32),
        "scale_t": np.tile(2.0 ** (2 * np.arange(ROUNDS - 1, -1, -1)), (128, 1)).astype(np.float32),
        "cand_t": np.tile(np.append(np.arange(1, 4) * 4 ** np.arange(ROUNDS - 1, -1, -1)[:, None], [[0, 0, 0]], 0),
                          (128, 1, 1)).astype(np.int32),
        "iota32": np.tile(np.arange(32), (128, 1)).astype(np.float32),
        "tok16": (np.arange(128 // NE)[None, :] * 128 + part[:, None]).astype(np.float32),
    }
    arrays = {k: np.ascontiguousarray(v) for k, v in arrays.items()}
    nc = bacc.Bacc("TRN2", target_bir_lowering=False, num_devices=1)
    t = {k: nc.dram_tensor("in_" + k, list(v.shape), mybir.dt.from_np(v.dtype), kind="ExternalInput").ap()
         for k, v in arrays.items()}
    out = nc.dram_tensor("out", [NB, L, D], mybir.dt.float32, kind="ExternalOutput").ap()
    build(nc, t, out)
    r = run(nc, [{"in_" + k: v for k, v in arrays.items()}], core_ids=[0])
    return r.results[0]["out"]
```

```python
import numpy as np
import concourse.bass as bass
from concourse import mybir
from contextlib import ExitStack

NB, L, D = 4, 512, 128
NT = NB * L
NH, HD = 16, 8
DC = 64
TC = L // 128
NS = NB * NH // 4
NE, FF, CAP = 8, 512, 2
TOP = NT * CAP // NE
FC = FF // 128
SC = TOP // 128
SCALE = 1.0 / 12.0
EPS = 1e-5
PART_Q = [0, 0, 0, 1, 1, 2]
PART_K = [1, 0, 2, 0, 1, 0]
PR = 8 * len(PART_Q)
HW = D + NE + D
ROUNDS = 15
EXACT = 10
CHUNKS, SLOT_BANK = ((0, 2), (2, NE)), (2, 6)
M_GA, M_SB, M_CB, M_GB = range(4)


def build(nc, t, out):
    fp32, bf16, fp16, i32 = mybir.dt.float32, mybir.dt.bfloat16, mybir.dt.float16, mybir.dt.int32
    ACT = mybir.ActivationFunctionType
    ALU = mybir.AluOpType
    AX = mybir.AxisListType
    ds = bass.ds

    qs_dram = nc.dram_tensor("q_parts", [NB, len(PART_Q), 2, HD, 8, L], bf16, kind="Internal").ap()
    ks_dram = nc.dram_tensor("k_parts", [NB, len(PART_Q), 2, HD, 8, L], bf16, kind="Internal").ap()
    rows_dram = nc.dram_tensor("rows", [NT, HW], fp32, kind="Internal").ap()

    ctx = ExitStack()
    with ctx:
        def sb(name, shape, dt=fp32):
            return ctx.enter_context(nc.sbuf_tensor(name, shape, dt))

        def sem(name):
            return ctx.enter_context(nc.semaphore(name))

        X = sb("X", [128, NB * TC, D])
        cT = sb("cT", [D, NB])
        wmod = sb("wmod", [D, 6 * D])
        w_x = sb("w_x", [D, 3 * D])
        w_ct = sb("w_ct", [128, 5 * D])
        bcol = sb("bcol", [D, 7])
        bv_row = sb("bv_row", [128, D])
        bo_row = sb("bo_row", [128, D])
        cos_t = sb("cos_t", [D, L])
        sin_t = sb("sin_t", [D, L])
        wo = sb("wo", [D, D])
        wg = sb("wg", [D, NE])
        wg_wide = sb("wg_wide", [D, 15 + 128])
        ident = sb("ident", [128, 128])

        se = sb("se", [D, 4, NB])
        modcol = sb("modcol", [D, 4, NB])
        modrow = sb("modrow", [128, NB, 4 * D])
        wo_g = sb("wo_g", [D, NB, D])
        bo_g = sb("bo_g", [128, NB, D])

        stat = sb("stat", [128, NB * TC, 6])
        mv = sb("mv", [128, NB * TC, 2])
        var = sb("var", [128, NB * TC])
        rstd = sb("rstd", [128, NB * TC])
        mhalf = sb("mhalf", [128, NB * TC])
        Vall = sb("Vall", [128, NB, 4, TC, 32])

        MQ, EK = (sb(n, [128, 2, 2, L], bf16) for n in ("MQ", "EK"))
        MK, EQ = (sb(n, [128, 2, 2, 2, L], bf16) for n in ("MK", "EQ"))
        mx = sb("mx", [128, 2, 16])
        mxn, mxr = (sb(n, [16, 128]) for n in ("mxn", "mxr"))
        mxp = sb("mxp", [16, 2, 3, 128], bf16)
        big = sb("big", [128, 2 * 4 * TC * L])
        PT = big[:, :].rearrange("p (u j c q) -> p u j c q", u=2, j=4, c=TC)
        VA = sb("VA", [128, 2, TC, 4, 32])
        osb = sb("osb", [128, L])
        rs = sb("rs", [128, 16])
        An = sb("An", [128, NB, TC, 4, 32])

        def carve():
            at = [0]

            def view(*shape, dt=fp32):
                n = int(np.prod(shape)) * (4 if dt in (fp32, i32) else 2) // 4
                v = big[:, at[0]:at[0] + n]
                at[0] += n
                assert at[0] <= 2 * 4 * TC * L
                v = v if dt == fp32 else v.bitcast(dt)
                names = "abcd"[:len(shape)]
                return v.rearrange(f"p ({' '.join(names)}) -> p {' '.join(names)}", **dict(zip(names, shape)))
            return view

        view = carve()
        xn = view(NB * TC, D)
        hT, ct = view(NB, L), view(NB, L)
        kcs, kss, kad, kf, kr = (view(L) for _ in range(5))
        qcs, qss, qad, qu, qf, qr = (view(L) for _ in range(6))
        kp, qp = view(2, 3, L, dt=bf16), view(2, 3, L, dt=bf16)
        def flat(buf, letters):
            axes = " ".join(letters)
            return buf[:].rearrange(f"p {axes} -> p ({axes})")

        x2 = X
        aT = flat(MQ, "abt").bitcast(fp32).rearrange("p (u t) -> p u t", t=L)
        mk_place = flat(MK, "abct").bitcast(fp32)
        xn2 = mk_place[:, 0:2 * L].rearrange("p (u c d) -> p u c d", u=2, c=TC)
        h2T = mk_place[:, 2 * L:4 * L].rearrange("p (u t) -> p u t", t=L)
        rw = sb("rw", [128, NB * TC, D + NE])
        rw_place = flat(rw, "ab")
        sgn, mag = (rw_place[:, i * 2 * NB * D:(i + 1) * 2 * NB * D].rearrange("p (b j d) -> p b j d", b=NB, j=2)
                    for i in range(2))
        ge = sb("ge", [128, NB * TC * NE])
        stat2, mv2 = sb("stat2", [128, NB * TC, 6]), sb("mv2", [128, NB * TC, 2])
        var2, rstd2 = sb("var2", [128, NB * TC]), sb("rstd2", [128, NB * TC])

        view = carve()
        NSEG = 128 // NE
        NSEG_ACT = 13
        sv, junk, gt, eq, ep, sel, pp = (view(128) for _ in range(7))
        cnt3, cnt_gt = (view(4, dt=fp16)[:, 0:w] for w in (3, 1))
        reach3, ge3 = view(3), view(3, 128)
        reached, lim, lim1 = (view(1) for _ in range(3))
        cand, next4, found = view(2, 4, dt=i32), view(4), view(1, dt=i32)
        posi, posa, posb = (view(128, dt=i32) for _ in range(3))
        posa_h, posb_h = view(128, dt=fp16), view(128, dt=fp16)
        one_a, one_b = view(128, 16, dt=fp16), view(128, 32, dt=fp16)
        slots = view(NE * 32)
        assert NSEG * 128 == NT
        ex = sb("ex", [128, 2, SC, HW])
        w1s, w2s = sb("w1s", [D, 2, FF]), sb("w2s", [128, 2, FC, D])
        view = carve()
        exT, hid, yb, gg, ys = view(2, TOP), view(2, FC, TOP), view(2, SC, D), view(2, SC, D), view(2, SC, D)
        idx = sb("idx", [128, NE, SC], i32)
        b1c, b2r = sb("b1c", [128, NE, FC]), sb("b2r", [128, NE, D])
        same_e, lower = sb("same_e", [128, 128], fp16), sb("lower", [128, 128])
        scale_t, cand_t = sb("scale_t", [128, ROUNDS]), sb("cand_t", [128, ROUNDS + 1, 4], i32)
        iota32, tok16 = sb("iota32", [128, 32], fp16), sb("tok16", [128, NSEG], fp16)
        tok32, warm = sb("tok32", [128, NSEG]), sb("warm", [128, 1])
        ones = sb("ones", [128, 128])

        ps = ctx.enter_context(nc.psum_tensor("ps", [128, 8, 512], fp32))

        l_x = [sem(f"l_x{b}") for b in range(NB)]
        l_id, l_w, l_tab, l_c = sem("l_id"), sem("l_w"), sem("l_tab"), sem("l_c")
        s_silu, s_mod, s_modc, s_modr = sem("s_silu"), sem("s_mod"), sem("s_modc"), sem("s_modr")
        s_stat, s_ln = sem("s_stat"), sem("s_ln")
        s_const = sem("s_const")
        s_rstd, s_xn = sem("s_rstd"), sem("s_xn")
        s_T, s_hT, s_CT, s_ct, s_V, s_vd = (sem(n) for n in ("s_T", "s_hT", "s_CT", "s_ct", "s_V", "s_vd"))
        s_held = sem("s_held")
        s_kt, s_qt, s_kf, s_u, s_qad, s_qf = (sem(n) for n in ("s_kt", "s_qt", "s_kf", "s_u", "s_qad", "s_qf"))
        s_kAB, s_qAB, s_qc, s_kc = (sem(n) for n in ("s_kAB", "s_qAB", "s_qc", "s_kc"))
        s_kad, s_kh, s_kr, s_km, s_kl = (sem(n) for n in ("s_kad", "s_kh", "s_kr", "s_km", "s_kl"))
        s_qh, s_qr, s_qm, s_ql = (sem(n) for n in ("s_qh", "s_qr", "s_qm", "s_ql"))
        w_k = [sem(f"w_k{u}") for u in range(2)]
        w_q = [sem(f"w_q{u}") for u in range(2)]

        s_one = sem("s_one")
        s_gate = sem("s_gate")
        l_m = [sem(f"l_m{u}") for u in range(2)]
        l_e = [sem(f"l_e{u}") for u in range(2)]
        s_mx, s_mxd, s_mt, s_mn, s_pp, s_parts = (
            sem(n) for n in ("s_mx", "s_mxd", "s_mt", "s_mn", "s_pp", "s_parts"))
        s_sc, s_ex, s_va, s_pv, s_oe, s_ot, s_rs, s_no = (
            sem(n) for n in ("s_sc", "s_ex", "s_va", "s_pv", "s_oe", "s_ot", "s_rs", "s_no"))
        s_prep, s_gp, s_xb = sem("s_prep"), sem("s_gp"), sem("s_xb")

        s_aT, s_aTe, s_y, s_x2 = (sem(n) for n in ("s_aT", "s_aTe", "s_y", "s_x2"))
        s_st2, s_v2, s_r2, s_xn2, s_xm2, s_h2 = (
            sem(n) for n in ("s_st2", "s_v2", "s_r2", "s_xn2", "s_xm2", "s_h2"))
        s_h2t, s_h2e, s_lg, s_gl, s_ge, s_g1, s_g = (
            sem(n) for n in ("s_h2t", "s_h2e", "s_lg", "s_gl", "s_ge", "s_g1", "s_g"))
        w_out, w_row = sem("w_out"), sem("w_row")
        w_gb = sem("w_gb")

        l_top = sem("l_top")
        s_cnt, s_tot, s_cand, s_sig, s_sel, s_selp, s_tk = (
            sem(n) for n in ("s_cnt", "s_tot", "s_cand", "s_sig", "s_sel", "s_selp", "s_tk"))
        s_one_a, s_one_t = sem("s_one_a"), sem("s_one_t")
        s_tok = sem("s_tok")
        s_next, s_reach, s_found = sem("s_next"), sem("s_reach"), sem("s_found")
        s_one_ab, s_slot, s_idx, s_ones = sem("s_one_ab"), sem("s_slot"), sem("s_idx"), sem("s_ones")
        l_w1 = [sem(f"l_w1_{u}") for u in range(2)]
        l_w2 = [sem(f"l_w2_{u}") for u in range(2)]
        g_in = [sem(f"g_in{u}") for u in range(2)]
        w_sc = [sem(f"w_sc{u}") for u in range(2)]
        s_gt, s_gx, s_gg, s_up, s_gelu, s_dn, s_yb, s_yo = (
            sem(n) for n in ("s_gt", "s_gx", "s_gg", "s_up", "s_gelu", "s_dn", "s_yb", "s_yo"))

        block = ctx.enter_context(nc.Block())

        @block.sync
        def _(sp):
            sp.dma_start(cT[:], t["cT"]).then_inc(l_c, 16)
            sp.dma_start(wmod[:], t["wmod"]).then_inc(l_c, 16)
            sp.dma_start(ident[:], t["ident"]).then_inc(l_id, 16)
            for b in range(NB):
                sp.dma_start(X[:, b * TC:(b + 1) * TC, :],
                             t["x"][b].rearrange("(c p) d -> p c d", p=128)).then_inc(l_x[b], 16)
                if b < 3:
                    dst, src = ((w_x, "w_x"), (bcol, "bcol"), (w_ct, "w_ct"))[b]
                    sp.dma_start(dst[:], t[src]).then_inc(l_w, 16)
            sp.dma_start(cos_t[:], t["cos"]).then_inc(l_tab, 16)
            sp.dma_start(sin_t[:], t["sin"]).then_inc(l_tab, 16)
            sp.dma_start(bv_row[:], t["brow"][0:1, :].to_broadcast([128, D])).then_inc(l_tab, 16)
            sp.dma_start(bo_row[:], t["brow"][1:2, :].to_broadcast([128, D])).then_inc(l_tab, 16)
            sp.dma_start(wo[:], t["wo"]).then_inc(l_tab, 16)
            sp.dma_start(wg[:], t["wg"]).then_inc(l_tab, 16)
            for dst, src in ((b1c, "b1c"), (same_e, "same_e"), (lower, "lower"), (scale_t, "scale_t"), (cand_t, "cand_t"),
                             (iota32, "iota32"), (tok16, "tok16")):
                sp.dma_start(dst[:], t[src]).then_inc(l_top, 16)
            sp.dma_start(b2r[:], t["b2"].unsqueeze(0).to_broadcast([128, NE, D])).then_inc(l_top, 16)

            def store_parts(b, u):
                for buf, dram, order, done, w in ((kp, ks_dram, PART_K, s_kl, w_k),
                                                  (qp, qs_dram, PART_Q, s_ql, w_q)):
                    sp.wait_ge(done, b + 1)
                    places = dram[b].rearrange("j a d h t -> (a d h) j t")
                    for p in range(3):
                        at = [j for j in range(len(order)) if order[j] == p]
                        step = at[1] - at[0] if len(at) > 1 else 1
                        sp.dma_start(
                            places[:, at[0]:at[-1] + 1:step, :],
                            buf[:, u, p, :].unsqueeze(1).to_broadcast([128, len(at), L])).then_inc(w[u], 16)

            def load_group(s, kbuf, qbuf, slot, done):
                for buf, part in ((kbuf, ks_dram), (qbuf, qs_dram)):
                    for half in range(2):
                        if isinstance(s, int):
                            src = part[s // 4:s // 4 + 1, :, half, :, 2 * (s % 4):2 * (s % 4) + 2, :]
                        else:
                            src = part[ds(s // 4, 1), :, half, :, ds((s % 4) * 2, 2), :]
                        rows = slice(64 * half, 64 * half + PR)
                        sp.dma_start(buf[rows, slot, half] if buf in (MK, EQ) else buf[rows, slot],
                                     src.rearrange("o j d i t -> (o j) d (i t)")).then_inc(done, 16)

            def load_max(s, slot):
                sp.wait_ge(s_parts, s + 1)
                for half in range(2):
                    for p in range(3):
                        r = 64 * half + PR + p
                        sp.dma_start(EQ[r:r + 1, slot, half].rearrange("p i q -> p (i q)"),
                                     mxp[8 * half:8 * half + 8, slot, p, :]).then_inc(l_e[slot], 16)

            def step(s, u, more_max=True, more=True):
                if more_max:
                    sp.wait_ge(s_mx, 8 * (s + 2))
                    load_group(s + 3, MK, MQ, 1 - u, l_m[1 - u])
                if more:
                    if not (isinstance(s, int) and s == 0):
                        sp.wait_ge(s_sc, 16 * s)
                    load_group(s + 1, EK, EQ, 1 - u, l_e[1 - u])
                    load_max(s + 1, 1 - u)

            store_parts(0, 0)
            sp.wait_ge(s_one, 4)
            sp.wait_ge(w_k[0], 16 + 48)
            sp.wait_ge(w_q[0], 16 + 48)
            load_group(0, MK, MQ, 0, l_m[0])
            store_parts(1, 1)
            load_group(1, MK, MQ, 1, l_m[1])
            load_group(0, EK, EQ, 0, l_e[0])
            store_parts(2, 0)
            store_parts(3, 1)
            sp.wait_ge(s_mx, 8)
            load_group(2, MK, MQ, 0, l_m[0])
            load_max(0, 0)
            for u in range(2):
                sp.wait_ge(w_k[u], 16 + 96)
                sp.wait_ge(w_q[u], 16 + 96)
            step(0, 0)
            step(1, 1)
            with sp.Fori(1, NS // 2 - 2) as it:
                step(it * 2, 0)
                step(it * 2 + 1, 1)
            step(12, 0)
            step(13, 1, more_max=False)
            step(14, 0, more_max=False)

            sp.wait_ge(s_gate, 2)
            for b in range(NB):
                sp.dma_start(
                    rows_dram[b * L:(b + 1) * L, D + NE:HW].rearrange("(c p) d -> p c d", p=128),
                    modrow[:, b:b + 1, M_GB * D:(M_GB + 1) * D].to_broadcast([128, TC, D])).then_inc(w_gb, 16)

            for b in range(NB):
                sp.wait_ge(s_x2, b + 1)
                sp.dma_start(out[b].rearrange("(c p) d -> p c d", p=128),
                             x2[:, b * TC:(b + 1) * TC, :]).then_inc(w_out, 16)
            sp.wait_ge(s_g, NB)
            sp.wait_ge(s_h2, NB)
            sp.dma_start(rows_dram[:, 0:D + NE].rearrange("(n p) d -> p n d", p=128), rw[:]).then_inc(w_row, 16)

            def load_expert(e, u):
                if isinstance(e, int):
                    a, b = t["w1"][e], t["w2"][e]
                else:
                    a = t["w1"][ds(e, 1)].rearrange("o h f -> (o h) f")
                    b = t["w2"][ds(e, 1)].rearrange("o f h -> (o f) h")
                    sp.wait_ge(s_up, (e - 1) * FC)
                sp.dma_start(w1s[:, u, :], a).then_inc(l_w1[u], 16)
                if not isinstance(e, int):
                    sp.wait_ge(s_dn, (e - 1) * 2)
                sp.dma_start(w2s[:, u, :, :], b.rearrange("(c p) h -> p c h", p=128)).then_inc(l_w2[u], 16)

            load_expert(0, 0)
            load_expert(1, 1)
            with sp.Fori(1, NE // 2) as it:
                for u in range(2):
                    load_expert(it * 2 + u, u)

        @block.gpsimd
        def _(pool):
            for s_ in (s_kt, s_qt, s_kf, s_u, s_qad, s_qf):
                pool.sem_inc(s_, 1)
            for s_ in (*w_k, *w_q):
                pool.sem_inc(s_, 16)
            nc.gpsimd.memset(mhalf[:], -0.5).then_inc(s_const, 1)
            pool.wait_ge(s_const, 1)
            for b in range(NB):
                t4 = slice(b * TC, (b + 1) * TC)
                pool.wait_ge(s_ln, b + 1)
                nc.gpsimd.tensor_tensor(rstd[:, t4], var[:, t4], mhalf[:, t4], ALU.pow).then_inc(s_rstd, 1)
            nc.gpsimd.memset(EK[:], 1.0).then_inc(s_one, 1)
            for buf in (MQ, MK, EQ):
                nc.gpsimd.memset(buf[:], 0.0).then_inc(s_one, 1)
            nc.gpsimd.memset(VA[:], 0.0).then_inc(s_prep, 1)
            pool.wait_ge(s_prep, 1)
            nc.gpsimd.memset(VA[:, :, :, :, HD:HD + 1], 1.0).then_inc(s_prep, 1)
            nc.gpsimd.memset(ones[:], 1.0).then_inc(s_ones, 1)
            nc.gpsimd.memset(wg_wide[:], 0.0).then_inc(s_prep, 1)
            pool.wait_ge(s_prep, 3)
            pool.wait_ge(l_tab, 96)
            nc.gpsimd.tensor_copy(wg_wide[:, 15:143].rearrange("p (e s) -> p e s", e=NE)[:, :, 0:1],
                                  wg[:].unsqueeze(2)).then_inc(s_prep, 1)
            def rotate_q(b):
                pool.wait_ge(s_qt, b + 2)
                nc.gpsimd.tensor_tensor(qad[:], qcs[:], qss[:], ALU.add).then_inc(s_qad, 1)

            def parts_q(b, u, more=True):
                pool.wait_ge(s_qad, b + 2)
                pool.wait_ge(s_u, b + 2)
                nc.gpsimd.tensor_tensor(qf[:], qad[:], qu[:], ALU.add).then_inc(s_qf, 1)
                pool.wait_ge(s_qf, b + 2)
                pool.wait_ge(s_qh, b + 1)
                nc.gpsimd.tensor_tensor(qr[:], qf[:], qp[:, u, 0, :], ALU.subtract).then_inc(s_qr, 1)
                if more:
                    rotate_q(b + 1)
                pool.wait_ge(s_qm, b + 1)
                nc.gpsimd.tensor_tensor(qp[:, u, 2, :], qr[:], qp[:, u, 1, :], ALU.subtract).then_inc(s_ql, 1)

            rotate_q(0)
            with pool.Fori(0, NB // 2 - 1) as it:
                parts_q(it * 2, 0)
                parts_q(it * 2 + 1, 1)
            parts_q(NB - 2, 0)
            parts_q(NB - 1, 1, more=False)
            pool.wait_ge(s_prep, 2)

            def values(s, u):
                if not (isinstance(s, int) and s < 2):
                    pool.wait_ge(s_pv, s - 1)
                pool.sem_inc(s_held, 1)
                src = (Vall[:, s // 4, s % 4] if isinstance(s, int)
                       else Vall[:, ds(s // 4, 1), ds(s % 4, 1)].rearrange("p a b c d -> p (a b c) d"))
                nc.gpsimd.tensor_copy(VA[:, u, :, :, 0:HD],
                                      src.rearrange("p c (j d) -> p c j d", d=HD)).then_inc(s_va, 1)

            def max_parts(s, u):
                if not (isinstance(s, int) and s < 2):
                    pool.wait_ge(l_e[u], (s // 2) * 160)
                pool.wait_ge(s_mn, s + 1)
                pool.sem_inc(s_held, 1)
                nc.gpsimd.tensor_copy(mxp[:, u, 0, :], mxn[:]).then_inc(s_pp, 1)
                pool.wait_ge(s_pp, 3 * s + 1)
                nc.gpsimd.tensor_tensor(mxr[:], mxn[:], mxp[:, u, 0, :], ALU.subtract).then_inc(s_pp, 1)
                pool.wait_ge(s_pp, 3 * s + 2)
                pool.sem_inc(s_held, 1)
                nc.gpsimd.tensor_copy(mxp[:, u, 1, :], mxr[:]).then_inc(s_pp, 1)
                pool.wait_ge(s_pp, 3 * s + 3)
                nc.gpsimd.tensor_tensor(mxp[:, u, 2, :], mxr[:], mxp[:, u, 1, :],
                                        ALU.subtract).then_inc(s_parts, 1)

            max_parts(0, 0)
            values(0, 0)
            max_parts(1, 1)

            values(1, 1)
            max_parts(2, 0)
            pool.wait_ge(s_gate, 2)
            xv = X[:, :, :].rearrange("p (b c) d -> p b c d", b=NB)
            nc.gpsimd.tensor_tensor(xv, xv, bo_g[:].unsqueeze(2).to_broadcast([128, NB, TC, D]),
                                    ALU.add).then_inc(s_xb, 1)
            with pool.Fori(1, NS // 2 - 1) as it:
                values(it * 2, 0)
                max_parts(it * 2 + 1, 1)
                values(it * 2 + 1, 1)
                max_parts(it * 2 + 2, 0)
            values(14, 0)
            max_parts(15, 1)

            def rstd_2(b):
                t4 = slice(b * TC, (b + 1) * TC)
                pool.wait_ge(s_v2, b + 1)
                nc.gpsimd.tensor_tensor(rstd2[:, t4], var2[:, t4], mhalf[:, 0:TC], ALU.pow).then_inc(s_r2, 1)

            def rows_2(b):
                pool.wait_ge(s_xn2, b + 1)
                rows = rw[:, b * TC:(b + 1) * TC, 0:D]
                scale, shift = (modrow[:, b:b + 1, m * D:(m + 1) * D].to_broadcast([128, TC, D]) for m in (M_CB, M_SB))
                nc.gpsimd.tensor_tensor(rows, xn2[:, b % 2], scale, ALU.mult).then_inc(s_xm2, 1)
                pool.wait_ge(s_xm2, b + 1)
                nc.gpsimd.tensor_tensor(rows, rows, shift, ALU.add).then_inc(s_h2, 1)

            rstd_2(0)
            rstd_2(1)
            rows_2(0)
            rstd_2(2)
            values(15, 1)
            rows_2(1)
            rows_2(2)
            rstd_2(3)
            rows_2(3)

            out_rows = out.rearrange("b l d -> (b l) d")

            def gather(e, tiles=range(SC)):
                if e >= 2 and tiles[0] == 0:
                    pool.wait_ge(s_gg, e - 1)
                for c in tiles:
                    pool.indirect_dma_start(
                        out=ex[:, e % 2, c, :], out_offset=None, in_=rows_dram,
                        in_offset=bass.IndirectOffsetOnAxis(ap=idx[:, e, c:c + 1], axis=0)).then_inc(g_in[e % 2], 16)

            def scatter(e):
                if e > 0:
                    pool.wait_ge(w_sc[(e - 1) % 2], (e - 1) // 2 * 64 + 64)
                for c in range(SC):
                    if c % (SC // 2) == 0:
                        pool.wait_ge(s_yo, 2 * e + c // (SC // 2) + 1)
                    pool.indirect_dma_start(
                        out=out_rows, out_offset=bass.IndirectOffsetOnAxis(ap=idx[:, e, c:c + 1], axis=0),
                        in_=ys[:, e % 2, c, :], in_offset=None, compute_op=ALU.add).then_inc(w_sc[e % 2], 16)

            pool.wait_ge(w_gb, 16 * NB)
            pool.wait_ge(w_row, 16)
            pool.wait_ge(w_out, 16 * NB)
            for e in range(4):
                pool.wait_ge(s_idx, 4 if e < 2 else 8)
                gather(e)
            for e in range(NE):
                scatter(e)
                if e + 4 < NE - 1:
                    gather(e + 4)
                elif e + 4 == NE - 1:
                    gather(NE - 1, range(SC // 2))
                elif e + 4 == NE:
                    gather(NE - 1, range(SC // 2, SC))
            for u in range(2):
                pool.wait_ge(w_sc[u], 64 * (NE // 2))

        @block.scalar
        def _(act):
            act.wait_ge(l_c, 32)
            nc.scalar.activation(se[:, 0, :], cT[:], ACT.Exp, scale=-1.0).then_inc(s_silu, 1)
            def modrow_out(b):
                act.wait_ge(s_mod, b + 2)
                nc.scalar.activation(modrow[:, b, :], ps[:, 2 + b % 2, :], ACT.Copy).then_inc(s_modr, 1)

            modrow_out(0)
            modrow_out(1)
            act.wait_ge(s_modc, 2)
            def h_out(b):
                act.wait_ge(s_T, b + 1)
                nc.scalar.activation(hT[:, b, :], ps[:, 6 + b % 2, :], ACT.Identity,
                                     bias=modcol[:, 0, b:b + 1], scale=modcol[:, 1, b:b + 1]).then_inc(s_hT, 1)

            def ct_out(b):
                act.wait_ge(s_CT, b + 1)
                nc.scalar.activation(ct[:, b, :], ps[:, b % 2, :], ACT.Identity, bias=bcol[:, 0:1]).then_inc(s_ct, 1)

            h_out(0)
            act.wait_ge(l_w, 48)
            for b in range(1, NB):
                h_out(b)
                ct_out(b - 1)
                if b >= 2:
                    modrow_out(b)
            ct_out(NB - 1)
            with act.Fori(0, NB // 2) as it:
                for u in range(2):
                    b = it * 2 + u
                    act.wait_ge(s_kf, b + 2)
                    act.wait_ge(w_k[u], it * 48 + 16)
                    nc.scalar.activation(kp[:, u, 0, :], kf[:], ACT.Copy).then_inc(s_kh, 1)
                    act.wait_ge(s_qc, b + 1)
                    act.wait_ge(s_qf, b + 1)
                    nc.scalar.activation(qu[:], ps[:, 4, :], ACT.Identity, bias=bcol[:, 1:2]).then_inc(s_u, 1)
                    act.wait_ge(s_kr, b + 1)
                    nc.scalar.activation(kp[:, u, 1, :], kr[:], ACT.Copy).then_inc(s_km, 1)
                    act.wait_ge(s_qf, b + 2)
                    act.wait_ge(w_q[u], it * 48 + 16)
                    nc.scalar.activation(qp[:, u, 0, :], qf[:], ACT.Copy).then_inc(s_qh, 1)
                    act.wait_ge(s_qr, b + 1)
                    nc.scalar.activation(qp[:, u, 1, :], qr[:], ACT.Copy).then_inc(s_qm, 1)

            def max_out(s):
                act.wait_ge(s_mt, s + 1)
                if not (isinstance(s, int) and s == 0):
                    act.wait_ge(s_parts, s)
                nc.scalar.activation(mxn[:], ps[0:16, 7, 0:128], ACT.Copy).then_inc(s_mn, 1)

            def out_copy(s):
                act.wait_ge(s_pv, s + 1)
                if not (isinstance(s, int) and s == 0):
                    act.wait_ge(s_ot, s)
                nc.scalar.activation(osb[:], ps[:, 6, :], ACT.Copy).then_inc(s_oe, 1)

            def gates_out(b):
                act.wait_ge(s_gl, b + 1)
                cols = slice(b * TC * NE, (b + 1) * TC * NE)
                nc.scalar.activation(ge[:, cols], ps[:, 1, cols], ACT.Exp, scale=-1.0).then_inc(s_ge, 1)

            def step(s, u, prev=True, more_max=True, last=False):
                for n in range(16):
                    if n == 1 and prev:
                        out_copy(s - 2)
                    if n == 4 and more_max:
                        max_out(s + 1)
                    if n == 9 and last:
                        out_copy(14)
                    if n in (7, 13) and last:
                        gates_out(n // 8)
                    i, kc, half = n // 8, (n // 2) % 4, n % 2
                    if n == 0 and not (isinstance(s, int) and s < 2):
                        act.wait_ge(s_pv, s - 1)
                    act.wait_ge(s_sc, 16 * s + n + 1)
                    nc.scalar.activation(PT[:, u, 2 * i + half, kc, :], ps[:, 4 + half, :], ACT.Exp,
                                         scale=SCALE).then_inc(s_ex, 1)

            max_out(0)
            max_out(1)
            step(0, 0, prev=False, more_max=False)
            step(1, 1, prev=False)
            with act.Fori(1, NS // 2 - 1) as it:
                step(it * 2, 0)
                step(it * 2 + 1, 1)
            step(14, 0)
            step(15, 1, more_max=False, last=True)
            out_copy(15)
            gates_out(2)

            act.wait_ge(s_lg, 1)
            nc.scalar.activation(sv, ps[:, 3, 0:128], ACT.Exp, scale=-1.0).then_inc(s_sig, 1)
            gates_out(3)

            act.wait_ge(l_top, 16 * 8)
            nc.scalar.activation(tok32[:], tok16[:], ACT.Copy).then_inc(s_tok, 1)
            act.wait_ge(s_ones, 1)
            nc.scalar.activation(warm[:], ones[:, 0:1], ACT.Gelu)
            for n, (first, last) in enumerate(CHUNKS):
                if n == 1:
                    a_n = one_a[:, first * NSEG:last * NSEG, :].rearrange("p (e s) a -> p e s a", s=NSEG)
                    act.wait_ge(s_tok, 1)
                    act.wait_ge(s_one_a, 1)
                    for s in range(NSEG_ACT):
                        ins = nc.scalar.activation(a_n[:, :, s, :], a_n[:, :, s, :], ACT.Copy, scale=tok32[:, s:s + 1])
                    ins.then_inc(s_one_t, 1)
                act.wait_ge(s_slot, 3 * n + 1)
                cols = slice(first * 32, last * 32)
                nc.scalar.activation(slots[0:16, cols], ps[0:16, SLOT_BANK[n], cols], ACT.Copy).then_inc(s_slot, 1)
            act.wait_ge(l_top, 16 * 8)

            def gelu(e, u):
                if not (isinstance(e, int) and e < 2):
                    act.wait_ge(s_dn, (e - 1) * 2)
                for f in range(FC):
                    act.wait_ge(s_up, e * FC + f + 1)
                    bias = b1c[:, e, f:f + 1] if isinstance(e, int) else b1c[:, ds(e, 1), f]
                    nc.scalar.activation(hid[:, u, f, :], ps[:, 1 + f, :], ACT.Gelu, bias=bias).then_inc(s_gelu, 1)

            gelu(0, 0)
            gelu(1, 1)
            with act.Fori(1, NE // 2) as it:
                gelu(it * 2, 0)
                gelu(it * 2 + 1, 1)

        @block.vector
        def _(dve):
            dve.wait_ge(s_silu, 1)
            nc.vector.tensor_scalar_add(se[:, 1, :], se[:, 0, :], 1.0).then_inc(s_silu, 1)
            dve.wait_ge(s_silu, 2)
            nc.vector.reciprocal(se[:, 2, :], se[:, 1, :]).then_inc(s_silu, 1)
            dve.wait_ge(s_silu, 3)
            nc.vector.tensor_tensor(se[:, 3, :], se[:, 2, :], cT[:], ALU.mult).then_inc(s_silu, 1)
            def moments(b):
                t4 = slice(b * TC, (b + 1) * TC)
                dve.wait_ge(l_x[b], 16)
                for n in range(b * TC, (b + 1) * TC):
                    ins = nc.vector.bn_stats(stat[:, n, :], X[:, n, :])
                ins.then_inc(s_stat, 1)
                dve.wait_ge(s_stat, 2 * b + 1)
                for n in range(b * TC, (b + 1) * TC):
                    ins = nc.vector.bn_aggr(mv[:, n, :], stat[:, n, :])
                ins.then_inc(s_stat, 1)
                dve.wait_ge(s_stat, 2 * b + 2)
                nc.vector.tensor_scalar_add(var[:, t4], mv[:, t4, 1], EPS).then_inc(s_ln, 1)

            def norm(b):
                dve.wait_ge(s_rstd, b + 1)
                for n in range(b * TC, (b + 1) * TC):
                    ins = nc.vector.tensor_scalar(xn[:, n, :], X[:, n, :], mv[:, n, 0:1], rstd[:, n:n + 1],
                                                  ALU.subtract, ALU.mult)
                ins.then_inc(s_xn, 1)

            moments(0)
            dve.wait_ge(s_mod, 1)
            cols = ps[:, 4, 0:4 * NB].rearrange("p (j b) -> p j b", b=NB)
            nc.vector.tensor_copy(modcol[:, 0:4:2, :], cols[:, 0:4:2, :]).then_inc(s_modc, 1)
            nc.vector.tensor_scalar_add(modcol[:, 1:4:2, :], cols[:, 1:4:2, :], 1.0).then_inc(s_modc, 1)
            for b in range(1, NB):
                moments(b)
                norm(b - 1)
            norm(NB - 1)
            gate_rows = modrow[:, :, :].rearrange("p b (j c) -> p b j c", c=D)[:, :, 0:4:3, :]
            ga, cb = (modrow[:, :, m * D:(m + 1) * D] for m in (M_GA, M_CB))

            def gates_prep(n):
                b2 = slice(2 * n, 2 * n + 2)
                v, sgn_n, mag_n = gate_rows[:, b2], sgn[:, b2], mag[:, b2]
                dve.wait_ge(s_modr, 2 * n + 2)
                nc.vector.tensor_scalar(sgn_n, v, 0.0, 0.5, ALU.is_ge, ALU.subtract).then_inc(s_gp, 1)
                dve.wait_ge(s_gp, 4 * n + 1)
                nc.vector.tensor_tensor(mag_n, v, sgn_n, ALU.mult).then_inc(s_gp, 1)
                dve.wait_ge(s_gp, 4 * n + 2)
                nc.vector.scalar_tensor_tensor(out=mag_n, in0=mag_n, scalar=0.125, in1=sgn_n, op0=ALU.max,
                                               op1=ALU.mult).then_inc(s_gp, 1)
                nc.vector.tensor_scalar(cb[:, b2], cb[:, b2], 1.0, None, ALU.add)
                dve.wait_ge(s_gp, 4 * n + 3)
                nc.vector.tensor_scalar(v, mag_n, 4.0, None, ALU.mult).then_inc(s_gp, 1)
                dve.wait_ge(s_gp, 4 * n + 4)
                nc.vector.tensor_tensor(wo_g[:, b2], ga[:, b2], wo[:].unsqueeze(1).to_broadcast([D, 2, D]), ALU.mult)
                nc.vector.tensor_tensor(bo_g[:, b2], ga[:, b2], bo_row[:].unsqueeze(1).to_broadcast([128, 2, D]),
                                        ALU.mult).then_inc(s_gate, 1)

            def values_out(b):
                dve.wait_ge(s_V, b + 1)
                nc.vector.tensor_tensor(
                    Vall[:, b], ps[:, 4 + b % 2, :].rearrange("p (c g d) -> p g c d", c=TC, g=4),
                    bv_row[:].rearrange("p (g d) -> p g d", g=4).unsqueeze(2).to_broadcast([128, 4, TC, 32]),
                    ALU.add).then_inc(s_vd, 1)

            dve.wait_ge(l_tab, 96)
            gates_prep(0)
            for b in range(NB):
                values_out(b)
            gates_prep(1)
            dve.wait_ge(l_w, 48)
            def rotate_k(b):
                dve.wait_ge(s_kAB, b + 1)
                nc.vector.scalar_tensor_tensor(out=kcs[:], in0=ps[:, 2, :], scalar=bcol[:, 5:6], in1=cos_t[:],
                                               op0=ALU.add, op1=ALU.mult)
                nc.vector.scalar_tensor_tensor(out=kss[:], in0=ps[:, 3, :], scalar=bcol[:, 6:7], in1=sin_t[:],
                                               op0=ALU.add, op1=ALU.mult).then_inc(s_kt, 1)

            def parts_k(b, u, more=True):
                dve.wait_ge(s_kt, b + 2)
                nc.vector.tensor_tensor(kad[:], kcs[:], kss[:], ALU.add).then_inc(s_kad, 1)
                dve.wait_ge(s_kad, b + 1)
                dve.wait_ge(s_kc, b + 1)
                nc.vector.scalar_tensor_tensor(out=kf[:], in0=ps[:, 5, :], scalar=bcol[:, 4:5], in1=kad[:],
                                               op0=ALU.add, op1=ALU.add).then_inc(s_kf, 1)
                dve.wait_ge(s_qAB, b + 1)
                dve.wait_ge(s_qad, b + 1)
                nc.vector.scalar_tensor_tensor(out=qcs[:], in0=ps[:, 6, :], scalar=bcol[:, 2:3], in1=cos_t[:],
                                               op0=ALU.add, op1=ALU.mult)
                nc.vector.scalar_tensor_tensor(out=qss[:], in0=ps[:, 7, :], scalar=bcol[:, 3:4], in1=sin_t[:],
                                               op0=ALU.add, op1=ALU.mult).then_inc(s_qt, 1)
                if not more:
                    maxima(0, 0, 0)
                    maxima(0, 0, 1)
                dve.wait_ge(s_kh, b + 1)
                nc.vector.tensor_tensor(kr[:], kf[:], kp[:, u, 0, :], ALU.subtract).then_inc(s_kr, 1)
                if more:
                    rotate_k(b + 1)
                else:
                    maxima(0, 0, 2)
                dve.wait_ge(s_km, b + 1)
                nc.vector.tensor_tensor(kp[:, u, 2, :], kr[:], kp[:, u, 1, :], ALU.subtract).then_inc(s_kl, 1)

            def normed(s):
                dve.wait_ge(s_ot, s + 1)
                o = ps[:, 7, :].rearrange("p (a d) -> p a d", d=32)
                nc.vector.reciprocal(rs[:].unsqueeze(2), o[:, :, HD:HD + 1]).then_inc(s_rs, 1)
                dve.wait_ge(s_rs, s + 1)
                dst = (An[:, s // 4, :, s % 4, :] if isinstance(s, int) else
                       An[:, ds(s // 4, 1), :, ds(s % 4, 1), :].rearrange("p a q g c -> p (a q g) c"))
                nc.vector.tensor_tensor(
                    dst.rearrange("p q (j d) -> p q j d", d=HD),
                    o.rearrange("p (q j) d -> p q j d", j=4)[:, :, :, 0:HD],
                    rs[:].rearrange("p (q j) -> p q j", j=4).unsqueeze(3).to_broadcast([128, TC, 4, HD]),
                    ALU.mult).then_inc(s_no, 1)

            def maxima(s, u, n):
                if n == 0 and not (isinstance(s, int) and s < 2):
                    dve.wait_ge(s_mt, s - 1)
                dve.wait_ge(s_mx, 8 * s + n + 1)
                nc.vector.tensor_reduce(mx[:, u, :].rearrange("p (h a) -> p h a", h=2)[:, :, n],
                                        ps[:, 2 * (n % 2):2 * (n % 2) + 2, :], AX.X, ALU.max,
                                        negate=True).then_inc(s_mxd, 1)

            def step(s, u, prev=True, more_max=True):
                for n in range(8):
                    if more_max:
                        maxima(s + 2, u, n)
                    if n == 5 and prev:
                        normed(s - 2)

            def residual(b):
                t4 = range(b * TC, (b + 1) * TC)
                rows = slice(b * TC, (b + 1) * TC)
                dve.wait_ge(s_y, b + 1)
                nc.vector.tensor_tensor(x2[:, rows], ps[:, 1, :].rearrange("p (c d) -> p c d", c=TC),
                                        X[:, rows, :], ALU.add).then_inc(s_x2, 1)
                dve.wait_ge(s_x2, b + 1)
                for n in t4:
                    ins = nc.vector.bn_stats(stat2[:, n, :], x2[:, n, :])
                ins.then_inc(s_st2, 1)
                dve.wait_ge(s_st2, b * 2 + 1)
                for n in t4:
                    ins = nc.vector.bn_aggr(mv2[:, n, :], stat2[:, n, :])
                ins.then_inc(s_st2, 1)
                dve.wait_ge(s_st2, b * 2 + 2)
                nc.vector.tensor_scalar_add(var2[:, rows], mv2[:, rows, 1], EPS).then_inc(s_v2, 1)

            def normed_2(b):
                dve.wait_ge(s_r2, b + 1)
                if b >= 2:
                    dve.wait_ge(s_xm2, b - 1)
                    dve.wait_ge(s_h2t, b - 1)
                for c in range(TC):
                    n = b * TC + c
                    ins = nc.vector.tensor_scalar(xn2[:, b % 2, c, :], x2[:, n, :], mv2[:, n, 0:1], rstd2[:, n:n + 1],
                                                  ALU.subtract, ALU.mult)
                ins.then_inc(s_xn2, 1)

            def a_out(b):
                dve.wait_ge(s_aT, b + 1)
                if b >= 2:
                    dve.wait_ge(s_y, b - 1)
                nc.vector.tensor_copy(aT[:, b % 2, :], ps[:, 0, :]).then_inc(s_aTe, 1)

            def h2_out(b):
                dve.wait_ge(s_h2t, b + 1)
                if b >= 2:
                    dve.wait_ge(s_gl, b - 1)
                nc.vector.tensor_scalar(h2T[:, b % 2, :], ps[:, 2, :], modcol[:, 3, b:b + 1], modcol[:, 2, b:b + 1],
                                        ALU.mult, ALU.add).then_inc(s_h2e, 1)

            def gates_in(b):
                cols = slice(b * TC * NE, (b + 1) * TC * NE)
                dve.wait_ge(s_ge, b + 1)
                nc.vector.tensor_scalar_add(ge[:, cols], ge[:, cols], 1.0).then_inc(s_g1, 1)
                dve.wait_ge(s_g1, b + 1)
                nc.vector.reciprocal(rw[:, b * TC:(b + 1) * TC, D:D + NE],
                                     ge[:, cols].rearrange("p (n e) -> p n e", e=NE)).then_inc(s_g, 1)

            rotate_k(0)
            with dve.Fori(0, NB // 2 - 1) as it:
                parts_k(it * 2, 0)
                parts_k(it * 2 + 1, 1)
            parts_k(NB - 2, 0)
            parts_k(NB - 1, 1, more=False)
            for n in range(3, 8):
                maxima(0, 0, n)
            for n in range(8):
                maxima(1, 1, n)
            step(0, 0, prev=False)
            step(1, 1, prev=False)
            with dve.Fori(1, NS // 2 - 1) as it:
                step(it * 2, 0)
                step(it * 2 + 1, 1)
            dve.wait_ge(s_xb, 1)
            a_out(0)
            residual(0)
            a_out(1)
            residual(1)
            a_out(2)
            normed_2(0)
            normed(12)
            residual(2)
            normed_2(1)
            h2_out(0)
            normed_2(2)
            h2_out(1)
            normed(13)
            normed(14)
            h2_out(2)
            normed(15)
            a_out(3)
            residual(3)
            normed_2(3)
            h2_out(3)

            dve.wait_ge(s_sig, 1)
            nc.vector.tensor_scalar_add(junk, sv, 1.0).then_inc(s_sig, 1)
            dve.wait_ge(l_top, 16 * 8)
            dve.wait_ge(s_sig, 2)
            nc.vector.reciprocal(sv, junk)
            nc.vector.tensor_copy(cand[:, 0], cand_t[:, 0, :]).then_inc(s_sig, 1)
            dve.wait_ge(s_sig, 3)

            def counts(now):
                for j in range(3):
                    ins = nc.vector.tensor_scalar(ge3[:, j, :], sv, now[:, j:j + 1].bitcast(fp32), None, ALU.is_ge,
                                                  ALU.add, accum_out=cnt3[:, j:j + 1])
                ins.then_inc(s_cnt, 1)

            def reach(k):
                dve.wait_ge(s_tot, k + 1)
                nc.vector.tensor_scalar(reach3, ps[:, 0, 0:3], float(TOP), None, ALU.is_ge, ALU.add,
                                        accum_out=reached).then_inc(s_reach, 1)
                dve.wait_ge(s_reach, k + 1)

            assert 2 * (EXACT + 1) <= 24
            with dve.Fori(0, EXACT // 5) as it:
                for v in range(5):
                    k = it * 5 + v
                    counts(cand[:, 0])
                    nc.vector.tensor_tensor(next4, cand_t[:, ds(k + 1, 1), :].rearrange("p o j -> p (o j)"),
                                            cand[:, 0, 3:4].to_broadcast([128, 4]), ALU.add).then_inc(s_next, 1)
                    reach(k)
                    dve.wait_ge(s_next, k + 1)
                    nc.vector.scalar_tensor_tensor(
                        out=cand[:, 0], in0=reached.to_broadcast([128, 4]), scalar=scale_t[:, ds(k, 1)], in1=next4,
                        op0=ALU.mult, op1=ALU.add).then_inc(s_cand, 1)
                    dve.wait_ge(s_cand, k + 1)
            for k in range(EXACT, ROUNDS):
                now, then = cand[:, (k - EXACT) % 2], cand[:, (k - EXACT + 1) % 2]
                counts(now)
                if k - EXACT < NB:
                    gates_in(k - EXACT)
                reach(k)
                nc.vector.tensor_scalar(found, reached, scale_t[:, k:k + 1], None, ALU.mult).then_inc(s_found, 1)
                dve.wait_ge(s_found, k - EXACT + 1)
                nc.vector.scalar_tensor_tensor(
                    out=then, in0=cand_t[:, k + 1, :], scalar=now[:, 3:4], in1=found.to_broadcast([128, 4]),
                    op0=ALU.bitwise_xor, op1=ALU.bitwise_xor).then_inc(s_cand, 1)
                dve.wait_ge(s_cand, k + 1)
            base = then[:, 3:4]

            step_ = [0]

            def link(ins):
                step_[0] += 1
                ins.then_inc(s_tk, 1)
                dve.wait_ge(s_tk, step_[0])

            link(nc.vector.tensor_scalar(gt, sv, base.bitcast(fp32), None, ALU.is_gt, ALU.add, accum_out=cnt_gt))
            link(nc.vector.tensor_scalar(eq, sv, base.bitcast(fp32), None, ALU.is_equal))
            dve.wait_ge(s_ones, 1)
            nc.vector.tensor_tensor_scan(ep, ones[:], eq, 0.0, ALU.mult, ALU.add).then_inc(s_sel, 1)
            dve.wait_ge(s_selp, 1)
            link(nc.vector.tensor_scalar(lim1, ps[:, 0, 0:1], -1.0, float(TOP), ALU.mult, ALU.add))
            link(nc.vector.tensor_tensor(lim, lim1, ps[:, 0, 1:2], ALU.subtract))
            link(nc.vector.scalar_tensor_tensor(out=junk, in0=ep, scalar=lim, in1=eq, op0=ALU.is_le, op1=ALU.mult))
            link(nc.vector.tensor_tensor(sel, junk, gt, ALU.add))
            nc.vector.tensor_tensor_scan(pp, ones[:], sel, 0.0, ALU.mult, ALU.add).then_inc(s_sel, 1)
            dve.wait_ge(s_selp, 2)
            nc.vector.scalar_tensor_tensor(out=junk, in0=pp, scalar=ps[:, 0, 2:3], in1=sel, op0=ALU.add,
                                           op1=ALU.mult).then_inc(s_sel, 1)
            dve.wait_ge(s_selp, 3)
            link(nc.vector.tensor_scalar(posi, ps[:, 1, 0:128], -1.0, None, ALU.add))
            link(nc.vector.tensor_scalar(posa, posi, 5, None, ALU.arith_shift_right))
            link(nc.vector.tensor_scalar(posb, posi, 31, None, ALU.bitwise_and))
            nc.vector.tensor_copy(posa_h, posa)
            link(nc.vector.tensor_copy(posb_h, posb))
            def rows_up(e, u):
                dve.wait_ge(s_gt, e + 1)
                nc.vector.tensor_copy(exT[:, u, :], ps[:, 0, :]).then_inc(s_gx, 1)

            def factors(e, u):
                if not (isinstance(e, int) and e < 2):
                    dve.wait_ge(s_yo, (e - 1) * 2)
                g = ex[:, u, :, D + e:D + e + 1] if isinstance(e, int) else ex[:, u, :, ds(e + D, 1)]
                nc.vector.tensor_tensor(gg[:, u], ex[:, u, :, D + NE:HW], g.to_broadcast([128, SC, D]),
                                        ALU.mult).then_inc(s_gg, 1)

            for n, (first, last) in enumerate(CHUNKS):
                t16 = slice(first * NSEG, last * NSEG)
                width = (last - first) * NSEG
                a_n = one_a[:, t16, :]
                is_a = nc.vector.tensor_tensor(a_n, posa_h[:, t16].unsqueeze(2).to_broadcast([128, width, 16]),
                                               iota32[:, 0:16].unsqueeze(1).to_broadcast([128, width, 16]),
                                               ALU.is_equal)
                if n == 0:
                    link(is_a)
                    a_n = a_n.rearrange("p (e s) a -> p e s a", s=NSEG)
                    link(nc.vector.tensor_tensor(a_n, a_n, tok16[:].unsqueeze(1).unsqueeze(3).to_broadcast(
                        [128, last - first, NSEG, 16]), ALU.mult))
                else:
                    is_a.then_inc(s_one_a, 1)
                    dve.wait_ge(s_one_a, 1)
                    rest = a_n.rearrange("p (e s) a -> p e s a", s=NSEG)[:, :, NSEG_ACT:NSEG, :]
                    nc.vector.tensor_tensor(rest, rest, tok16[:, NSEG_ACT:NSEG].unsqueeze(1).unsqueeze(3).to_broadcast(
                        [128, last - first, NSEG - NSEG_ACT, 16]), ALU.mult)
                nc.vector.tensor_tensor(one_b[:, t16, :], posb_h[:, t16].unsqueeze(2).to_broadcast([128, width, 32]),
                                        iota32[:].unsqueeze(1).to_broadcast([128, width, 32]),
                                        ALU.is_equal).then_inc(s_one_ab, 1)
                if n == 1:
                    rows_up(0, 0)
                dve.wait_ge(s_slot, 3 * n + 3)
                for w in range(4):
                    nc.vector.tensor_copy(
                        idx[32 * w:32 * w + 32, first:last, :],
                        ps[0:32, SLOT_BANK[n] + 1, first * 16:last * 16].rearrange(
                            "p (e c w) -> p e c w", c=4, w=4)[:, :, :, w]).then_inc(s_idx, 1)

            def gated(e, u):
                b2v = b2r[:, e:e + 1, :] if isinstance(e, int) else b2r[:, ds(e, 1), :]
                for h in range(2):
                    tiles = slice(h * SC // 2, (h + 1) * SC // 2)
                    dve.wait_ge(s_dn, e * 2 + h + 1)
                    nc.vector.tensor_tensor(yb[:, u, tiles], ps[:, 5 + h, 0:TOP // 2].rearrange("p (c d) -> p c d", d=D),
                                            b2v.to_broadcast([128, SC // 2, D]), ALU.add).then_inc(s_yb, 1)
                    if h == 0:
                        dve.wait_ge(s_gg, e + 1)
                        if not (isinstance(e, int) and e < 2):
                            dve.wait_ge(w_sc[u], (e // 2) * 64)
                    dve.wait_ge(s_yb, e * 2 + h + 1)
                    nc.vector.tensor_tensor(ys[:, u, tiles], yb[:, u, tiles], gg[:, u, tiles],
                                            ALU.mult).then_inc(s_yo, 1)

            factors(0, 0)
            rows_up(1, 1)
            factors(1, 1)
            gated(0, 0)
            with dve.Fori(0, NE // 2 - 1) as it:
                for u in (1, 0):
                    e = it * 2 + 2 - u
                    rows_up(e + 1, 1 - u)
                    factors(e + 1, 1 - u)
                    gated(e, u)
            gated(NE - 1, 1)

        @block.tensor
        def _(pe):
            mm = nc.tensor.matmul
            pe.wait_ge(s_silu, 4)
            for j, m in enumerate((0, 1, 3, 4)):
                ins = mm(ps[:, 4, j * NB:(j + 1) * NB], wmod[:, m * D:(m + 1) * D], se[:, 3, :], start=True, stop=True)
            ins.then_inc(s_mod, 1)

            def modrows(b):
                if b >= 2:
                    pe.wait_ge(s_modr, b - 1)
                mm(ps[:, 2 + b % 2, :], se[:, 3, b:b + 1].to_broadcast([D, 128]), wmod[:, 2 * D:6 * D],
                   start=True, stop=True).then_inc(s_mod, 1)

            modrows(0)
            modrows(1)
            pe.wait_ge(l_id, 16)
            pe.wait_ge(s_modc, 2)
            for n in range(NB + 2):
                if n < NB:
                    b = n
                    pe.wait_ge(s_xn, b + 1)
                    if b >= 2:
                        pe.wait_ge(s_hT, b - 1)
                    for c in range(TC):
                        ins = nc.tensor.transpose(ps[:, 6 + b % 2, c * 128:(c + 1) * 128], xn[:, b * TC + c, :],
                                                  ident[:])
                    ins.then_inc(s_T, 1)
                if 1 <= n <= NB:
                    b = n - 1
                    pe.wait_ge(s_hT, b + 1)
                    if b == 0:
                        pe.wait_ge(l_w, 48)
                    if b >= 2:
                        pe.wait_ge(s_ct, b - 1)
                    mm(ps[:, b % 2, :], w_x[:, 0:D], hT[:, b, :], start=True, stop=True).then_inc(s_CT, 1)
                if n >= 2:
                    b = n - 2
                    pe.wait_ge(s_ct, b + 1)
                    if b >= 2:
                        pe.wait_ge(s_vd, b - 1)
                    for c in range(TC):
                        ins = mm(ps[:, 4 + b % 2, c * 128:(c + 1) * 128], ct[64:128, b, c * 128:(c + 1) * 128],
                                 w_ct[64:128, 4 * D:5 * D], start=True, stop=True)
                    ins.then_inc(s_V, 1)
                if 2 <= n < NB:
                    modrows(n)
            pe.wait_ge(s_modr, NB)
            with pe.Fori(0, NB) as b:
                h_b = hT[:, ds(b, 1), :].rearrange("p o t -> p (o t)")
                c_b = ct[:, ds(b, 1), :].rearrange("p o t -> p (o t)")
                pe.wait_ge(s_kt, b + 1)
                mm(ps[:, 2, :], w_x[:, D:2 * D], h_b, start=True, stop=True)
                mm(ps[:, 3, :], w_x[:, 2 * D:3 * D], h_b, start=True, stop=True).then_inc(s_kAB, 1)
                pe.wait_ge(s_vd, NB)
                pe.wait_ge(s_kf, b + 1)
                mm(ps[:, 5, :], w_ct[:, 3 * D:4 * D], c_b, start=True, stop=True).then_inc(s_kc, 1)
                pe.wait_ge(s_qt, b + 1)
                mm(ps[:, 6, :], w_ct[:, D:2 * D], c_b, start=True, stop=True)
                mm(ps[:, 7, :], w_ct[:, 2 * D:3 * D], c_b, start=True, stop=True).then_inc(s_qAB, 1)
                pe.wait_ge(s_u, b + 1)
                mm(ps[:, 4, :], w_ct[:, 0:D], c_b, start=True, stop=True).then_inc(s_qc, 1)

            def max_unit(s, u, n):
                i, qc = n // 4, n % 4
                if n == 0:
                    pe.wait_ge(l_m[u], (s // 2 + 1) * 64)
                if not (isinstance(s, int) and 8 * s + n < 2):
                    pe.wait_ge(s_mxd, 8 * s + n - 1)
                for half in range(2):
                    ins = mm(ps[:, 2 * (n % 2) + half, :], MQ[:, u, i, qc * 128:(qc + 1) * 128], MK[:, u, half, i, :],
                             start=True, stop=True)
                ins.then_inc(s_mx, 1)

            def max_turn(s, u):
                pe.wait_ge(s_mxd, 8 * s + 8)
                if not (isinstance(s, int) and s < 4):
                    pe.wait_ge(s_no, s - 3)
                if not (isinstance(s, int) and s == 0):
                    pe.wait_ge(s_mn, s)
                nc.tensor.transpose(ps[0:16, 7, 0:128], mx[:, u, :], ident[:]).then_inc(s_mt, 1)

            def exp_unit(s, u, n):
                i, kc, half = n // 8, (n // 2) % 4, n % 2
                if n == 0:
                    pe.wait_ge(l_e[u], (s // 2 + 1) * 160)
                if not (isinstance(s, int) and 16 * s + n < 2):
                    pe.wait_ge(s_ex, 16 * s + n - 1)
                mm(ps[:, 4 + half, :], EK[:, u, i, kc * 128:(kc + 1) * 128], EQ[:, u, half, i, :],
                   start=True, stop=True).then_inc(s_sc, 1)

            def weigh(s, u, kc):
                if isinstance(s, int):
                    pe.wait_ge(s_ex, 16 * s + 2 * kc + 10)
                elif kc == 0:
                    pe.wait_ge(s_ex, 16 * s + 16)
                if kc == 0:
                    pe.wait_ge(s_va, s + 1)
                    if not (isinstance(s, int) and s == 0):
                        pe.wait_ge(s_oe, s)
                for j in range(4):
                    ins = mm(ps[32 * j:32 * j + 32, 6, :], VA[:, u, kc, j, :], PT[:, u, j, kc, :],
                             start=kc == 0, stop=kc == TC - 1)
                if kc == TC - 1:
                    ins.then_inc(s_pv, 1)

            def out_turn(s):
                pe.wait_ge(s_oe, s + 1)
                pe.wait_ge(s_mn, s + 4 if not isinstance(s, int) else min(s + 4, NS))
                if not (isinstance(s, int) and s == 0):
                    pe.wait_ge(s_no, s)
                for c in range(TC):
                    ins = nc.tensor.transpose(ps[:, 7, c * 128:(c + 1) * 128], osb[:, c * 128:(c + 1) * 128], ident[:])
                ins.then_inc(s_ot, 1)

            def turn_a(b):
                pe.wait_ge(s_no, 4 * b + 4)
                if b >= 1:
                    pe.wait_ge(s_aTe, b)
                for c in range(TC):
                    ins = nc.tensor.transpose(ps[:, 0, c * 128:(c + 1) * 128],
                                              An[:, b, c].rearrange("p g d -> p (g d)"), ident[:])
                ins.then_inc(s_aT, 1)

            def project(b):
                pe.wait_ge(s_aTe, b + 1)
                if b >= 1:
                    pe.wait_ge(s_x2, b)
                if b == NB - 1:
                    pe.wait_ge(s_ge, b)
                for c in range(TC):
                    ins = mm(ps[:, 1, c * 128:(c + 1) * 128], aT[:, b % 2, c * 128:(c + 1) * 128],
                             wo_g[:, b, :], start=True, stop=True)
                ins.then_inc(s_y, 1)

            def turn_h(b):
                pe.wait_ge(s_xn2, b + 1)
                if b >= 1:
                    pe.wait_ge(s_h2e, b)
                for c in range(TC):
                    ins = nc.tensor.transpose(ps[:, 2, c * 128:(c + 1) * 128], xn2[:, b % 2, c, :], ident[:])
                ins.then_inc(s_h2t, 1)

            def route_top(b):
                pe.wait_ge(s_h2e, b + 1)
                for c in range(TC):
                    n = b * TC + c
                    ins = mm(ps[:, 3, 0:128], wg_wide[:, 15 - n:143 - n], h2T[:, b % 2, c * 128:(c + 1) * 128],
                             start=n == 0, stop=n == NB * TC - 1)
                if b == NB - 1:
                    ins.then_inc(s_lg, 1)

            def route_gates(b):
                pe.wait_ge(s_x2, max(b, NB - 2) + 1)
                if b >= 1:
                    pe.wait_ge(s_ge, b)
                for c in range(TC):
                    n = b * TC + c
                    ins = mm(ps[:, 1, n * NE:(n + 1) * NE], h2T[:, b % 2, c * 128:(c + 1) * 128], wg[:],
                             start=True, stop=True)
                ins.then_inc(s_gl, 1)

            def keep_warm(n):
                for _ in range(n):
                    mm(ps[:, 4, :], ident[:], wmod[:, 0:512], start=True, stop=True)

            def beside_14(n):
                for at, stage, b in ((0, turn_a, 0), (1, project, 0), (2, turn_a, 1), (4, project, 1),
                                     (5, turn_a, 2), (7, project, 2)):
                    if n == at:
                        stage(b)

            def step(s, u, prev=True, prev2=True, more_max=True, turn=True, beside=None):
                for n in range(8):
                    if n == 1 and turn:
                        max_turn(s + 1, 1 - u)
                    if n == 4 and prev2:
                        out_turn(s - 2)
                    if more_max:
                        max_unit(s + 2, u, n)
                    exp_unit(s, u, 2 * n)
                    if n % 2 and prev:
                        weigh(s - 1, 1 - u, n // 2)
                    exp_unit(s, u, 2 * n + 1)
                    if beside is not None:
                        beside(n)

            pe.wait_ge(s_kt, NB + 1)
            for n in range(8):
                max_unit(0, 0, n)
            for done in (s_kf, s_u, s_qt):
                pe.wait_ge(done, NB + 1)
            max_turn(0, 0)
            for n in range(8):
                max_unit(1, 1, n)
            max_turn(1, 1)
            step(0, 0, prev=False, prev2=False, turn=False)
            step(1, 1, prev2=False)
            with pe.Fori(1, NS // 2 - 1) as it:
                step(it * 2, 0)
                step(it * 2 + 1, 1)
            pe.wait_ge(s_mxd, 8 * NS)
            pe.wait_ge(s_gate, 2)
            pe.wait_ge(s_prep, 4)
            step(14, 0, more_max=False, beside=beside_14)
            for n in range(8):
                if n == 4:
                    out_turn(13)
                exp_unit(15, 1, 2 * n)
                exp_unit(15, 1, 2 * n + 1)
                if n < TC:
                    weigh(14, 0, n)
                elif n > TC:
                    weigh(15, 1, n - TC - 1)
                if n in (0, 3, 7):
                    turn_h(n // 3)
                elif n in (2, 5):
                    route_top(n // 3)
                    route_gates(n // 3)
                elif n == 6:
                    out_turn(14)
            weigh(15, 1, TC - 1)
            route_top(2)
            out_turn(15)
            route_gates(2)
            turn_a(3)
            project(3)
            keep_warm(1)
            turn_h(3)
            route_top(3)
            route_gates(3)

            pe.wait_ge(l_top, 16 * 8)
            with pe.Fori(0, ROUNDS // 5) as it:
                for v in range(5):
                    pe.wait_ge(s_cnt, it * 5 + v + 1)
                    mm(ps[:, 0, 0:3], same_e[:], cnt3, start=True, stop=True).then_inc(s_tot, 1)
            pe.wait_ge(s_sel, 1)
            mm(ps[:, 0, 0:1], same_e[:], cnt_gt, start=True, stop=True)
            mm(ps[:, 0, 1:2], lower[:], ep[:, 127:128], start=True, stop=True).then_inc(s_selp, 1)
            pe.wait_ge(s_sel, 2)
            mm(ps[:, 0, 2:3], lower[:], pp[:, 127:128], start=True, stop=True).then_inc(s_selp, 1)
            pe.wait_ge(s_sel, 3)
            pe.wait_ge(s_ge, NB)
            nc.tensor.transpose(ps[:, 1, 0:128], junk, ident[:]).then_inc(s_selp, 1)
            def turn(e, u):
                pe.wait_ge(g_in[u], (e // 2 + 1) * 64)
                if not (isinstance(e, int) and e == 0):
                    pe.wait_ge(s_gx, e)
                for c in range(SC):
                    ins = nc.tensor.transpose(ps[:, 0, c * 128:(c + 1) * 128], ex[:, u, c, 0:D], ident[:])
                ins.then_inc(s_gt, 1)

            def up(e, u, chunks):
                if 0 in chunks:
                    pe.wait_ge(s_gx, e + 1)
                    pe.wait_ge(l_w1[u], (e // 2 + 1) * 16)
                for f in chunks:
                    if not (isinstance(e, int) and e == 0):
                        pe.wait_ge(s_gelu, (e - 1) * FC + f + 1)
                    mm(ps[:, 1 + f, :], w1s[:, u, f * 128:(f + 1) * 128], exT[:, u, :],
                       start=True, stop=True).then_inc(s_up, 1)

            TURN_AT = 5
            for n, (first, last) in enumerate(CHUNKS):
                if n == 1:
                    keep_warm(4)
                pe.wait_ge(s_one_ab, n + 1)
                if n == 1:
                    pe.wait_ge(s_one_t, 1)
                for e in range(first, last):
                    if n == 1 and e == TURN_AT:
                        turn(0, 0)
                    for s in range(NSEG):
                        ins = mm(ps[0:16, SLOT_BANK[n], 32 * e:32 * e + 32], one_a[:, e * NSEG + s, :],
                                 one_b[:, e * NSEG + s, :], start=s == 0, stop=s == NSEG - 1)
                ins.then_inc(s_slot, 1)
                pe.wait_ge(s_slot, 3 * n + 2)
                for e in range(first, last):
                    ins = nc.tensor.transpose(ps[0:32, SLOT_BANK[n] + 1, 16 * e:16 * e + 16],
                                              slots[0:16, 32 * e:32 * e + 32], ident[0:16, 0:16])
                ins.then_inc(s_slot, 1)

            def down(e, u):
                pe.wait_ge(s_gelu, e * FC + FC)
                pe.wait_ge(l_w2[u], (e // 2 + 1) * 16)
                for c in range(SC):
                    h, at = c // (SC // 2), c % (SC // 2)
                    if at == 0 and not (isinstance(e, int) and e == 0):
                        pe.wait_ge(s_yb, e * 2 + h - 1)
                    for f in range(FC):
                        ins = mm(ps[:, 5 + h, at * 128:(at + 1) * 128], hid[:, u, f, c * 128:(c + 1) * 128],
                                 w2s[:, u, f, :], start=f == 0, stop=f == FC - 1)
                    if at == SC // 2 - 1:
                        ins.then_inc(s_dn, 1)

            def expert(e, u):
                up(e, u, range(1, FC - 1))
                turn(e + 1, 1 - u)
                up(e, u, range(FC - 1, FC))
                up(e + 1, 1 - u, range(1))
                down(e, u)

            up(0, 0, range(FC))
            turn(1, 1)
            up(1, 1, range(1))
            pe.wait_ge(s_idx, 8)
            down(0, 0)
            with pe.Fori(0, NE // 2 - 1) as it:
                expert(it * 2 + 1, 1)
                expert(it * 2 + 2, 0)
            up(NE - 1, 1, range(1, FC))
            down(NE - 1, 1)


def tables():
    ids = np.arange(D // 2, dtype=np.float32)
    theta = (np.float32(10000.0) ** (np.float32(-2.0) * ids) / np.float32(D // 2)).astype(np.float32)
    r = np.arange(L, dtype=np.float32)[None, :] * theta[:, None]
    cos, sin = np.repeat(np.cos(r), 2, 0), np.repeat(np.sin(r), 2, 0)
    sin[0::2] *= -1.0
    return cos.astype(np.float32), sin.astype(np.float32)


def kernel(**inputs):
    import concourse.bacc as bacc
    from concourse.bass_utils import run_bass_kernel_spmd as run

    a = {k.replace("L0_attn_", "").replace("L0_ffn_", "").replace("L0_", ""): np.asarray(v) for k, v in inputs.items()}
    order = np.array([(8 * half + h8) * HD + d for half in range(2) for d in range(HD) for h8 in range(8)])
    swapped = order ^ 1
    vorder = np.array([(8 * half + 2 * g + i) * HD + d
                       for g in range(4) for i in range(2) for half in range(2) for d in range(HD)])
    none = np.zeros((DC, D), np.float32)
    cos, sin = tables()
    part = np.arange(128)
    seg = part // (128 // NE)
    arrays = {
        "x": a["x"],
        "cT": a["c"].T,
        "wmod": a["wmod"],
        "w_x": np.concatenate([a["Wd_q_w"], a["Wd_kv_w"], a["Wk_r_w"][:, order], a["Wk_r_w"][:, swapped]], 1),
        "w_ct": np.concatenate([
            np.concatenate([a["Wu_q_w"][:, order], a["Wq_r_w"][:, order], a["Wq_r_w"][:, swapped], none, none], 1),
            np.concatenate([none, none, none, a["Wu_k_w"][:, order], a["Wu_v_w"][:, vorder]], 1)], 0),
        "bcol": np.stack([np.concatenate([a["Wd_q_b"], a["Wd_kv_b"]]), a["Wu_q_b"][order], a["Wq_r_b"][order],
                          a["Wq_r_b"][swapped], a["Wu_k_b"][order], a["Wk_r_b"][order], a["Wk_r_b"][swapped]], 1),
        "brow": np.stack([a["Wu_v_b"][vorder], a["Wo_b"]]),
        "cos": cos[order], "sin": sin[order],
        "wo": a["Wo_w"][vorder, :],
        "wg": a["Wg"],
        "ident": np.eye(128, dtype=np.float32),
        "w1": a["W1"], "w2": a["W2"], "b2": a["b2"],
        "b1c": a["b1"].reshape(NE, FC, 128).transpose(2, 0, 1),
        "same_e": (seg[:, None] == seg[None, :]).astype(np.float16),
        "lower": ((seg[:, None] == seg[None, :]) & (part[:, None] < part[None, :])).astype(np.float32),
        "scale_t": np.tile(2.0 ** (2 * np.arange(ROUNDS - 1, -1, -1)), (128, 1)).astype(np.float32),
        "cand_t": np.tile(np.append(np.array([1, 2, 3, 0]) * 4 ** np.arange(ROUNDS - 1, -1, -1)[:, None], [[0] * 4], 0),
                          (128, 1, 1)).astype(np.int32),
        "iota32": np.tile(np.arange(32), (128, 1)).astype(np.float16),
        "tok16": (np.arange(128 // NE)[None, :] * 128 + part[:, None]).astype(np.float16),
    }
    arrays = {k: np.ascontiguousarray(v) for k, v in arrays.items()}
    nc = bacc.Bacc("TRN2", target_bir_lowering=False, num_devices=1)
    t = {k: nc.dram_tensor("in_" + k, list(v.shape), mybir.dt.from_np(v.dtype), kind="ExternalInput").ap()
         for k, v in arrays.items()}
    out = nc.dram_tensor("out", [NB, L, D], mybir.dt.float32, kind="ExternalOutput").ap()
    build(nc, t, out)
    r = run(nc, [{"in_" + k: v for k, v in arrays.items()}], core_ids=[0])
    return r.results[0]["out"]
```
